# Optimizing a Trainium2 kernel written in Bass

```python
import numpy as np
import jax
import jax.numpy as jnp

def _softmax(x, axis=-1):
    return jax.nn.softmax(x, axis=axis)

def _gelu(x):
    return jax.nn.gelu(x, approximate=True)

def _silu(x):
    return jax.nn.silu(x)

def _sigmoid(x):
    return jax.nn.sigmoid(x)

def _layernorm(x, axis=-1, eps=1e-05):
    m = jnp.mean(x, axis=axis, keepdims=True)
    v = jnp.var(x, axis=axis, keepdims=True)
    return (x - m) / jnp.sqrt(v + eps)

def _scatter_add(tgt, idx, src, axis=0):
    return tgt.at[idx].add(src)

def _segment_sum(src, seg, n):
    return jax.ops.segment_sum(src, seg, n)
kernel_name = 'mk_gnn_preln_d2_gnn_r8_e0487f'

def setup_inputs(seed: int=0):
    np.random.seed(seed)
    _w = jnp.asarray

    def _rec_inputs():
        import jax
        import jax.numpy as jnp
        _gk = jax.random.key(seed)
        x = -0.0005121 + 1.001 * jax.random.normal(jax.random.fold_in(_gk, 1), (12500, 32), jnp.float32)
        src = jax.random.randint(jax.random.fold_in(_gk, 2), (200000,), 0, 12500, jnp.int32)
        dst = jax.random.randint(jax.random.fold_in(_gk, 3), (200000,), 0, 12500, jnp.int32)
        _o = jnp.argsort(dst, stable=True)
        src = src[_o]
        dst = dst[_o]
        edge_attr_3 = jax.random.uniform(jax.random.fold_in(_gk, 12), (200000, 3), jnp.float32, 0.0, 0.999998)
        return (x, src, dst, edge_attr_3)
    x, src, dst, edge_attr_3 = _rec_inputs()

    def _L0_gnn_setup():
        import jax, jax.numpy as jnp
        import numpy as np
        NEG_SLOPE = 0.2

        def _cheb(src, dst, n, x, norm, re_norm, W, b):

            def prop(h):
                return norm * jax.ops.segment_sum((h * norm)[src], dst, num_segments=n)
            X0 = x
            X1 = -re_norm * prop(X0) + X0 * (re_norm - 1.0)
            X2 = -2.0 * re_norm * prop(X1) + X1 * 2.0 * (re_norm - 1.0) - X0
            Xt = jnp.concatenate([X0, X1, X2], axis=1)
            return jax.nn.relu(Xt @ W.T + b)

        def _gatv2(src, dst, n, x, Wsrc, bsrc, Wdst, bdst, attn, bias):
            H, D = (attn.shape[1], attn.shape[2])
            fs = (x @ Wsrc.T + bsrc).reshape(n, H, D)
            fd = (x @ Wdst.T + bdst).reshape(n, H, D)
            e = jax.nn.leaky_relu(fs[src] + fd[dst], NEG_SLOPE)
            logits = jnp.sum(e * attn, axis=-1)
            m = jax.ops.segment_max(logits, dst, num_segments=n)
            m = jnp.where(jnp.isfinite(m), m, 0.0)
            ex = jnp.exp(logits - m[dst])
            s = jax.ops.segment_sum(ex, dst, num_segments=n)
            a = ex / s[dst]
            rst = jax.ops.segment_sum(a[:, :, None] * fs[src], dst, num_segments=n)
            return rst + bias.reshape(1, H, D)
        key = jax.random.key(seed)
        ks = jax.random.split(key, 8)
        N, E, Dm, K, Hh = (12500, 200000, 32, 3, 1)
        return {'user_embed': jax.random.normal(ks[0], (N, Dm), jnp.float32), 'src': jax.random.randint(ks[1], (E,), 0, N), 'dst': jax.random.randint(ks[2], (E,), 0, N), 'laplacian_lambda_max': jnp.ones((1,), jnp.float32), 'cheb_W': jax.random.normal(ks[3], (Dm, K * Dm), jnp.float32) * 0.1, 'cheb_b': jnp.zeros((Dm,), jnp.float32), 'gat_Wsrc': jax.random.normal(ks[4], (Hh * Dm, Dm), jnp.float32) * 0.1, 'gat_bsrc': jnp.zeros((Hh * Dm,), jnp.float32), 'gat_Wdst': jax.random.normal(ks[5], (Hh * Dm, Dm), jnp.float32) * 0.1, 'gat_bdst': jnp.zeros((Hh * Dm,), jnp.float32), 'gat_attn': jax.random.normal(ks[6], (1, Hh, Dm), jnp.float32) * 0.1, 'gat_bias': jnp.zeros((Hh * Dm,), jnp.float32)}
    _L0_gnn_all = _L0_gnn_setup()
    _L0_gnn_in = {k: v for k, v in _L0_gnn_all.items() if k in ('laplacian_lambda_max', 'cheb_W', 'cheb_b', 'gat_Wsrc', 'gat_bsrc', 'gat_Wdst', 'gat_bdst', 'gat_attn', 'gat_bias')}
    del _L0_gnn_all

    def _L1_gnn_setup():
        import jax, jax.numpy as jnp
        import numpy as np
        D = 3
        KS = 5
        K = KS ** D
        S = 2 ** D
        _COMBOS = np.array([[s >> d & 1 for d in range(D)] for s in range(S)], dtype=np.int32)
        _STRIDES = np.array([KS ** (D - 1 - d) for d in range(D)], dtype=np.int32)

        def spline_basis(pseudo):
            pos = pseudo * (KS - 1)
            i0 = jnp.clip(jnp.floor(pos), 0, KS - 2).astype(jnp.int32)
            frac = pos - i0
            combos = jnp.asarray(_COMBOS)
            basis = jnp.prod(jnp.where(combos[None] == 1, frac[:, None, :], 1.0 - frac[:, None, :]), axis=-1)
            idx = jnp.sum((i0[:, None, :] + combos[None]) * jnp.asarray(_STRIDES)[None, None, :], axis=-1)
            return (basis, idx)

        def spline_conv(x, row, col, basis, idx, W, b):
            N = x.shape[0]
            Fout = W.shape[2]
            z = jnp.einsum('ni,kio->nko', x, W).reshape(N * K, Fout)
            gathered = z[col[:, None] * K + idx]
            msg = jnp.einsum('es,eso->eo', basis, gathered)
            out = jax.ops.segment_sum(msg, row, num_segments=N)
            deg = jax.ops.segment_sum(jnp.ones_like(msg[:, 0]), row, num_segments=N)
            return out / jnp.maximum(deg, 1.0)[:, None] + b
        key = jax.random.key(seed)
        ks = jax.random.split(key, 13)
        N, E, Fin, Fout = (2500, 40000, 32, 32)

        def u(k, shape, size):
            bound = 1.0 / np.sqrt(size)
            return jax.random.uniform(k, shape, jnp.float32, -bound, bound)
        return dict(x=jax.random.normal(ks[0], (N, Fin), jnp.float32), edge_index=jax.random.randint(ks[1], (2, E), 0, N, dtype=jnp.int32), pseudo=jax.random.uniform(ks[2], (E, D), jnp.float32), stn1_w=u(ks[3], (K, 1, 64), 1 * S), stn1_b=u(ks[4], (64,), 1 * S), stn2_w=u(ks[5], (K, 64, 64), 64 * S), stn2_b=u(ks[6], (64,), 64 * S), stn3_w=u(ks[7], (64, 64), 64), stn3_b=u(ks[8], (64,), 64), stn4_w=u(ks[9], (64, 3), 64), stn4_b=u(ks[10], (3,), 64), conv_w=u(ks[11], (K, Fin, Fout), Fin * S), conv_b=u(ks[12], (Fout,), Fin * S))
    _L1_gnn_all = _L1_gnn_setup()
    _L1_gnn_in = {k: v for k, v in _L1_gnn_all.items() if k in ('stn1_w', 'stn1_b', 'stn2_w', 'stn2_b', 'stn3_w', 'stn3_b', 'stn4_w', 'stn4_b', 'conv_w', 'conv_b')}
    del _L1_gnn_all
    return {'x': x, 'src': src, 'dst': dst, 'edge_attr_3': edge_attr_3, 'L0_gnn_laplacian_lambda_max': _L0_gnn_in['laplacian_lambda_max'], 'L0_gnn_cheb_W': _L0_gnn_in['cheb_W'], 'L0_gnn_cheb_b': _L0_gnn_in['cheb_b'], 'L0_gnn_gat_Wsrc': _L0_gnn_in['gat_Wsrc'], 'L0_gnn_gat_bsrc': _L0_gnn_in['gat_bsrc'], 'L0_gnn_gat_Wdst': _L0_gnn_in['gat_Wdst'], 'L0_gnn_gat_bdst': _L0_gnn_in['gat_bdst'], 'L0_gnn_gat_attn': _L0_gnn_in['gat_attn'], 'L0_gnn_gat_bias': _L0_gnn_in['gat_bias'], 'L1_gnn_stn1_w': _L1_gnn_in['stn1_w'], 'L1_gnn_stn1_b': _L1_gnn_in['stn1_b'], 'L1_gnn_stn2_w': _L1_gnn_in['stn2_w'], 'L1_gnn_stn2_b': _L1_gnn_in['stn2_b'], 'L1_gnn_stn3_w': _L1_gnn_in['stn3_w'], 'L1_gnn_stn3_b': _L1_gnn_in['stn3_b'], 'L1_gnn_stn4_w': _L1_gnn_in['stn4_w'], 'L1_gnn_stn4_b': _L1_gnn_in['stn4_b'], 'L1_gnn_conv_w': _L1_gnn_in['conv_w'], 'L1_gnn_conv_b': _L1_gnn_in['conv_b']}

def reference(x, src, dst, edge_attr_3, L0_gnn_laplacian_lambda_max, L0_gnn_cheb_W, L0_gnn_cheb_b, L0_gnn_gat_Wsrc, L0_gnn_gat_bsrc, L0_gnn_gat_Wdst, L0_gnn_gat_bdst, L0_gnn_gat_attn, L0_gnn_gat_bias, L1_gnn_stn1_w, L1_gnn_stn1_b, L1_gnn_stn2_w, L1_gnn_stn2_b, L1_gnn_stn3_w, L1_gnn_stn3_b, L1_gnn_stn4_w, L1_gnn_stn4_b, L1_gnn_conv_w, L1_gnn_conv_b):
    import jax
    import jax.numpy as jnp

    def _L0_gnn_ref(user_embed, src, dst, laplacian_lambda_max, cheb_W, cheb_b, gat_Wsrc, gat_bsrc, gat_Wdst, gat_bdst, gat_attn, gat_bias):
        import jax, jax.numpy as jnp
        import numpy as np
        NEG_SLOPE = 0.2

        def _cheb(src, dst, n, x, norm, re_norm, W, b):

            def prop(h):
                return norm * jax.ops.segment_sum((h * norm)[src], dst, num_segments=n)
            X0 = x
            X1 = -re_norm * prop(X0) + X0 * (re_norm - 1.0)
            X2 = -2.0 * re_norm * prop(X1) + X1 * 2.0 * (re_norm - 1.0) - X0
            Xt = jnp.concatenate([X0, X1, X2], axis=1)
            return jax.nn.relu(Xt @ W.T + b)

        def _gatv2(src, dst, n, x, Wsrc, bsrc, Wdst, bdst, attn, bias):
            H, D = (attn.shape[1], attn.shape[2])
            fs = (x @ Wsrc.T + bsrc).reshape(n, H, D)
            fd = (x @ Wdst.T + bdst).reshape(n, H, D)
            e = jax.nn.leaky_relu(fs[src] + fd[dst], NEG_SLOPE)
            logits = jnp.sum(e * attn, axis=-1)
            m = jax.ops.segment_max(logits, dst, num_segments=n)
            m = jnp.where(jnp.isfinite(m), m, 0.0)
            ex = jnp.exp(logits - m[dst])
            s = jax.ops.segment_sum(ex, dst, num_segments=n)
            a = ex / s[dst]
            rst = jax.ops.segment_sum(a[:, :, None] * fs[src], dst, num_segments=n)
            return rst + bias.reshape(1, H, D)
        n = user_embed.shape[0]
        deg = jax.ops.segment_sum(jnp.ones((src.shape[0],), user_embed.dtype), dst, num_segments=n)
        norm = jnp.clip(deg, 1.0, None)[:, None] ** (-0.5)
        re_norm = 2.0 / laplacian_lambda_max
        h = _cheb(src, dst, n, user_embed, norm, re_norm, cheb_W, cheb_b)
        h = _cheb(src, dst, n, h, norm, re_norm, cheb_W, cheb_b)
        out = _gatv2(src, dst, n, h, gat_Wsrc, gat_bsrc, gat_Wdst, gat_bdst, gat_attn, gat_bias)
        return out[:, 0, :]

    def _L1_gnn_ref(x, edge_index, pseudo, stn1_w, stn1_b, stn2_w, stn2_b, stn3_w, stn3_b, stn4_w, stn4_b, conv_w, conv_b):
        import jax, jax.numpy as jnp
        import numpy as np
        D = 3
        KS = 5
        K = KS ** D
        S = 2 ** D
        _COMBOS = np.array([[s >> d & 1 for d in range(D)] for s in range(S)], dtype=np.int32)
        _STRIDES = np.array([KS ** (D - 1 - d) for d in range(D)], dtype=np.int32)

        def spline_basis(pseudo):
            pos = pseudo * (KS - 1)
            i0 = jnp.clip(jnp.floor(pos), 0, KS - 2).astype(jnp.int32)
            frac = pos - i0
            combos = jnp.asarray(_COMBOS)
            basis = jnp.prod(jnp.where(combos[None] == 1, frac[:, None, :], 1.0 - frac[:, None, :]), axis=-1)
            idx = jnp.sum((i0[:, None, :] + combos[None]) * jnp.asarray(_STRIDES)[None, None, :], axis=-1)
            return (basis, idx)

        def spline_conv(x, row, col, basis, idx, W, b):
            N = x.shape[0]
            Fout = W.shape[2]
            z = jnp.einsum('ni,kio->nko', x, W).reshape(N * K, Fout)
            gathered = z[col[:, None] * K + idx]
            msg = jnp.einsum('es,eso->eo', basis, gathered)
            out = jax.ops.segment_sum(msg, row, num_segments=N)
            deg = jax.ops.segment_sum(jnp.ones_like(msg[:, 0]), row, num_segments=N)
            return out / jnp.maximum(deg, 1.0)[:, None] + b
        N = x.shape[0]
        row, col = (edge_index[0], edge_index[1])
        basis, idx = spline_basis(pseudo)
        h = jnp.ones((N, 1), x.dtype)
        h = jax.nn.elu(spline_conv(h, row, col, basis, idx, stn1_w, stn1_b))
        h = jax.nn.elu(spline_conv(h, row, col, basis, idx, stn2_w, stn2_b))
        h = jax.nn.elu(h @ stn3_w + stn3_b)
        t = h @ stn4_w + stn4_b
        new_pseudo = jnp.clip(pseudo + t[col] - t[row], 0.0, 1.0)
        basis2, idx2 = spline_basis(new_pseudo)
        return spline_conv(x, row, col, basis2, idx2, conv_w, conv_b)
    edge_index = jnp.stack([src, dst])
    h = jnp.maximum(_layernorm(x, axis=-1), 0.0)
    x = x + _L0_gnn_ref(h, src, dst, L0_gnn_laplacian_lambda_max, L0_gnn_cheb_W, L0_gnn_cheb_b, L0_gnn_gat_Wsrc, L0_gnn_gat_bsrc, L0_gnn_gat_Wdst, L0_gnn_gat_bdst, L0_gnn_gat_attn, L0_gnn_gat_bias)
    h = jnp.maximum(_layernorm(x, axis=-1), 0.0)
    x = x + _L1_gnn_ref(h, edge_index, edge_attr_3, L1_gnn_stn1_w, L1_gnn_stn1_b, L1_gnn_stn2_w, L1_gnn_stn2_b, L1_gnn_stn3_w, L1_gnn_stn3_b, L1_gnn_stn4_w, L1_gnn_stn4_b, L1_gnn_conv_w, L1_gnn_conv_b)
    return x

_drawn_inputs = setup_inputs


def setup_inputs(seed=0):
    import zlib

    import numpy as np

    out = dict(_drawn_inputs(seed))
    spreads = {'L0_gnn_cheb_b': (0.0, 0.313),
     'L0_gnn_gat_bsrc': (0.0, 0.1),
     'L0_gnn_gat_bdst': (0.0, 2.0),
     'L0_gnn_gat_bias': (0.0, 0.1)}
    factors = {'edge_attr_3': 2.983,
     'L0_gnn_gat_Wdst': 8.0,
     'L0_gnn_gat_attn': 4.03,
     'L1_gnn_stn1_w': 8.0,
     'L1_gnn_stn1_b': 26.184,
     'L1_gnn_stn2_w': 8.0,
     'L1_gnn_stn2_b': 64.0,
     'L1_gnn_stn3_w': 8.0,
     'L1_gnn_stn3_b': 64.0,
     'L1_gnn_stn4_w': 8.0,
     'L1_gnn_stn4_b': 8.0,
     'L1_gnn_conv_w': 2.741}
    for name, (base, spread) in spreads.items():
        noise = np.random.default_rng([zlib.crc32(name.encode()), seed]).standard_normal(out[name].shape)
        drawn = base * np.exp(spread * noise) if base else spread * noise
        out[name] = jnp.asarray(drawn.astype(out[name].dtype))
    for name, factor in factors.items():
        out[name] = (out[name] * factor).astype(out[name].dtype)
    return out
```

```python
from contextlib import ExitStack

import concourse.bass as bass
from concourse import mybir

F32, BF16, I32 = mybir.dt.float32, mybir.dt.bfloat16, mybir.dt.int32
ALU = mybir.AluOpType
ACT = mybir.ActivationFunctionType
AX = mybir.AxisListType.X

P = 128
N, D = 12500, 32
LO, NT = 125, 100
E = 200000
EC = -(-E // P)
GRP = 8
ECP = -(-EC // (2 * GRP)) * 2 * GRP
HID = 64
KS = 5
K3 = KS ** 3
CELLS = 4 ** 3
NC = -(-((E + NT * (P - 1)) // P) // (2 * GRP)) * 2 * GRP
NCC = -(-((E + CELLS * (P - 1)) // P) // (2 * GRP)) * 2 * GRP
BIG = 1.0e6
RND = 12582912.0
LOW = 1.0e30
SRC, ROWS, ATT, DLO, RECD = 0, 1, 2, 5, 6
SLO, SATT, RECS = 0, 1, 4


def bc(ap, axis, shape):
    return ap.unsqueeze(axis).to_broadcast(shape)


class Tensors:
    pass


class Steps:

    def __init__(self, engine, sem, base=0):
        self.engine, self.sem, self.base, self.n = engine, sem, base, 0

    def __call__(self, instruction):
        instruction.then_inc(self.sem, 1)
        self.n += 1
        self.engine.wait_ge(self.sem, self.base + self.n)


class Phase:

    def __init__(self, nc, name):
        self.nc, self.name, self.ctx, self.sems = nc, name, ExitStack(), []

    def __enter__(self):
        self.ctx.__enter__()
        return self

    def __exit__(self, *e):
        if e[0] is None:
            self.nc.clear_and_free_semaphores(self.sems)
            self.nc.all_engine_barrier()
        return self.ctx.__exit__(*e)

    def sb(self, name, shape, dt=F32):
        return self.ctx.enter_context(self.nc.sbuf_tensor(f"{self.name}_{name}", shape, dt))

    def ps(self, name, shape, dt=F32):
        return self.ctx.enter_context(self.nc.psum_tensor(f"{self.name}_{name}", shape, dt))

    def sem(self, name):
        self.sems.append(self.nc.alloc_semaphore(f"{self.name}_{name}"))
        return self.sems[-1]

    def pool_dma_sem(self, name):
        return self.nc.alloc_semaphore(f"{self.name}_{name}")


def constants(nc, g):
    with Phase(nc, "const") as ph:
        ii = ph.sb("ii", [P, P], I32)
        jj = ph.sb("jj", [P, NC // P], I32)
        made, steps = ph.sem("made"), ph.sem("steps")
        with nc.Block() as block:
            @block.gpsimd
            def _(pool):
                nc.gpsimd.iota(ii[:, :], [[1, P]], base=0, channel_multiplier=0)
                nc.gpsimd.iota(jj[:, :], [[P, NC // P]], base=0, channel_multiplier=1)
                nc.gpsimd.memset(g.ones[:, :], 1.0)
                nc.gpsimd.memset(g.ident[:, :], 1.0).then_inc(made, 1)
                pool.wait_ge(made, 1)
                nc.gpsimd.affine_select(out=g.tri[:, :], in_=g.ones[:, :], pattern=[[1, P]], compare_op=ALU.is_gt,
                                        fill=0.0, base=0, channel_multiplier=-1)
                nc.gpsimd.affine_select(out=g.ident[:, :], in_=g.ident[:, :], pattern=[[1, P]],
                                        compare_op=ALU.is_equal, fill=0.0, base=0,
                                        channel_multiplier=-1).then_inc(made, 1)

            @block.vector
            def _(dve):
                dve.wait_ge(made, 2)
                nc.vector.tensor_copy(g.iota[:, :], ii[:, :])
                nc.vector.tensor_copy(g.jcol[:, :], jj[:, :])


def split_nodes(nc, steps, ids, lo, tile):
    steps(nc.vector.tensor_copy(tile, ids))
    steps(nc.vector.tensor_scalar(lo, tile, 1.0 / NT, -0.5 + 0.5 / NT, ALU.mult, ALU.add))
    steps(nc.vector.tensor_scalar(lo, lo, RND, RND, ALU.add, ALU.subtract))
    steps(nc.vector.scalar_tensor_tensor(out=tile, in0=lo, scalar=-float(NT), in1=tile, op0=ALU.mult, op1=ALU.add))


def load_edges(nc, g, e, src, dst):
    full = P - 1
    rest = E - full * EC
    with Phase(nc, "load") as ph:
        dst_i = ph.sb("dst_i", [P, ECP], I32)
        oh = [[ph.sb(f"oh{b}{k}", [P, GRP, LO if k % 2 == 0 else NT], BF16) for k in range(4)] for b in range(2)]
        deg_ps = [ph.ps("degd", [LO, NT]), ph.ps("degs", [LO, NT])]
        zero = ph.sb("zero", [P, LO], BF16)
        cleared, loaded, split, padded = ph.sem("cleared"), ph.sem("loaded"), ph.sem("split"), ph.sem("padded")
        steps_s, ready, used, total = ph.sem("steps"), ph.sem("ready"), ph.sem("used"), ph.sem("total")
        groups = ECP // GRP
        with nc.Block() as block:
            @block.sync
            def _(sp):
                sp.wait_ge(cleared, 1)
                for ids, given in ((e.src, src), (dst_i, dst)):
                    sp.dma_start(ids[0:full, 0:EC], given[0:full * EC].rearrange("(p c) -> p c", p=full)
                                 ).then_inc(loaded, 16)
                    sp.dma_start(ids[full:P, 0:rest], given[full * EC:E].rearrange("(p c) -> p c", p=1)
                                 ).then_inc(loaded, 16)

            @block.gpsimd
            def _(pool):
                nc.gpsimd.memset(e.src[:, :], 0)
                nc.gpsimd.memset(zero[:, :], 0.0)
                nc.gpsimd.memset(dst_i[:, :], 0).then_inc(cleared, 1)
                pool.wait_ge(split, 1)
                for tile in (e.tiled, e.tiles):
                    nc.gpsimd.memset(tile[:, EC:ECP], -1.0)
                    last = nc.gpsimd.affine_select(out=tile[:, 0:EC], in_=tile[:, 0:EC], pattern=[[-1, EC]],
                                                   compare_op=ALU.is_ge, fill=-1.0, base=E - 1,
                                                   channel_multiplier=-EC)
                last.then_inc(padded, 1)

            @block.vector
            def _(dve):
                steps = Steps(dve, steps_s)
                dve.wait_ge(loaded, 64)
                split_nodes(nc, steps, dst_i[:, :], e.lod[:, :], e.tiled[:, :])
                split_nodes(nc, steps, e.src[:, :], e.los[:, :], e.tiles[:, :])
                nc.vector.memset(g.junk[:, :], 0.0).then_inc(split, 1)
                dve.wait_ge(padded, 1)
                with dve.Fori(0, groups // 2) as t:
                    for b in range(2):
                        dve.wait_ge(used, 2 * t + b + 1)
                        at = bass.ds((2 * t + b) * GRP, GRP)
                        for k, (keys, n) in enumerate(((e.lod, LO), (e.tiled, NT), (e.los, LO), (e.tiles, NT))):
                            last = nc.vector.tensor_tensor(oh[b][k][:, :, :], bc(g.iota[:, 0:n], 1, [P, GRP, n]),
                                                           bc(keys[:, at], 2, [P, GRP, n]), ALU.is_equal)
                        last.then_inc(ready, 1)
                dve.wait_ge(total, 1)
                nc.vector.tensor_copy(g.degd[:, :], deg_ps[0][:, :])
                nc.vector.tensor_copy(g.degs[:, :], deg_ps[1][:, :])

            @block.tensor
            def _(pe):
                pe.wait_ge(cleared, 1)
                for d in range(2):
                    last = nc.tensor.matmul(deg_ps[d][:, :], zero[:, :], zero[:, 0:NT], start=True, stop=False,
                                            skip_group_check=True)
                last.then_inc(used, 2)
                with pe.Fori(0, groups // 2) as t:
                    for b in range(2):
                        pe.wait_ge(ready, 2 * t + b + 1)
                        for d in range(2):
                            for c in range(GRP):
                                last = nc.tensor.matmul(deg_ps[d][:, :], oh[b][2 * d][:, c, :],
                                                        oh[b][2 * d + 1][:, c, :], start=False, stop=False,
                                                        skip_group_check=True)
                        last.then_inc(used, 1)
                for d in range(2):
                    last = nc.tensor.matmul(deg_ps[d][:, :], zero[:, :], zero[:, 0:NT], start=False, stop=True,
                                            skip_group_check=True)
                last.then_inc(total, 1)


def rank(nc, g, name, key, width, buckets, chunks, row, chunk_map, map_dram):
    mg = NC // P
    with Phase(nc, name) as ph:
        m = ph.sb("m", [P, width])
        run = ph.sb("run", [P, width])
        pos = ph.sb("pos", [P, width])
        cnt = ph.sb("cnt", [P, buckets])
        cc = ph.sb("cc", [P, buckets])
        cend = ph.sb("cend", [P, buckets])
        off = ph.sb("off", [P, buckets])
        bm = ph.sb("bm", [P, mg])
        bmi = ph.sb("bmi", [P, mg], I32)
        pre, tot = ph.ps("pre", [P, buckets]), ph.ps("tot", [P, buckets])
        scanned = ph.sem("scanned")
        steps_s, counted, summed, mapped, stored = (ph.sem(x) for x in
                                                    ("steps", "counted", "summed", "mapped", "stored"))
        with nc.Block() as block:
            @block.vector
            def _(dve):
                with dve.Fori(0, buckets) as b:
                    steps = Steps(dve, steps_s, b)
                    steps(nc.vector.tensor_scalar(m[:, :], key, g.iota[:, bass.ds(b, 1)], None, ALU.is_equal,
                                                  ALU.add, accum_out=cnt[:, bass.ds(b, 1)]))
                steps = Steps(dve, steps_s, buckets)
                steps(nc.vector.memset(pos[:, :], 0.0))
                nc.vector.memset(g.junk[:, :], 0.0).then_inc(counted, 1)
                dve.wait_ge(summed, 1)
                steps(nc.vector.tensor_scalar(cc[:, :], tot[:, :], P / 2 - 0.5, 1.0 / P, ALU.add, ALU.mult))
                steps(nc.vector.tensor_scalar(cc[:, :], cc[:, :], RND, RND, ALU.add, ALU.subtract))
                steps(nc.vector.tensor_tensor_scan(cend[:, :], cc[:, :], cc[:, :], 0.0, ALU.add, ALU.bypass))
                steps(nc.vector.tensor_tensor(cc[:, :], cend[:, :], cc[:, :], ALU.subtract))
                steps(nc.vector.tensor_scalar(cc[:, :], cc[:, :], float(P), -1.0, ALU.mult, ALU.add))
                steps(nc.vector.tensor_tensor(off[:, :], cc[:, :], pre[:, :], ALU.add))
                for q in range(mg):
                    steps(nc.vector.tensor_scalar(cc[:, :], cend[:, :], g.jcol[:, q:q + 1], None, ALU.is_le,
                                                  ALU.add, accum_out=bm[:, q:q + 1]))
                steps(nc.vector.tensor_scalar(bm[:, :], bm[:, :], float(buckets - 1), None, ALU.min))
                if chunk_map is not None:
                    chunk_map(steps, bm)
                steps(nc.vector.tensor_copy(bmi[:, :], bm[:, :]))
                nc.vector.memset(g.junk[:, :], 0.0).then_inc(mapped, 1)
                before = steps.base + steps.n
                with dve.Fori(0, buckets) as b:
                    steps = Steps(dve, steps_s, before + 3 * b)
                    steps(nc.vector.tensor_scalar(m[:, :], key, g.iota[:, bass.ds(b, 1)], None, ALU.is_equal))
                    steps(nc.vector.tensor_tensor_scan(run[:, :], m[:, :], m[:, :], off[:, bass.ds(b, 1)],
                                                       ALU.add, ALU.bypass))
                    dve.sem_inc(scanned, 1)
                    steps(nc.vector.copy_predicated(pos[:, :], m[:, :].bitcast(I32), run[:, :]))
                steps = Steps(dve, steps_s, before + 3 * buckets)
                steps(nc.vector.tensor_scalar(run[:, :], pos[:, :], 1.0 / P, -0.5 + 0.5 / P, ALU.mult, ALU.add))
                steps(nc.vector.tensor_scalar(run[:, :], run[:, :], RND, RND, ALU.add, ALU.subtract))
                steps(nc.vector.scalar_tensor_tensor(out=pos[:, :], in0=run[:, :], scalar=-float(P), in1=pos[:, :],
                                                     op0=ALU.mult, op1=ALU.add))
                steps(nc.vector.scalar_tensor_tensor(out=pos[:, :], in0=pos[:, :], scalar=float(chunks),
                                                     in1=run[:, :], op0=ALU.mult, op1=ALU.add))
                steps(nc.vector.tensor_scalar(m[:, :], key, 0.0, BIG, ALU.is_lt, ALU.mult))
                steps(nc.vector.tensor_tensor(pos[:, :], pos[:, :], m[:, :], ALU.add))
                steps(nc.vector.tensor_copy(row, pos[:, :]))

            @block.tensor
            def _(pe):
                pe.wait_ge(counted, 1)
                nc.tensor.matmul(pre[:, :], g.tri[:, :], cnt[:, :], start=True, stop=True)
                nc.tensor.matmul(tot[:, :], g.ones[:, :], cnt[:, :], start=True, stop=True).then_inc(summed, 1)

            @block.sync
            def _(sp):
                sp.wait_ge(mapped, 1)
                with nc.allow_non_contiguous_dma("a map of chunks, one word each"):
                    sp.dma_start(map_dram.rearrange("(g p) -> p g", p=P), bmi[:, :]).then_inc(stored, 16)
                sp.wait_ge(stored, 16)


def scatter_records(nc, g, e, attr, rec_d, rec_s):
    full = P - 1
    rest = E - full * EC
    fill_n = NC // 8
    with Phase(nc, "scat") as ph:
        att = ph.sb("att", [P, ECP, 3])
        fill_d = ph.sb("fill_d", [P, fill_n, RECD])
        fill_s = ph.sb("fill_s", [P, fill_n, RECS])
        at_d = [ph.sb(f"at_d{b}", [P, GRP], I32) for b in range(2)]
        at_s = [ph.sb(f"at_s{b}", [P, GRP], I32) for b in range(2)]
        out_d = [ph.sb(f"out_d{b}", [P, GRP, RECD]) for b in range(2)]
        out_s = [ph.sb(f"out_s{b}", [P, GRP, RECS]) for b in range(2)]
        cleared, loaded, filled = ph.sem("cleared"), ph.sem("loaded"), ph.sem("filled")
        started = ph.sem("started")
        ready = ph.sem("ready")
        sent = [ph.pool_dma_sem(f"sent{b}") for b in range(2)]
        groups = ECP // GRP
        with nc.Block() as block:
            @block.gpsimd
            def _(pool):
                nc.gpsimd.memset(att[:, :, :], 0.0)
                nc.gpsimd.memset(fill_d[:, :, :].bitcast(I32), 0)
                nc.gpsimd.memset(fill_s[:, :, :], 0.0).then_inc(cleared, 1)
                pool.wait_ge(cleared, 1)
                nc.gpsimd.memset(fill_d[:, :, ROWS:ROWS + 1].bitcast(I32), int(BIG))
                nc.gpsimd.memset(fill_d[:, :, DLO:DLO + 1], -1.0)
                nc.gpsimd.memset(fill_s[:, :, SLO:SLO + 1], -1.0).then_inc(cleared, 1)
                pool.wait_ge(filled, 16 * 16)
                with pool.Fori(0, groups // 2) as t:
                    for b in range(2):
                        pool.wait_ge(ready, 2 * t + b + 1)
                        pool.sem_inc(started, 1)
                        for c in range(GRP):
                            pool.indirect_dma_start(rec_d[:, :], bass.IndirectOffsetOnAxis(ap=at_d[b][:, c:c + 1], axis=0),
                                                    out_d[b][:, c, :], None, bounds_check=P * NC - 1,
                                                    oob_is_err=False).then_inc(sent[b], 16)
                            pool.indirect_dma_start(rec_s[:, :], bass.IndirectOffsetOnAxis(ap=at_s[b][:, c:c + 1], axis=0),
                                                    out_s[b][:, c, :], None, bounds_check=P * NC - 1,
                                                    oob_is_err=False).then_inc(sent[b], 16)
                for b in range(2):
                    pool.wait_ge(sent[b], 2 * GRP * 16 * (groups // 2))

            @block.sync
            def _(sp):
                sp.wait_ge(cleared, 2)
                sp.dma_start(att[0:full, 0:EC, :], attr[0:full * EC, :].rearrange("(p c) k -> p c k", p=full)
                             ).then_inc(loaded, 16)
                sp.dma_start(att[full:P, 0:rest, :], attr[full * EC:E, :].rearrange("(p c) k -> p c k", p=1)
                             ).then_inc(loaded, 16)
                for rec, fill in ((rec_d, fill_d), (rec_s, fill_s)):
                    rows = rec.rearrange("(p j) w -> p j w", p=P)
                    for q in range(8):
                        sp.dma_start(rows[:, q * fill_n:(q + 1) * fill_n, :], fill[:, :, :]).then_inc(filled, 16)

            @block.vector
            def _(dve):
                dve.wait_ge(loaded, 32)

                def stage(t, first):
                    for b in range(2):
                        if not first:
                            dve.wait_ge(sent[b], 2 * GRP * 16 * t)
                        at = bass.ds((2 * t + b) * GRP, GRP)
                        nc.vector.tensor_copy(out_d[b][:, :, SRC].bitcast(I32), e.src[:, at])
                        nc.vector.tensor_copy(out_d[b][:, :, ROWS].bitcast(I32), e.rows[:, at])
                        nc.vector.tensor_copy(out_d[b][:, :, ATT:ATT + 3], att[:, at, :])
                        nc.vector.tensor_copy(out_d[b][:, :, DLO], e.lod[:, at])
                        nc.vector.tensor_copy(out_s[b][:, :, SLO], e.los[:, at])
                        nc.vector.tensor_copy(out_s[b][:, :, SATT:SATT + 3], att[:, at, :])
                        nc.vector.tensor_copy(at_d[b][:, :], e.rowd[:, at])
                        nc.vector.tensor_copy(at_s[b][:, :], e.rows[:, at]).then_inc(ready, 1)

                stage(0, True)
                with dve.Fori(1, groups // 2) as t:
                    stage(t, False)


def values(nc, engine_type, row, n, hi):
    _, got = nc.values_load_multi_w_load_instructions(
        row, engines=(engine_type,), min_val=0, max_val=hi,
        skip_runtime_bounds_check_because="the map is clamped to the last bucket when it is made")
    return got


def load_table(nc, g, name, pairs):
    with Phase(nc, name) as ph:
        loaded = ph.sem("loaded")
        with nc.Block() as block:
            @block.sync
            def _(sp):
                with nc.allow_non_contiguous_dma("small weights, once"):
                    for to, of in pairs:
                        sp.dma_start(to, of).then_inc(loaded, 16)
                sp.wait_ge(loaded, 16 * len(pairs))


def propagate(nc, g, name, rec, tmap, table, acc):
    groups = NC // GRP
    with Phase(nc, name) as ph:
        at = [ph.sb(f"at{b}", [P, GRP], I32) for b in range(2)]
        rows = [ph.sb(f"rows{b}", [P, GRP, D]) for b in range(2)]
        oh = [ph.sb(f"oh{b}", [P, GRP, LO]) for b in range(2)]
        sums = [ph.ps(f"sums{b}", [LO, GRP, D]) for b in range(2)]
        at_ready, oh_ready, mm_done = ph.sem("at_ready"), ph.sem("oh_ready"), ph.sem("mm_done")
        added, steps_s = ph.sem("added"), ph.sem("steps")
        started = ph.sem("started")
        got = [ph.pool_dma_sem(f"got{b}") for b in range(2)]
        with nc.Block() as block:
            @block.scalar
            def _(act):
                def stage(t, first):
                    for b in range(2):
                        if not first:
                            act.wait_ge(got[b], GRP * 16 * t)
                        nc.scalar.copy(at[b][:, :], rec[:, bass.ds((2 * t + b) * GRP, GRP), SRC].bitcast(I32)
                                       ).then_inc(at_ready, 1)

                stage(0, True)
                with act.Fori(1, groups // 2) as t:
                    stage(t, False)

            @block.gpsimd
            def _(pool):
                def gather(t, first):
                    for b in range(2):
                        pool.wait_ge(at_ready, 2 * t + b + 1)
                        pool.sem_inc(started, 1)
                        if not first:
                            pool.wait_ge(mm_done, 2 * t + b - 1)
                            pool.sem_inc(started, 1)
                        for c in range(GRP):
                            pool.indirect_dma_start(rows[b][:, c, :], None, table[:, :],
                                                    bass.IndirectOffsetOnAxis(ap=at[b][:, c:c + 1], axis=0)
                                                    ).then_inc(got[b], 16)

                gather(0, True)
                with pool.Fori(1, groups // 2) as t:
                    gather(t, False)

            @block.vector
            def _(dve):
                steps = Steps(dve, steps_s)
                steps(nc.vector.memset(acc, 0.0))

                def hot(t, b, first):
                    if not first:
                        dve.wait_ge(mm_done, 2 * t + b - 1)
                    nc.vector.tensor_tensor(oh[b][:, :, :], bc(g.iota[:, 0:LO], 1, [P, GRP, LO]),
                                            bc(rec[:, bass.ds((2 * t + b) * GRP, GRP), DLO], 2, [P, GRP, LO]),
                                            ALU.is_equal).then_inc(oh_ready, 1)

                def add(t, b):
                    dve.wait_ge(mm_done, 2 * t + b + 1)
                    add_tiles(nc, dve, steps_s, 1, 2 * t + b, tmap, acc,
                              [sums[b][:, c:c + 1, :] for c in range(GRP)], ALU.add)
                    dve.sem_inc(added, 1)

                hot(0, 0, True)
                hot(0, 1, True)
                add(0, 0)
                add(0, 1)
                with dve.Fori(1, groups // 2) as t:
                    hot(t, 0, False)
                    hot(t, 1, False)
                    add(t, 0)
                    add(t, 1)

            @block.tensor
            def _(pe):
                def product(t, first):
                    for b in range(2):
                        pe.wait_ge(oh_ready, 2 * t + b + 1)
                        pe.wait_ge(got[b], GRP * 16 * (t + 1))
                        if not first:
                            pe.wait_ge(added, 2 * t + b - 1)
                        for c in range(GRP):
                            last = nc.tensor.matmul(sums[b][:, c, :], oh[b][:, c, :], rows[b][:, c, :],
                                                    start=True, stop=True)
                        last.then_inc(mm_done, 1)

                product(0, True)
                with pe.Fori(1, groups // 2) as t:
                    product(t, False)


def layer_norm_relu(nc, g, name, x, h):
    wide = [LO, NT, D]
    with Phase(nc, name) as ph:
        sq = ph.sb("sq", wide)
        mean, var = ph.sb("mean", [LO, NT]), ph.sb("var", [LO, NT])
        steps_s, asked, rooted = ph.sem("steps"), ph.sem("asked"), ph.sem("rooted")
        with nc.Block() as block:
            @block.vector
            def _(dve):
                steps = Steps(dve, steps_s)
                steps(nc.vector.tensor_reduce(mean[:, :], x, AX, ALU.add))
                steps(nc.vector.tensor_scalar(mean[:, :], mean[:, :], 1.0 / D, None, ALU.mult))
                steps(nc.vector.tensor_tensor(h, x, bc(mean[:, :], 2, wide), ALU.subtract))
                steps(nc.vector.tensor_tensor(sq[:, :, :], h, h, ALU.mult))
                steps(nc.vector.tensor_reduce(var[:, :], sq[:, :, :], AX, ALU.add))
                nc.vector.tensor_scalar(var[:, :], var[:, :], 1.0 / D, 1.0e-5, ALU.mult, ALU.add).then_inc(asked, 1)
                dve.wait_ge(rooted, 1)
                steps(nc.vector.reciprocal(var[:, :], var[:, :]))
                steps(nc.vector.tensor_tensor(h, h, bc(var[:, :], 2, wide), ALU.mult))
                steps(nc.vector.tensor_scalar(h, h, 0.0, None, ALU.max))

            @block.scalar
            def _(act):
                act.wait_ge(asked, 1)
                nc.scalar.activation(var[:, :], var[:, :], ACT.Sqrt).then_inc(rooted, 1)


def node_scales(nc, g, lam):
    with Phase(nc, "scales") as ph:
        steps_s, asked, rooted = ph.sem("steps"), ph.sem("asked"), ph.sem("rooted")
        with nc.Block() as block:
            @block.vector
            def _(dve):
                steps = Steps(dve, steps_s)
                steps(nc.vector.tensor_scalar(g.rdeg[:, :], g.degs[:, :], 1.0, None, ALU.max))
                steps(nc.vector.reciprocal(g.rdeg[:, :], g.rdeg[:, :]))
                steps(nc.vector.reciprocal(g.re[:, 0:1], lam))
                steps(nc.vector.tensor_scalar(g.re[:, 0:1], g.re[:, 0:1], 2.0, None, ALU.mult))
                steps(nc.vector.tensor_scalar(g.re[:, 1:2], g.re[:, 0:1], -1.0, None, ALU.mult))
                steps(nc.vector.tensor_scalar(g.re[:, 2:3], g.re[:, 0:1], 1.0, None, ALU.subtract))
                steps(nc.vector.tensor_scalar(g.re[:, 3:4], g.re[:, 0:1], -2.0, None, ALU.mult))
                steps(nc.vector.tensor_scalar(g.re[:, 4:5], g.re[:, 2:3], 2.0, None, ALU.mult))
                nc.vector.tensor_scalar(g.norm[:, :], g.degd[:, :], 1.0, None, ALU.max).then_inc(asked, 1)
                dve.wait_ge(rooted, 1)
                steps(nc.vector.reciprocal(g.norm[:, :], g.norm[:, :]))

            @block.scalar
            def _(act):
                act.wait_ge(asked, 1)
                nc.scalar.activation(g.norm[:, :], g.norm[:, :], ACT.Sqrt).then_inc(rooted, 1)


def store_scaled(nc, g, name, h, scale, table):
    shape = [LO, NT, h.shape[2]]
    with Phase(nc, name) as ph:
        out = ph.sb("out", shape)
        made, stored = ph.sem("made"), ph.sem("stored")
        with nc.Block() as block:
            @block.vector
            def _(dve):
                if scale is None:
                    nc.vector.tensor_copy(out[:, :, :], h).then_inc(made, 1)
                else:
                    nc.vector.tensor_tensor(out[:, :, :], h, bc(scale, 2, shape), ALU.mult).then_inc(made, 1)

            @block.sync
            def _(sp):
                sp.wait_ge(made, 1)
                sp.dma_start(table.rearrange("(p c) f -> p c f", p=LO), out[:, :, :]).then_inc(stored, 16)
                sp.wait_ge(stored, 16)


def chebyshev(nc, g, name, acc, cat, order):
    wide = [LO, NT, D]
    a, b = (1, 2) if order == 1 else (3, 4)
    before, to = cat[:, :, (order - 1) * D:order * D], cat[:, :, order * D:(order + 1) * D]
    with Phase(nc, name) as ph:
        steps_s = ph.sem("steps")
        with nc.Block() as block:
            @block.vector
            def _(dve):
                steps = Steps(dve, steps_s)
                steps(nc.vector.tensor_tensor(acc, acc, bc(g.norm[:, :], 2, wide), ALU.mult))
                steps(nc.vector.tensor_scalar(acc, acc, g.re[:, a:a + 1], None, ALU.mult))
                steps(nc.vector.scalar_tensor_tensor(out=to, in0=before, scalar=g.re[:, b:b + 1], in1=acc,
                                                     op0=ALU.mult, op1=ALU.add))
                if order == 2:
                    steps(nc.vector.tensor_tensor(to, to, cat[:, :, 0:D], ALU.subtract))


def node_linear(nc, g, name, x, K, w, bias, FO, y, relu=False, transposed=False):
    T = 4
    with Phase(nc, name) as ph:
        xs = ph.sb("xs", [K, T, LO] if transposed else [LO, T, K])
        xt = ph.sb("xt", [K, T, LO])
        ys = ph.sb("ys", [LO, T, FO])
        pt, py = ph.ps("pt", [K, T, LO]), ph.ps("py", [LO, T, FO])
        staged, turned, kept, made, steps_s, begun = (ph.sem(s) for s in ("staged", "turned", "kept", "made",
                                                                           "steps", "begun"))
        with nc.Block() as block:
            @block.vector
            def _(dve):
                with dve.Fori(0, NT // T) as t:
                    steps = Steps(dve, steps_s, 2 * t)
                    at = bass.ds(t * T, T)
                    nc.vector.tensor_copy(xs[:, :, :], x[:, at, :]).then_inc(staged, 1)
                    if not transposed:
                        dve.wait_ge(turned, t + 1)
                        nc.vector.tensor_copy(xt[:, :, :], pt[:, :, :]).then_inc(kept, 1)
                    dve.wait_ge(made, t + 1)
                    if bias is None:
                        steps(nc.vector.tensor_copy(ys[:, :, :], py[:, :, :]))
                    else:
                        steps(nc.vector.tensor_tensor(ys[:, :, :], py[:, :, :], bc(bias, 1, [LO, T, FO]), ALU.add))
                    steps(nc.vector.tensor_scalar(y[:, at, :], ys[:, :, :], 0.0 if relu else 1.0, None,
                                                  ALU.max if relu else ALU.mult))

            @block.tensor
            def _(pe):
                with pe.Fori(0, NT // T) as t:
                    pe.wait_ge(staged, t + 1)
                    pe.sem_inc(begun, 1)
                    if not transposed:
                        for c in range(T):
                            last = nc.tensor.transpose(pt[:, c, :], xs[:, c, :], g.ident[0:LO, 0:LO])
                        last.then_inc(turned, 1)
                        pe.wait_ge(kept, t + 1)
                    for c in range(T):
                        last = nc.tensor.matmul(py[:, c, :], (xs if transposed else xt)[:, c, :], w,
                                                start=True, stop=True)
                    last.then_inc(made, 1)


def scale_bias_elu(nc, g, name, y, F, scale, bias):
    wide = [LO, NT, F]
    with Phase(nc, name) as ph:
        low = ph.sb("low", wide)
        steps_s, asked, done = ph.sem("steps"), ph.sem("asked"), ph.sem("done")
        with nc.Block() as block:
            @block.vector
            def _(dve):
                steps = Steps(dve, steps_s)
                if scale is not None:
                    steps(nc.vector.tensor_tensor(y, y, bc(scale, 2, wide), ALU.mult))
                if bias is not None:
                    steps(nc.vector.tensor_tensor(y, y, bc(bias, 1, wide), ALU.add))
                nc.vector.tensor_scalar(low[:, :, :], y, 0.0, None, ALU.min).then_inc(asked, 1)
                dve.wait_ge(done, 1)
                steps(nc.vector.tensor_scalar(low[:, :, :], low[:, :, :], 1.0, None, ALU.subtract))
                steps(nc.vector.scalar_tensor_tensor(out=y, in0=y, scalar=0.0, in1=low[:, :, :],
                                                     op0=ALU.max, op1=ALU.add))

            @block.scalar
            def _(act):
                act.wait_ge(asked, 1)
                nc.scalar.activation(low[:, :, :], low[:, :, :], ACT.Exp).then_inc(done, 1)


def add_tiles(nc, dve, sem, base, group, tmap, acc, sums, op):
    tiles = values(nc, mybir.EngineType.DVE, tmap[0:1, bass.ds(group * GRP, GRP)], GRP, NT - 1)
    steps = Steps(dve, sem, group * GRP + base)
    for c in range(GRP):
        to = acc[:, bass.ds(tiles[c], 1), :]
        steps(nc.vector.tensor_tensor(to, to, sums[c], op))


def attention_scores(nc, g, rec, tmap, table, fse, fd, attn, lgs, mx):
    groups = NC // GRP
    with Phase(nc, "att1") as ph:
        at = [ph.sb(f"at{b}", [P, GRP], I32) for b in range(2)]
        rows = [ph.sb(f"rows{b}", [P, GRP, D]) for b in range(2)]
        oh = [ph.sb(f"oh{b}", [P, GRP, LO]) for b in range(2)]
        ohT = ph.sb("ohT", [LO, GRP, P])
        sc = ph.sb("sc", [P, GRP, D])
        am = [ph.sb(f"am{b}", [P, GRP, LO]) for b in range(2)]
        red = ph.sb("red", [LO, GRP])
        pt = [ph.ps(f"pt{h}", [LO, GRP // 2, P]) for h in range(2)]
        pa = [ph.ps(f"pa{h}", [LO, GRP // 2, P]) for h in range(2)]
        pe_fd = ph.ps("pe_fd", [P, GRP, D])
        (at_ready, oh_ready, turned, kept, fd_ready, masked, am_ready, am_turned, reduced, steps_s, steps_m) = (
            ph.sem(s) for s in ("at_ready", "oh_ready", "turned", "kept", "fd_ready", "masked",
                                "am_ready", "am_turned", "reduced", "steps", "steps_m"))
        started = ph.sem("started")
        got = [ph.pool_dma_sem(f"got{b}") for b in range(2)]
        stored = [ph.sem(f"stored{b}") for b in range(2)]
        with nc.Block() as block:
            @block.scalar
            def _(act):
                def group(t, b, first):
                    n = 2 * t + b
                    if not first:
                        act.wait_ge(got[b], GRP * 16 * t)
                    nc.scalar.copy(at[b][:, :], rec[:, bass.ds(n * GRP, GRP), SRC].bitcast(I32)).then_inc(at_ready, 1)
                    act.wait_ge(oh_ready, n + 1)
                    if not first:
                        act.wait_ge(am_turned, n - 1)
                    nc.scalar.activation(am[b][:, :, :], oh[b][:, :, :], ACT.Copy, bias=-LOW, scale=LOW
                                         ).then_inc(masked, 1)
                    act.wait_ge(turned, n + 1)
                    if not first or b == 1:
                        act.wait_ge(fd_ready, n)
                    for h in range(2):
                        last = nc.scalar.copy(ohT[:, h * GRP // 2:(h + 1) * GRP // 2, :], pt[h][:, :, :])
                    last.then_inc(kept, 1)

                group(0, 0, True)
                group(0, 1, True)
                with act.Fori(1, groups // 2) as t:
                    group(t, 0, False)
                    group(t, 1, False)

            @block.gpsimd
            def _(pool):
                def gather(t, first):
                    for b in range(2):
                        pool.wait_ge(at_ready, 2 * t + b + 1)
                        pool.sem_inc(started, 1)
                        if not first:
                            pool.wait_ge(am_ready, 2 * t + b - 1)
                            pool.sem_inc(started, 1)
                            pool.wait_ge(stored[b], 16 * t)
                            pool.sem_inc(started, 1)
                        for c in range(GRP):
                            pool.indirect_dma_start(rows[b][:, c, :], None, table[:, :],
                                                    bass.IndirectOffsetOnAxis(ap=at[b][:, c:c + 1], axis=0)
                                                    ).then_inc(got[b], 16)

                gather(0, True)
                with pool.Fori(1, groups // 2) as t:
                    gather(t, False)

            @block.sync
            def _(sp):
                to = fse.rearrange("(p j) f -> p j f", p=P)
                with sp.Fori(0, groups // 2) as t:
                    for b in range(2):
                        sp.wait_ge(got[b], GRP * 16 * (t + 1))
                        sp.dma_start(to[:, bass.ds((2 * t + b) * GRP, GRP), :], rows[b][:, :, :]
                                     ).then_inc(stored[b], 16)
                for b in range(2):
                    sp.wait_ge(stored[b], 16 * (groups // 2))

            @block.vector
            def _(dve):
                def hot(t, b, first):
                    if not first:
                        dve.wait_ge(masked, 2 * t + b - 1)
                        dve.wait_ge(turned, 2 * t + b - 1)
                    nc.vector.tensor_tensor(oh[b][:, :, :], bc(g.iota[:, 0:LO], 1, [P, GRP, LO]),
                                            bc(rec[:, bass.ds((2 * t + b) * GRP, GRP), DLO], 2, [P, GRP, LO]),
                                            ALU.is_equal).then_inc(oh_ready, 1)

                def score(t, b):
                    n = 2 * t + b
                    steps = Steps(dve, steps_s, 4 * n)
                    lg = lgs[:, bass.ds(n * GRP, GRP)]
                    dve.wait_ge(got[b], GRP * 16 * (t + 1))
                    dve.wait_ge(fd_ready, n + 1)
                    steps(nc.vector.tensor_tensor(sc[:, :, :], pe_fd[:, :, :], rows[b][:, :, :], ALU.add))
                    steps(nc.vector.scalar_tensor_tensor(out=sc[:, :, :], in0=sc[:, :, :], scalar=0.2,
                                                         in1=sc[:, :, :], op0=ALU.mult, op1=ALU.max))
                    steps(nc.vector.tensor_tensor(sc[:, :, :], sc[:, :, :], bc(attn, 1, [P, GRP, D]), ALU.mult))
                    steps(nc.vector.tensor_reduce(lg, sc[:, :, :], AX, ALU.add))
                    dve.wait_ge(masked, n + 1)
                    nc.vector.tensor_tensor(am[b][:, :, :], am[b][:, :, :], bc(lg, 2, [P, GRP, LO]),
                                            ALU.add).then_inc(am_ready, 1)

                def highest(n):
                    dve.wait_ge(am_turned, n + 1)
                    for h in range(2):
                        last = nc.vector.tensor_reduce(red[:, h * GRP // 2:(h + 1) * GRP // 2], pa[h][:, :, :],
                                                       AX, ALU.max)
                    last.then_inc(reduced, 1)
                    dve.wait_ge(reduced, n + 1)
                    add_tiles(nc, dve, steps_m, 1, n, tmap, mx, [red[:, c:c + 1].unsqueeze(2) for c in range(GRP)], ALU.max)

                steps = Steps(dve, steps_m)
                steps(nc.vector.memset(mx, -LOW))
                hot(0, 0, True)
                hot(0, 1, True)
                score(0, 0)
                score(0, 1)
                highest(0)
                with dve.Fori(1, groups // 2) as t:
                    hot(t, 0, False)
                    score(t, 0)
                    highest(2 * t - 1)
                    hot(t, 1, False)
                    score(t, 1)
                    highest(2 * t)
                highest(groups - 1)

            @block.tensor
            def _(pe):
                def turn_scores(n, b, first):
                    pe.wait_ge(am_ready, n + 1)
                    if not first:
                        pe.wait_ge(reduced, n)
                    for c in range(GRP):
                        last = nc.tensor.transpose(pa[c // (GRP // 2)][:, c % (GRP // 2), :], am[b][:, c, :],
                                                   g.ident[:, :])
                    last.then_inc(am_turned, 1)

                def group(t, b, first):
                    n = 2 * t + b
                    pe.wait_ge(oh_ready, n + 1)
                    if not (first and b == 0):
                        pe.wait_ge(kept, n)
                    for c in range(GRP):
                        last = nc.tensor.transpose(pt[c // (GRP // 2)][:, c % (GRP // 2), :], oh[b][:, c, :],
                                                   g.ident[:, :])
                    last.then_inc(turned, 1)
                    tiles = values(nc, mybir.EngineType.PE, tmap[0:1, bass.ds(n * GRP, GRP)], GRP, NT - 1)
                    pe.wait_ge(kept, n + 1)
                    if not (first and b == 0):
                        pe.wait_ge(am_ready, n)
                    for c in range(GRP):
                        last = nc.tensor.matmul(pe_fd[:, c, :], ohT[:, c, :], fd[:, bass.ds(tiles[c], 1), :],
                                                start=True, stop=True)
                    last.then_inc(fd_ready, 1)
                    if not (first and b == 0):
                        turn_scores(n - 1, 1 - b, first)

                group(0, 0, True)
                group(0, 1, True)
                with pe.Fori(1, groups // 2) as t:
                    group(t, 0, False)
                    group(t, 1, False)
                turn_scores(groups - 1, 1, False)


def attention_sums(nc, g, rec, tmap, fse, lgs, mx, acc):
    groups = NC // GRP
    W = D + 1
    with Phase(nc, "att2") as ph:
        rows = [ph.sb(f"rows{b}", [P, GRP, D]) for b in range(2)]
        oh = [ph.sb(f"oh{b}", [P, GRP, LO]) for b in range(2)]
        ohT = ph.sb("ohT", [LO, GRP, P])
        ex = ph.sb("ex", [P, GRP])
        msg = [ph.sb(f"msg{b}", [P, GRP, W]) for b in range(2)]
        pt = [ph.ps(f"pt{h}", [LO, GRP // 2, P]) for h in range(2)]
        pm = ph.ps("pm", [P, GRP])
        sums = [ph.ps(f"sums{b}", [LO, GRP, W]) for b in range(2)]
        oh_ready, turned, kept, m_ready, less, exped, msg_ready, mm_done, added, steps_s, steps_a = (
            ph.sem(s) for s in ("oh_ready", "turned", "kept", "m_ready", "less", "exped", "msg_ready", "mm_done",
                                "added", "steps", "steps_a"))
        loaded = [ph.sem(f"loaded{b}") for b in range(2)]
        with nc.Block() as block:
            @block.sync
            def _(sp):
                of = fse.rearrange("(p j) f -> p j f", p=P)

                def load(t, first):
                    for b in range(2):
                        if not first:
                            sp.wait_ge(msg_ready, 2 * t + b - 1)
                        sp.dma_start(rows[b][:, :, :], of[:, bass.ds((2 * t + b) * GRP, GRP), :]
                                     ).then_inc(loaded[b], 16)

                load(0, True)
                with sp.Fori(1, groups // 2) as t:
                    load(t, False)

            @block.scalar
            def _(act):
                def group(n, first):
                    act.wait_ge(turned, n + 1)
                    if not first:
                        act.wait_ge(m_ready, n)
                    for h in range(2):
                        last = nc.scalar.copy(ohT[:, h * GRP // 2:(h + 1) * GRP // 2, :], pt[h][:, :, :])
                    last.then_inc(kept, 1)
                    act.wait_ge(less, n + 1)
                    nc.scalar.activation(ex[:, :], ex[:, :], ACT.Exp).then_inc(exped, 1)

                group(0, True)
                with act.Fori(1, groups) as n:
                    group(n, False)

            @block.vector
            def _(dve):
                def hot(n, b, first):
                    if not first:
                        dve.wait_ge(mm_done, n - 1)
                    nc.vector.tensor_tensor(oh[b][:, :, :], bc(g.iota[:, 0:LO], 1, [P, GRP, LO]),
                                            bc(rec[:, bass.ds(n * GRP, GRP), DLO], 2, [P, GRP, LO]),
                                            ALU.is_equal).then_inc(oh_ready, 1)

                def message(t, b, first):
                    n = 2 * t + b
                    steps = Steps(dve, steps_s, 2 * n)
                    dve.wait_ge(m_ready, n + 1)
                    steps(nc.vector.tensor_tensor(ex[:, :], lgs[:, bass.ds(n * GRP, GRP)], pm[:, :], ALU.subtract))
                    nc.vector.tensor_scalar(ex[:, :], ex[:, :], 0.0, None, ALU.min).then_inc(less, 1)
                    dve.wait_ge(exped, n + 1)
                    if not first:
                        dve.wait_ge(mm_done, n - 1)
                    dve.wait_ge(loaded[b], 16 * (t + 1))
                    nc.vector.tensor_tensor(msg[b][:, :, 0:D], rows[b][:, :, :], bc(ex[:, :], 2, [P, GRP, D]),
                                            ALU.mult)
                    steps(nc.vector.tensor_copy(msg[b][:, :, D], ex[:, :]))
                    dve.sem_inc(msg_ready, 1)

                def add(n, b):
                    dve.wait_ge(mm_done, n + 1)
                    add_tiles(nc, dve, steps_a, 1, n, tmap, acc, [sums[b][:, c:c + 1, :] for c in range(GRP)],
                              ALU.add)
                    dve.sem_inc(added, 1)

                steps = Steps(dve, steps_a)
                steps(nc.vector.memset(acc, 0.0))
                hot(0, 0, True)
                hot(1, 1, True)
                message(0, 0, True)
                message(0, 1, True)
                add(0, 0)
                with dve.Fori(1, groups // 2) as t:
                    for b in range(2):
                        hot(2 * t + b, b, False)
                        message(t, b, False)
                        add(2 * t + b - 1, 1 - b)
                add(groups - 1, 1)

            @block.tensor
            def _(pe):
                def total(n, b, first):
                    pe.wait_ge(msg_ready, n + 1)
                    if not first:
                        pe.wait_ge(added, n - 1)
                    for c in range(GRP):
                        last = nc.tensor.matmul(sums[b][:, c, :], oh[b][:, c, :], msg[b][:, c, :],
                                                start=True, stop=True)
                    last.then_inc(mm_done, 1)

                def turn(n, b, first):
                    pe.wait_ge(oh_ready, n + 1)
                    if not first:
                        pe.wait_ge(kept, n)
                    for c in range(GRP):
                        last = nc.tensor.transpose(pt[c // (GRP // 2)][:, c % (GRP // 2), :], oh[b][:, c, :],
                                                   g.ident[:, :])
                    last.then_inc(turned, 1)
                    tiles = values(nc, mybir.EngineType.PE, tmap[0:1, bass.ds(n * GRP, GRP)], GRP, NT - 1)
                    pe.wait_ge(kept, n + 1)
                    if not first:
                        pe.wait_ge(less, n)
                    for c in range(GRP):
                        last = nc.tensor.matmul(pm[:, c:c + 1], ohT[:, c, :], mx[:, bass.ds(tiles[c], 1), :],
                                                start=True, stop=True)
                    last.then_inc(m_ready, 1)

                turn(0, 0, True)
                turn(1, 1, False)
                total(0, 0, True)
                total(1, 1, True)
                with pe.Fori(1, groups // 2) as t:
                    for b in range(2):
                        turn(2 * t + b, b, False)
                        total(2 * t + b, b, False)


def attention_end(nc, g, acc, bias, x):
    with Phase(nc, "att3") as ph:
        den = ph.sb("den", [LO, NT])
        one = ph.sb("one", [LO, NT])
        steps_s = ph.sem("steps")
        wide = [LO, NT, D]
        with nc.Block() as block:
            @block.vector
            def _(dve):
                steps = Steps(dve, steps_s)
                steps(nc.vector.tensor_scalar(one[:, :], acc[:, :, D], 0.0, None, ALU.is_equal))
                steps(nc.vector.tensor_tensor(den[:, :], acc[:, :, D], one[:, :], ALU.add))
                steps(nc.vector.reciprocal(den[:, :], den[:, :]))
                steps(nc.vector.tensor_tensor(acc[:, :, 0:D], acc[:, :, 0:D], bc(den[:, :], 2, wide), ALU.mult))
                steps(nc.vector.tensor_tensor(acc[:, :, 0:D], acc[:, :, 0:D], bc(bias, 1, wide), ALU.add))
                steps(nc.vector.tensor_tensor(x, x, acc[:, :, 0:D], ALU.add))


def cell_of(nc, steps, pos, i0, frac):
    steps(nc.vector.tensor_scalar(frac, pos, 1.0, None, ALU.is_ge))
    steps(nc.vector.scalar_tensor_tensor(out=i0, in0=pos, scalar=2.0, in1=frac, op0=ALU.is_ge, op1=ALU.add))
    steps(nc.vector.scalar_tensor_tensor(out=i0, in0=pos, scalar=3.0, in1=i0, op0=ALU.is_ge, op1=ALU.add))
    steps(nc.vector.tensor_tensor(frac, pos, i0, ALU.subtract))


def basis_sums(nc, g, rec, tmap, acc):
    groups = NC // GRP
    half = GRP // 2
    with Phase(nc, "basis") as ph:
        k5 = ph.sb("k5", [P, 2, KS])
        pos = ph.sb("pos", [P, GRP, 3])
        cell = ph.sb("cell", [P, GRP, 3])
        frac = ph.sb("frac", [P, GRP, 3])
        rest = ph.sb("rest", [P, GRP, 3])
        left = ph.sb("left", [P, GRP * 3, KS])
        hat = ph.sb("hat", [P, GRP * 3, KS])
        h01 = ph.sb("h01", [P, GRP, KS, KS])
        bas = [ph.sb(f"bas{b}", [P, GRP, K3]) for b in range(2)]
        oh = [ph.sb(f"oh{b}", [P, GRP, LO]) for b in range(2)]
        sums = [[ph.ps(f"sums{b}{h}", [K3, half, LO]) for h in range(2)] for b in range(2)]
        ready, mm_done, added, steps_s, steps_a = (ph.sem(s) for s in
                                                   ("ready", "mm_done", "added", "steps", "steps_a"))
        PER = 4 + 2 + 5
        with nc.Block() as block:
            @block.vector
            def _(dve):
                def build(n, b, first):
                    at = bass.ds(n * GRP, GRP)
                    steps = Steps(dve, steps_s, n * PER + 1)
                    steps(nc.vector.tensor_scalar(pos[:, :, :], rec[:, at, SATT:SATT + 3], float(KS - 1), None,
                                                  ALU.mult))
                    cell_of(nc, steps, pos[:, :, :], cell[:, :, :], frac[:, :, :])
                    steps(nc.vector.tensor_scalar(rest[:, :, :], frac[:, :, :], -1.0, 1.0, ALU.mult, ALU.add))
                    flat = [a[:, :, :].rearrange("p c d -> p (c d)") for a in (cell, frac, rest)]
                    shape = [P, GRP * 3, KS]
                    nc.vector.tensor_tensor(left[:, :, :], bc(k5[:, 0, :], 1, shape), bc(flat[0], 2, shape),
                                            ALU.is_equal)
                    steps(nc.vector.tensor_tensor(hat[:, :, :], bc(k5[:, 1, :], 1, shape), bc(flat[0], 2, shape),
                                                  ALU.is_equal))
                    nc.vector.tensor_tensor(left[:, :, :], left[:, :, :], bc(flat[2], 2, shape), ALU.mult)
                    steps(nc.vector.tensor_tensor(hat[:, :, :], hat[:, :, :], bc(flat[1], 2, shape), ALU.mult))
                    steps(nc.vector.tensor_tensor(hat[:, :, :], hat[:, :, :], left[:, :, :], ALU.add))
                    hats = hat[:, :, :].rearrange("p (c d) k -> p c d k", d=3)
                    steps(nc.vector.tensor_tensor(h01[:, :, :, :],
                                                  bc(hats[:, :, 0, :], 3, [P, GRP, KS, KS]),
                                                  bc(hats[:, :, 1, :], 2, [P, GRP, KS, KS]), ALU.mult))
                    if not first:
                        dve.wait_ge(mm_done, n - 1)
                    big = [P, GRP, KS * KS, KS]
                    steps(nc.vector.tensor_tensor(
                        bas[b][:, :, :].rearrange("p c (a k) -> p c a k", k=KS),
                        bc(h01[:, :, :, :].rearrange("p c a k -> p c (a k)"), 3, big),
                        bc(hats[:, :, 2, :], 2, big), ALU.mult))
                    nc.vector.tensor_tensor(oh[b][:, :, :], bc(g.iota[:, 0:LO], 1, [P, GRP, LO]),
                                            bc(rec[:, at, SLO], 2, [P, GRP, LO]), ALU.is_equal).then_inc(ready, 1)
                    assert steps.n == PER

                def add(n, b):
                    dve.wait_ge(mm_done, n + 1)
                    add_tiles(nc, dve, steps_a, 1, n, tmap, acc,
                              [sums[b][c // half][:, c % half:c % half + 1, :] for c in range(GRP)], ALU.add)
                    dve.sem_inc(added, 1)

                steps = Steps(dve, steps_s)
                nc.vector.tensor_scalar(k5[:, 1, :], g.iota[:, 0:KS], 1.0, None, ALU.subtract)
                steps(nc.vector.tensor_copy(k5[:, 0, :], g.iota[:, 0:KS]))
                steps = Steps(dve, steps_a)
                steps(nc.vector.memset(acc, 0.0))
                build(0, 0, True)
                build(1, 1, True)
                add(0, 0)
                with dve.Fori(1, groups // 2) as t:
                    for b in range(2):
                        build(2 * t + b, b, False)
                        add(2 * t + b - 1, 1 - b)
                add(groups - 1, 1)

            @block.tensor
            def _(pe):
                def group(n, b, first):
                    pe.wait_ge(ready, n + 1)
                    if not first:
                        pe.wait_ge(added, n - 1)
                    for c in range(GRP):
                        last = nc.tensor.matmul(sums[b][c // half][:, c % half, :], bas[b][:, c, :],
                                                oh[b][:, c, :], start=True, stop=True)
                    last.then_inc(mm_done, 1)

                group(0, 0, True)
                group(1, 1, True)
                with pe.Fori(1, groups // 2) as t:
                    for b in range(2):
                        group(2 * t + b, b, False)


def spline_cells(nc, g, name, att, dlo, key, frac):
    with Phase(nc, name) as ph:
        pos = ph.sb("pos", [P, NC, 3])
        i0 = ph.sb("i0", [P, NC, 3])
        steps_s = ph.sem("steps")
        with nc.Block() as block:
            @block.vector
            def _(dve):
                steps = Steps(dve, steps_s)
                steps(nc.vector.tensor_scalar(pos[:, :, :], att, float(KS - 1), None, ALU.mult))
                cell_of(nc, steps, pos[:, :, :], i0[:, :, :], frac)
                steps(nc.vector.scalar_tensor_tensor(out=key, in0=i0[:, :, 0], scalar=4.0, in1=i0[:, :, 1],
                                                     op0=ALU.mult, op1=ALU.add))
                steps(nc.vector.scalar_tensor_tensor(out=key, in0=key, scalar=4.0, in1=i0[:, :, 2],
                                                     op0=ALU.mult, op1=ALU.add))
                steps(nc.vector.tensor_scalar(pos[:, :, 0], dlo, 0.0, None, ALU.is_ge))
                steps(nc.vector.scalar_tensor_tensor(out=key, in0=key, scalar=1.0, in1=pos[:, :, 0],
                                                     op0=ALU.add, op1=ALU.mult))
                steps(nc.vector.tensor_scalar(key, key, 1.0, None, ALU.subtract))


def cell_offsets(nc, ph_tmp, width):
    q, i0, i1 = ph_tmp

    def convert(steps, bm):
        steps(nc.vector.tensor_scalar(i0[:, :], bm[:, :], 1.0 / 16, -0.5 + 0.5 / 16, ALU.mult, ALU.add))
        steps(nc.vector.tensor_scalar(i0[:, :], i0[:, :], RND, RND, ALU.add, ALU.subtract))
        steps(nc.vector.scalar_tensor_tensor(out=q[:, :], in0=i0[:, :], scalar=-16.0, in1=bm[:, :],
                                             op0=ALU.mult, op1=ALU.add))
        steps(nc.vector.tensor_scalar(i1[:, :], q[:, :], 1.0 / 4, -0.5 + 0.5 / 4, ALU.mult, ALU.add))
        steps(nc.vector.tensor_scalar(i1[:, :], i1[:, :], RND, RND, ALU.add, ALU.subtract))
        steps(nc.vector.scalar_tensor_tensor(out=bm[:, :], in0=i0[:, :], scalar=9.0, in1=bm[:, :],
                                             op0=ALU.mult, op1=ALU.add))
        steps(nc.vector.tensor_tensor(bm[:, :], bm[:, :], i1[:, :], ALU.add))
        steps(nc.vector.tensor_scalar(bm[:, :], bm[:, :], float(width), None, ALU.mult))

    return convert


def fill_rows(nc, name, tables):
    with Phase(nc, name) as ph:
        filled, cleared, marked = ph.sem("filled"), ph.sem("cleared"), ph.sem("marked")
        fills = []
        for n, (table, rows, width, mark) in enumerate(tables):
            fills.append(ph.sb(f"fill{n}", [P, rows // P // 16, width]))
        with nc.Block() as block:
            @block.gpsimd
            def _(pool):
                for fill in fills:
                    last = nc.gpsimd.memset(fill[:, :, :], 0.0)
                last.then_inc(cleared, 1)
                pool.wait_ge(cleared, 1)
                for fill, (table, rows, width, mark) in zip(fills, tables):
                    if mark:
                        last = nc.gpsimd.memset(fill[:, :, width - 1:width].bitcast(I32), int(BIG))
                last.then_inc(marked, 1)

            @block.sync
            def _(sp):
                sp.wait_ge(marked, 1)
                for fill, (table, rows, width, mark) in zip(fills, tables):
                    n = rows // P // 16
                    to = table.rearrange("(p j) w -> p j w", p=P)
                    for q in range(16):
                        sp.dma_start(to[:, q * n:(q + 1) * n, :], fill[:, :, :]).then_inc(filled, 16)
                sp.wait_ge(filled, 256 * len(fills))


def to_cells(nc, g, name, rec, tmap, h, F, frac, rowc, table):
    groups = NC // GRP
    W = F + 4
    with Phase(nc, name) as ph:
        at = [ph.sb(f"at{b}", [P, GRP], I32) for b in range(2)]
        pay = [ph.sb(f"pay{b}", [P, GRP, W]) for b in range(2)]
        oh = [ph.sb(f"oh{b}", [P, GRP, LO]) for b in range(2)]
        ohT = [ph.sb(f"ohT{b}", [LO, GRP, P]) for b in range(2)]
        pt = [ph.ps(f"pt{k}", [LO, GRP // 2, P]) for k in range(2)]
        px = [ph.ps(f"px{b}", [P, GRP, F]) for b in range(2)]
        oh_ready, turned, kept, spread, ready = (ph.sem(s) for s in ("oh_ready", "turned", "kept", "spread", "ready"))
        started = ph.sem("started")
        sent = [ph.pool_dma_sem(f"sent{b}") for b in range(2)]
        with nc.Block() as block:
            @block.scalar
            def _(act):
                def group(n, b, first):
                    act.wait_ge(turned, n + 1)
                    if not first:
                        act.wait_ge(spread, n - 1)
                    for k in range(2):
                        last = nc.scalar.copy(ohT[b][:, k * GRP // 2:(k + 1) * GRP // 2, :], pt[k][:, :, :])
                    last.then_inc(kept, 1)

                group(0, 0, True)
                group(1, 1, True)
                with act.Fori(1, groups // 2) as t:
                    for b in range(2):
                        group(2 * t + b, b, False)

            @block.vector
            def _(dve):
                def hot(n, b, first):
                    if not first:
                        dve.wait_ge(turned, n - 1)
                    nc.vector.tensor_tensor(oh[b][:, :, :], bc(g.iota[:, 0:LO], 1, [P, GRP, LO]),
                                            bc(rec[:, bass.ds(n * GRP, GRP), DLO], 2, [P, GRP, LO]),
                                            ALU.is_equal).then_inc(oh_ready, 1)

                def pack(t, b, first):
                    n = 2 * t + b
                    slots = bass.ds(n * GRP, GRP)
                    if not first:
                        dve.wait_ge(sent[b], GRP * 16 * t)
                    nc.vector.tensor_copy(pay[b][:, :, F:F + 3], frac[:, slots, :])
                    nc.vector.tensor_copy(pay[b][:, :, F + 3].bitcast(I32), rec[:, slots, ROWS].bitcast(I32))
                    nc.vector.tensor_copy(at[b][:, :], rowc[:, slots])
                    dve.wait_ge(spread, n + 1)
                    nc.vector.tensor_copy(pay[b][:, :, 0:F], px[b][:, :, :]).then_inc(ready, 1)

                hot(0, 0, True)
                hot(1, 1, True)
                pack(0, 0, True)
                pack(0, 1, True)
                with dve.Fori(1, groups // 2) as t:
                    hot(2 * t, 0, False)
                    hot(2 * t + 1, 1, False)
                    pack(t, 0, False)
                    pack(t, 1, False)

            @block.tensor
            def _(pe):
                def turn(n, b, first):
                    pe.wait_ge(oh_ready, n + 1)
                    if not first:
                        pe.wait_ge(kept, n)
                    for c in range(GRP):
                        last = nc.tensor.transpose(pt[c // (GRP // 2)][:, c % (GRP // 2), :], oh[b][:, c, :],
                                                   g.ident[:, :])
                    last.then_inc(turned, 1)

                def spread_rows(n, b, first):
                    tiles = values(nc, mybir.EngineType.PE, tmap[0:1, bass.ds(n * GRP, GRP)], GRP, NT - 1)
                    pe.wait_ge(kept, n + 1)
                    if not first:
                        pe.wait_ge(ready, n - 1)
                    for c in range(GRP):
                        last = nc.tensor.matmul(px[b][:, c, :], ohT[b][:, c, :], h[:, bass.ds(tiles[c], 1), :],
                                                start=True, stop=True)
                    last.then_inc(spread, 1)

                turn(0, 0, True)
                turn(1, 1, False)
                spread_rows(0, 0, True)
                spread_rows(1, 1, True)
                with pe.Fori(1, groups // 2) as t:
                    turn(2 * t, 0, False)
                    turn(2 * t + 1, 1, False)
                    spread_rows(2 * t, 0, False)
                    spread_rows(2 * t + 1, 1, False)

            @block.gpsimd
            def _(pool):
                with pool.Fori(0, groups // 2) as t:
                    for b in range(2):
                        pool.wait_ge(ready, 2 * t + b + 1)
                        pool.sem_inc(started, 1)
                        for c in range(GRP):
                            pool.indirect_dma_start(table[:, :],
                                                    bass.IndirectOffsetOnAxis(ap=at[b][:, c:c + 1], axis=0),
                                                    pay[b][:, c, :], None, bounds_check=P * NCC - 1,
                                                    oob_is_err=False).then_inc(sent[b], 16)
                for b in range(2):
                    pool.wait_ge(sent[b], GRP * 16 * (groups // 2))


def cell_messages(nc, g, name, table, cmap, w, F, FO, msgs):
    groups = NCC // GRP
    W = F + 4
    Q = 4 * FO
    row = KS * KS * FO
    reach = 2 * row
    with Phase(nc, name) as ph:
        pay = [ph.sb(f"pay{b}", [P, GRP, W]) for b in range(2)]
        at = [ph.sb(f"at{b}", [P, GRP], I32) for b in range(2)]
        hT = [ph.sb(f"hT{b}", [F, GRP, P]) for b in range(2)]
        rest = ph.sb("rest", [P, GRP, 3])
        low = [ph.sb(f"low{k}", [P, Q]) for k in range(2)]
        u = ph.sb("u", [P, GRP, Q])
        v = ph.sb("v", [P, GRP, Q // 2])
        v2 = ph.sb("v2", [P, GRP, Q // 2])
        out = [ph.sb(f"out{b}", [P, GRP, FO]) for b in range(2)]
        o2 = ph.sb("o2", [P, GRP, FO])
        pt = [ph.ps(f"pt{k}", [F, GRP // 2, P]) for k in range(2)]
        pp = [ph.ps(f"pp{k}", [P, 2, Q]) for k in range(4)]
        turned, kept, mm_done, lows, halves, ready, steps_s, eased, staged = (
            ph.sem(s) for s in ("turned", "kept", "mm_done", "lows", "halves", "ready", "steps", "eased", "staged"))
        started, begun = ph.sem("started"), ph.sem("begun")
        loaded = [ph.sem(f"loaded{b}") for b in range(2)]
        sent = [ph.pool_dma_sem(f"sent{b}") for b in range(2)]
        PER = 7
        with nc.Block() as block:
            @block.sync
            def _(sp):
                of = table.rearrange("(p j) w -> p j w", p=P)

                def load(t, first):
                    for b in range(2):
                        if not first:
                            sp.wait_ge(staged, 2 * t + b - 1)
                        sp.dma_start(pay[b][:, :, :], of[:, bass.ds((2 * t + b) * GRP, GRP), :]
                                     ).then_inc(loaded[b], 16)

                load(0, True)
                with sp.Fori(1, groups // 2) as t:
                    load(t, False)

            @block.tensor
            def _(pe):
                def turn(t, b, first):
                    n = 2 * t + b
                    pe.wait_ge(loaded[b], 16 * (t + 1))
                    if not first:
                        pe.wait_ge(kept, n)
                    pe.sem_inc(begun, 1)
                    for c in range(GRP):
                        last = nc.tensor.transpose(pt[c // (GRP // 2)][:, c % (GRP // 2), :], pay[b][:, c, 0:F],
                                                   g.ident[:, :])
                    last.then_inc(turned, 1)

                def product(n, b, first):
                    offs = values(nc, mybir.EngineType.PE, cmap[0:1, bass.ds(n * GRP, GRP)], GRP,
                                  (3 * 31) * FO)
                    pe.wait_ge(kept, n + 1)
                    for c in range(GRP):
                        if not (first and c < 4):
                            pe.wait_ge(halves, n * GRP + c - 3)
                        win = w[:, bass.ds(offs[c], reach)].rearrange("p (a x) -> p a x", a=2)[:, :, 0:2 * KS * FO]
                        win = win.rearrange("p a (b y) -> p a b y", b=2)[:, :, :, 0:2 * FO]
                        nc.tensor.matmul(pp[c % 4][:, :, :].rearrange("p a (b y) -> p a b y", b=2),
                                         hT[b][:, c, :], win, start=True, stop=True).then_inc(mm_done, 1)

                turn(0, 0, True)
                product(0, 0, True)
                turn(0, 1, False)
                product(1, 1, False)
                with pe.Fori(1, groups // 2) as t:
                    for b in range(2):
                        turn(t, b, False)
                        product(2 * t + b, b, False)

            @block.scalar
            def _(act):
                def group(n, b, first):
                    act.wait_ge(turned, n + 1)
                    for k in range(2):
                        last = nc.scalar.copy(hT[b][:, k * GRP // 2:(k + 1) * GRP // 2, :], pt[k][:, :, :])
                    last.then_inc(kept, 1)
                    act.wait_ge(eased, n + 1)
                    for c in range(GRP):
                        act.wait_ge(mm_done, n * GRP + c + 1)
                        if not (first and c < 2):
                            act.wait_ge(halves, n * GRP + c - 1)
                        nc.scalar.activation(low[c % 2][:, :], pp[c % 4][:, 0, :], ACT.Copy,
                                             scale=rest[:, c, 0:1]).then_inc(lows, 1)

                group(0, 0, True)
                group(1, 1, False)
                with act.Fori(1, groups // 2) as t:
                    for b in range(2):
                        group(2 * t + b, b, False)

            @block.vector
            def _(dve):
                def group(t, b, first):
                    n = 2 * t + b
                    steps = Steps(dve, steps_s, n * PER)
                    f = pay[b][:, :, F:F + 3]
                    dve.wait_ge(loaded[b], 16 * (t + 1))
                    if not (first and b == 0):
                        dve.wait_ge(lows, n * GRP)
                    nc.vector.tensor_scalar(rest[:, :, :], f, -1.0, 1.0, ALU.mult, ALU.add).then_inc(eased, 1)
                    for c in range(GRP):
                        dve.wait_ge(lows, n * GRP + c + 1)
                        nc.vector.scalar_tensor_tensor(out=u[:, c, :], in0=pp[c % 4][:, 1, :],
                                                       scalar=pay[b][:, c, F:F + 1], in1=low[c % 2][:, :],
                                                       op0=ALU.mult, op1=ALU.add).then_inc(halves, 1)
                    dve.wait_ge(halves, (n + 1) * GRP)
                    half = [P, GRP, Q // 2]
                    nc.vector.tensor_tensor(v[:, :, :], u[:, :, 0:Q // 2], bc(rest[:, :, 1], 2, half), ALU.mult)
                    steps(nc.vector.tensor_tensor(v2[:, :, :], u[:, :, Q // 2:Q],
                                                  bc(pay[b][:, :, F + 1], 2, half), ALU.mult))
                    steps(nc.vector.tensor_tensor(v[:, :, :], v[:, :, :], v2[:, :, :], ALU.add))
                    if not first:
                        dve.wait_ge(sent[b], GRP * 16 * t)
                    full = [P, GRP, FO]
                    steps(nc.vector.tensor_tensor(out[b][:, :, :], v[:, :, 0:FO], bc(rest[:, :, 2], 2, full),
                                                  ALU.mult))
                    steps(nc.vector.tensor_tensor(o2[:, :, :], v[:, :, FO:2 * FO],
                                                  bc(pay[b][:, :, F + 2], 2, full), ALU.mult))
                    steps(nc.vector.tensor_tensor(out[b][:, :, :], out[b][:, :, :], o2[:, :, :], ALU.add))
                    steps(nc.vector.tensor_copy(at[b][:, :], pay[b][:, :, F + 3].bitcast(I32)))
                    steps(nc.vector.memset(g.junk[:, :], 0.0))
                    nc.vector.sem_inc(ready, 1)
                    nc.vector.sem_inc(staged, 1)

                group(0, 0, True)
                group(0, 1, True)
                with dve.Fori(1, groups // 2) as t:
                    group(t, 0, False)
                    group(t, 1, False)

            @block.gpsimd
            def _(pool):
                with pool.Fori(0, groups // 2) as t:
                    for b in range(2):
                        pool.wait_ge(ready, 2 * t + b + 1)
                        pool.sem_inc(started, 1)
                        for c in range(GRP):
                            pool.indirect_dma_start(msgs[:, :],
                                                    bass.IndirectOffsetOnAxis(ap=at[b][:, c:c + 1], axis=0),
                                                    out[b][:, c, :], None, bounds_check=P * NC - 1,
                                                    oob_is_err=False).then_inc(sent[b], 16)
                for b in range(2):
                    pool.wait_ge(sent[b], GRP * 16 * (groups // 2))


def src_sums(nc, g, name, slo, tmap, msgs, F, acc):
    groups = NC // GRP
    with Phase(nc, name) as ph:
        rows = [ph.sb(f"rows{b}", [P, GRP, F]) for b in range(2)]
        oh = [ph.sb(f"oh{b}", [P, GRP, LO]) for b in range(2)]
        sums = [ph.ps(f"sums{b}", [LO, GRP, F]) for b in range(2)]
        oh_ready, mm_done, added, steps_a = (ph.sem(s) for s in ("oh_ready", "mm_done", "added", "steps_a"))
        loaded = [ph.sem(f"loaded{b}") for b in range(2)]
        with nc.Block() as block:
            @block.sync
            def _(sp):
                of = msgs.rearrange("(p j) w -> p j w", p=P)

                def load(t, first):
                    for b in range(2):
                        if not first:
                            sp.wait_ge(mm_done, 2 * t + b - 1)
                        sp.dma_start(rows[b][:, :, :], of[:, bass.ds((2 * t + b) * GRP, GRP), :]
                                     ).then_inc(loaded[b], 16)

                load(0, True)
                with sp.Fori(1, groups // 2) as t:
                    load(t, False)

            @block.vector
            def _(dve):
                def hot(n, b, first):
                    if not first:
                        dve.wait_ge(mm_done, n - 1)
                    nc.vector.tensor_tensor(oh[b][:, :, :], bc(g.iota[:, 0:LO], 1, [P, GRP, LO]),
                                            bc(slo[:, bass.ds(n * GRP, GRP)], 2, [P, GRP, LO]),
                                            ALU.is_equal).then_inc(oh_ready, 1)

                def add(n, b):
                    dve.wait_ge(mm_done, n + 1)
                    add_tiles(nc, dve, steps_a, 1, n, tmap, acc, [sums[b][:, c:c + 1, :] for c in range(GRP)],
                              ALU.add)
                    dve.sem_inc(added, 1)

                steps = Steps(dve, steps_a)
                steps(nc.vector.memset(acc, 0.0))
                hot(0, 0, True)
                hot(1, 1, True)
                add(0, 0)
                with dve.Fori(1, groups // 2) as t:
                    for b in range(2):
                        hot(2 * t + b, b, False)
                        add(2 * t + b - 1, 1 - b)
                add(groups - 1, 1)

            @block.tensor
            def _(pe):
                def product(t, b, first):
                    n = 2 * t + b
                    pe.wait_ge(oh_ready, n + 1)
                    pe.wait_ge(loaded[b], 16 * (t + 1))
                    if not first:
                        pe.wait_ge(added, n - 1)
                    for c in range(GRP):
                        last = nc.tensor.matmul(sums[b][:, c, :], oh[b][:, c, :], rows[b][:, c, :],
                                                start=True, stop=True)
                    last.then_inc(mm_done, 1)

                product(0, 0, True)
                product(0, 1, True)
                with pe.Fori(1, groups // 2) as t:
                    product(t, 0, False)
                    product(t, 1, False)


def moved_attributes(nc, g, rec, tmap, t4, table, att2):
    groups = NC // GRP
    T = 4
    with Phase(nc, "moved") as ph:
        at = [ph.sb(f"at{b}", [P, GRP], I32) for b in range(2)]
        rows = [ph.sb(f"rows{b}", [P, GRP, T]) for b in range(2)]
        oh = [ph.sb(f"oh{b}", [P, GRP, LO]) for b in range(2)]
        ohT = [ph.sb(f"ohT{b}", [LO, GRP, P]) for b in range(2)]
        new = ph.sb("new", [P, GRP, 3])
        pt = [ph.ps(f"pt{k}", [LO, GRP // 2, P]) for k in range(2)]
        px = [ph.ps(f"px{b}", [P, GRP, T]) for b in range(2)]
        at_ready, oh_ready, turned, kept, spread, made, steps_s, started = (
            ph.sem(s) for s in ("at_ready", "oh_ready", "turned", "kept", "spread", "made", "steps", "started"))
        got = [ph.pool_dma_sem(f"got{b}") for b in range(2)]
        with nc.Block() as block:
            @block.scalar
            def _(act):
                def group(t, b, first):
                    n = 2 * t + b
                    if not first:
                        act.wait_ge(got[b], GRP * 16 * t)
                    nc.scalar.copy(at[b][:, :], rec[:, bass.ds(n * GRP, GRP), SRC].bitcast(I32)).then_inc(at_ready, 1)
                    act.wait_ge(turned, n + 1)
                    if not first:
                        act.wait_ge(spread, n - 1)
                    for k in range(2):
                        last = nc.scalar.copy(ohT[b][:, k * GRP // 2:(k + 1) * GRP // 2, :], pt[k][:, :, :])
                    last.then_inc(kept, 1)

                group(0, 0, True)
                group(0, 1, True)
                with act.Fori(1, groups // 2) as t:
                    group(t, 0, False)
                    group(t, 1, False)

            @block.gpsimd
            def _(pool):
                def gather(t, first):
                    for b in range(2):
                        pool.wait_ge(at_ready, 2 * t + b + 1)
                        pool.sem_inc(started, 1)
                        if not first:
                            pool.wait_ge(made, 2 * t + b - 1)
                            pool.sem_inc(started, 1)
                        for c in range(GRP):
                            pool.indirect_dma_start(rows[b][:, c, :], None, table[:, :],
                                                    bass.IndirectOffsetOnAxis(ap=at[b][:, c:c + 1], axis=0)
                                                    ).then_inc(got[b], 16)

                gather(0, True)
                with pool.Fori(1, groups // 2) as t:
                    gather(t, False)

            @block.vector
            def _(dve):
                def hot(n, b, first):
                    if not first:
                        dve.wait_ge(turned, n - 1)
                    nc.vector.tensor_tensor(oh[b][:, :, :], bc(g.iota[:, 0:LO], 1, [P, GRP, LO]),
                                            bc(rec[:, bass.ds(n * GRP, GRP), DLO], 2, [P, GRP, LO]),
                                            ALU.is_equal).then_inc(oh_ready, 1)

                def make(t, b):
                    n = 2 * t + b
                    slots = bass.ds(n * GRP, GRP)
                    steps = Steps(dve, steps_s, 3 * n)
                    dve.wait_ge(spread, n + 1)
                    steps(nc.vector.tensor_tensor(new[:, :, :], rec[:, slots, ATT:ATT + 3], px[b][:, :, 0:3],
                                                  ALU.add))
                    dve.wait_ge(got[b], GRP * 16 * (t + 1))
                    steps(nc.vector.tensor_tensor(new[:, :, :], new[:, :, :], rows[b][:, :, 0:3], ALU.subtract))
                    steps(nc.vector.tensor_scalar(att2[:, slots, :], new[:, :, :], 0.0, 1.0, ALU.max, ALU.min))
                    dve.sem_inc(made, 1)

                hot(0, 0, True)
                hot(1, 1, True)
                make(0, 0)
                make(0, 1)
                with dve.Fori(1, groups // 2) as t:
                    hot(2 * t, 0, False)
                    hot(2 * t + 1, 1, False)
                    make(t, 0)
                    make(t, 1)

            @block.tensor
            def _(pe):
                def turn(n, b, first):
                    pe.wait_ge(oh_ready, n + 1)
                    if not first:
                        pe.wait_ge(kept, n)
                    for c in range(GRP):
                        last = nc.tensor.transpose(pt[c // (GRP // 2)][:, c % (GRP // 2), :], oh[b][:, c, :],
                                                   g.ident[:, :])
                    last.then_inc(turned, 1)

                def spread_rows(n, b, first):
                    tiles = values(nc, mybir.EngineType.PE, tmap[0:1, bass.ds(n * GRP, GRP)], GRP, NT - 1)
                    pe.wait_ge(kept, n + 1)
                    if not first:
                        pe.wait_ge(made, n - 1)
                    for c in range(GRP):
                        last = nc.tensor.matmul(px[b][:, c, :], ohT[b][:, c, :], t4[:, bass.ds(tiles[c], 1), :],
                                                start=True, stop=True)
                    last.then_inc(spread, 1)

                turn(0, 0, True)
                turn(1, 1, False)
                spread_rows(0, 0, True)
                spread_rows(1, 1, True)
                with pe.Fori(1, groups // 2) as t:
                    turn(2 * t, 0, False)
                    turn(2 * t + 1, 1, False)
                    spread_rows(2 * t, 0, False)
                    spread_rows(2 * t + 1, 1, False)


def finish(nc, g, acc, bias, x, out):
    wide = [LO, NT, D]
    with Phase(nc, "finish") as ph:
        steps_s, stored = ph.sem("steps"), ph.sem("stored")
        with nc.Block() as block:
            @block.vector
            def _(dve):
                steps = Steps(dve, steps_s)
                steps(nc.vector.tensor_tensor(acc, acc, bc(g.rdeg[:, :], 2, wide), ALU.mult))
                steps(nc.vector.tensor_tensor(acc, acc, bc(bias, 1, wide), ALU.add))
                steps(nc.vector.tensor_tensor(acc, acc, x, ALU.add))

            @block.sync
            def _(sp):
                sp.wait_ge(steps_s, 3)
                sp.dma_start(out.rearrange("(p c) f -> p c f", p=LO), acc).then_inc(stored, 16)
                sp.wait_ge(stored, 16)


def clear_column(nc, name, column):
    with nc.Block() as block:
        @block.vector
        def _(dve):
            nc.vector.memset(column, 0.0)


def program(nc, x_in, src, dst, edge_attr, lam, cheb_W, cheb_b, gat_Wsrc, gat_bsrc, gat_Wdst, gat_bdst, gat_attn,
            gat_bias, stn1_w, stn1_b, stn2_w, stn2_b, stn3_w, stn3_b, stn4_w, stn4_b, conv_w, conv_b, out):
    whole = ExitStack()
    with whole:
        def sb(name, shape, dt=F32, ctx=whole):
            return ctx.enter_context(nc.sbuf_tensor(name, shape, dt))

        def dram(name, shape, dt=F32):
            return nc.dram_tensor(name, shape, dt).ap()

        g = Tensors()
        g.iota, g.ones, g.ident, g.tri = (sb(n, [P, P]) for n in ("iota", "ones", "ident", "tri"))
        g.jcol, g.junk, g.re = sb("jcol", [P, NC // P]), sb("junk", [P, 1]), sb("re", [LO, 5])
        g.degd, g.degs, g.norm, g.rdeg = (sb(n, [LO, NT]) for n in ("degd", "degs", "norm", "rdeg"))
        rec_d, rec_s = dram("rec_d", [P * NC, RECD]), dram("rec_s", [P * NC, RECS])
        map_d, map_s = dram("map_d", [NC], I32), dram("map_s", [NC], I32)
        map_c, map_c2 = dram("map_c", [NC], I32), dram("map_c2", [NC], I32)
        table = dram("table", [N, D])
        t_table = dram("t_table", [N, 4])
        fse = dram("fse", [P * NC, D])
        cells1, cells2 = dram("cells1", [P * NCC, HID + 4]), dram("cells2", [P * NCC, D + 4])
        msgs1, msgs2 = dram("msgs1", [P * NC, HID]), dram("msgs2", [P * NC, D])

        constants(nc, g)
        fill_rows(nc, "fill", ((cells1, P * NCC, HID + 4, True), (cells2, P * NCC, D + 4, True),
                               (msgs1, P * NC, HID, False), (msgs2, P * NC, D, False)))

        with ExitStack() as c2:
            def eb(name, dt=F32):
                return sb(name, [P, ECP], dt, c2)

            e = Tensors()
            e.src, e.rows, e.rowd = (eb(n, I32) for n in ("src", "row_s", "row_d"))
            e.lod, e.tiled, e.los, e.tiles = (eb(n) for n in ("lod", "tiled", "los", "tiles"))
            load_edges(nc, g, e, src, dst)
            rank(nc, g, "rankd", e.tiled[:, :], ECP, NT, NC, e.rowd[:, :], None, map_d)
            rank(nc, g, "ranks", e.tiles[:, :], ECP, NT, NC, e.rows[:, :], None, map_s)
            scatter_records(nc, g, e, edge_attr, rec_d, rec_s)

        x = sb("x", [LO, NT, D])
        h1 = sb("h1", [LO, NT, HID])
        slo = sb("slo", [P, NC])
        tmd, tms = sb("tmd", [1, NC], I32), sb("tms", [1, NC], I32)
        lam_b, w1, w3, w4 = sb("lam_b", [LO, 1]), sb("w1", [K3, HID]), sb("w3", [HID, HID]), sb("w4", [HID, 3])
        cheb_w, gat_w = sb("cheb_w", [3 * D, D]), sb("gat_w", [D, 2 * D])
        b_cheb, b_gat, b_att = sb("b_cheb", [LO, D]), sb("b_gat", [LO, 2 * D]), sb("b_att", [LO, D])
        attn = sb("attn", [P, D])
        b1, b2, b3 = (sb(f"b{k}", [LO, HID]) for k in (1, 2, 3))
        b4, b5 = sb("b4", [LO, 3]), sb("b5", [LO, D])
        row = lambda a: a.rearrange("(o c) -> o c", o=1)
        spread = lambda a, n: a.partition_broadcast(n)
        load_table(nc, g, "params", [
            (x[:, :, :], x_in.rearrange("(p c) f -> p c f", p=LO)),
            (tmd[:, :], row(map_d)), (tms[:, :], row(map_s)), (lam_b[:, :], spread(lam, LO)),
            (w1[:, :], stn1_w.rearrange("k i o -> k (i o)")), (w3[:, :], stn3_w), (w4[:, :], stn4_w),
            (cheb_w[:, :], cheb_W.rearrange("o i -> i o")), (gat_w[:, 0:D], gat_Wsrc.rearrange("o i -> i o")),
            (gat_w[:, D:2 * D], gat_Wdst.rearrange("o i -> i o")), (b_cheb[:, :], spread(cheb_b, LO)),
            (b_gat[:, 0:D], spread(gat_bsrc, LO)), (b_gat[:, D:2 * D], spread(gat_bdst, LO)),
            (b_att[:, :], spread(gat_bias, LO)), (attn[:, :], spread(gat_attn.rearrange("a b c -> (a b c)"), P)),
            (b1[:, :], spread(stn1_b, LO)), (b2[:, :], spread(stn2_b, LO)), (b3[:, :], spread(stn3_b, LO)),
            (b4[:, :], spread(stn4_b, LO)), (b5[:, :], spread(conv_b, LO))])
        node_scales(nc, g, lam_b[:, :])

        with ExitStack() as c2:
            recs = sb("recs", [P, NC, RECS], F32, c2)
            bt = sb("bt", [K3, NT, LO], F32, c2)
            load_table(nc, g, "ldrecs", [(recs[:, :, :], rec_s.rearrange("(p j) w -> p j w", p=P)),
                                         (slo[:, :], rec_s.rearrange("(p j) w -> p j w", p=P)[:, :, SLO])])
            basis_sums(nc, g, recs, tms, bt[:, :, :])
            node_linear(nc, g, "stn1", bt[:, :, :], K3, w1[:, :], None, HID, h1[:, :, :], transposed=True)
        scale_bias_elu(nc, g, "elu1", h1[:, :, :], HID, g.rdeg[:, :], b1[:, :])

        rec = sb("rec", [P, NC, RECD])
        load_table(nc, g, "ldrec", [(rec[:, :, :], rec_d.rearrange("(p j) w -> p j w", p=P))])

        with ExitStack() as c1:
            fd = sb("fd", [LO, NT, D], F32, c1)
            with ExitStack() as c2:
                acc = sb("acc", [LO, NT, D], F32, c2)
                with ExitStack() as c3:
                    cat = sb("cat", [LO, NT, 3 * D], F32, c3)
                    layer_norm_relu(nc, g, "ln0", x[:, :, :], cat[:, :, 0:D])
                    for layer in range(2):
                        for order in (1, 2):
                            name = f"cheb{layer}{order}"
                            store_scaled(nc, g, name + "s", cat[:, :, (order - 1) * D:order * D], g.norm[:, :], table)
                            propagate(nc, g, name + "p", rec, tmd, table, acc[:, :, :])
                            chebyshev(nc, g, name + "c", acc[:, :, :], cat, order)
                        node_linear(nc, g, f"cheb{layer}l", cat[:, :, :], 3 * D, cheb_w[:, :], b_cheb[:, :], D,
                                    cat[:, :, 0:D] if layer == 0 else acc[:, :, :], relu=True)
                node_linear(nc, g, "gatfs", acc[:, :, :], D, gat_w[:, 0:D], b_gat[:, 0:D], D, fd[:, :, :])
                store_scaled(nc, g, "gats", fd[:, :, :], None, table)
                node_linear(nc, g, "gatfd", acc[:, :, :], D, gat_w[:, D:2 * D], b_gat[:, D:2 * D], D, fd[:, :, :])
            lgs = sb("lgs", [P, NC], F32, c1)
            mx = sb("mx", [LO, NT, 1], F32, c1)
            attention_scores(nc, g, rec, tmd, table, fse, fd[:, :, :], attn[:, :], lgs, mx[:, :, :])
            att = sb("att", [LO, NT, D + 1], F32, c1)
            attention_sums(nc, g, rec, tmd, fse, lgs, mx[:, :, :], att[:, :, :])
            attention_end(nc, g, att[:, :, :], b_att[:, :], x[:, :, :])

        cmap = sb("cmap", [1, NCC], I32)
        rowc = sb("rowc", [P, NC], I32)
        frac = sb("frac", [P, NC, 3])
        first = rec[:, :, ATT:ATT + 3]

        def cell_order(name, att, width, map_dram):
            with ExitStack() as c2:
                key = sb(name + "key", [P, NC], F32, c2)
                tmp = [sb(f"{name}tmp{k}", [P, NC // P], F32, c2) for k in range(3)]
                spline_cells(nc, g, name + "cells", att, rec[:, :, DLO], key[:, :], frac[:, :, :])
                rank(nc, g, name + "rank", key[:, :], NC, CELLS, NCC, rowc[:, :], cell_offsets(nc, tmp, width),
                     map_dram)
            load_table(nc, g, name + "ld", [(cmap[:, :], row(map_dram)[:, 0:NCC])])

        cell_order("c1", first, HID, map_c)
        to_cells(nc, g, "toc1", rec, tmd, h1[:, :, :], HID, frac, rowc, cells1)
        with ExitStack() as c2:
            w2 = sb("w2", [HID, (3 * 31 + 2 * KS * KS), HID], F32, c2)
            load_table(nc, g, "ldw2", [(w2[:, 0:K3, :], stn2_w.rearrange("k i o -> i k o"))])
            cell_messages(nc, g, "msg1", cells1, cmap, w2[:, :, :].rearrange("i k o -> i (k o)"), HID, HID, msgs1)
        src_sums(nc, g, "sum1", slo, tms, msgs1, HID, h1[:, :, :])
        scale_bias_elu(nc, g, "elu2", h1[:, :, :], HID, g.rdeg[:, :], b2[:, :])
        with ExitStack() as c2:
            t4 = sb("t4", [LO, NT, 4], F32, c2)
            with ExitStack() as c3:
                h3 = sb("h3", [LO, NT, HID], F32, c3)
                node_linear(nc, g, "stn3", h1[:, :, :], HID, w3[:, :], b3[:, :], HID, h3[:, :, :])
                scale_bias_elu(nc, g, "elu3", h3[:, :, :], HID, None, None)
                node_linear(nc, g, "stn4", h3[:, :, :], HID, w4[:, :], b4[:, :], 3, t4[:, :, 0:3])
            clear_column(nc, "t4c", t4[:, :, 3:4])
            store_scaled(nc, g, "t4s", t4[:, :, :], None, t_table)
            att2 = sb("att2", [P, NC, 3], F32, c2)
            moved_attributes(nc, g, rec, tmd, t4[:, :, :], t_table, att2)
            cell_order("c2", att2[:, :, :], D, map_c2)
        with ExitStack() as c2:
            h = sb("h", [LO, NT, D], F32, c2)
            w5 = sb("w5", [D, (3 * 31 + 2 * KS * KS), D], F32, c2)
            load_table(nc, g, "ldw5", [(w5[:, 0:K3, :], conv_w.rearrange("k i o -> i k o"))])
            layer_norm_relu(nc, g, "ln1", x[:, :, :], h[:, :, :])
            to_cells(nc, g, "toc2", rec, tmd, h[:, :, :], D, frac, rowc, cells2)
            cell_messages(nc, g, "msg2", cells2, cmap, w5[:, :, :].rearrange("i k o -> i (k o)"), D, D, msgs2)
            src_sums(nc, g, "sum2", slo, tms, msgs2, D, h[:, :, :])
            finish(nc, g, h[:, :, :], b5[:, :], x[:, :, :], out)


_INS = ["x", "src", "dst", "edge_attr_3", "L0_gnn_laplacian_lambda_max", "L0_gnn_cheb_W", "L0_gnn_cheb_b",
        "L0_gnn_gat_Wsrc", "L0_gnn_gat_bsrc", "L0_gnn_gat_Wdst", "L0_gnn_gat_bdst", "L0_gnn_gat_attn",
        "L0_gnn_gat_bias", "L1_gnn_stn1_w", "L1_gnn_stn1_b", "L1_gnn_stn2_w", "L1_gnn_stn2_b", "L1_gnn_stn3_w",
        "L1_gnn_stn3_b", "L1_gnn_stn4_w", "L1_gnn_stn4_b", "L1_gnn_conv_w", "L1_gnn_conv_b"]


def kernel(**inputs):
    import numpy as _np
    import concourse.bacc as _bacc
    from concourse import mybir as _mybir
    from concourse.bass_utils import run_bass_kernel_spmd as _run

    nc = _bacc.Bacc("TRN2", target_bir_lowering=False, num_devices=1)
    arrays, args = {}, []
    for name in _INS:
        a = _np.ascontiguousarray(inputs[name])
        arrays[f"in_{name}_dram"] = a
        args.append(nc.dram_tensor(f"in_{name}_dram", a.shape, _mybir.dt.from_np(a.dtype), kind="ExternalInput").ap())
    out = nc.dram_tensor("out_0_dram", (12500, 32), _mybir.dt.float32, kind="ExternalOutput").ap()
    program(nc, *args, out)
    r = _run(nc, [arrays], core_ids=[0])
    return r.results[0]["out_0_dram"]
```

```python
from contextlib import ExitStack

import concourse.bass as bass
from concourse import mybir

F32, BF16, I32 = mybir.dt.float32, mybir.dt.bfloat16, mybir.dt.int32
ALU = mybir.AluOpType
ACT = mybir.ActivationFunctionType
AX = mybir.AxisListType.X

P = 128
N, D = 12500, 32
LO, NT = 125, 100
E = 200000
EC = -(-E // P)
GRP = 8
DEEP = 4
ECP = -(-EC // (2 * GRP)) * 2 * GRP
HID = 64
KS = 5
K3 = KS ** 3
CELLS = 4 ** 3
NC = -(-((E + NT * (P - 1)) // P) // (DEEP * GRP)) * DEEP * GRP
NCC = -(-((E + CELLS * (P - 1)) // P) // (2 * GRP)) * 2 * GRP
BIG = 1.0e6
RND = 12582912.0
LOW = 1.0e30
SRC, ROWS, ROWC, ATT, DLO, RECD = 0, 1, 2, 3, 6, 7
SLO, SATT, RECS = 0, 1, 4


def bc(ap, axis, shape):
    return ap.unsqueeze(axis).to_broadcast(shape)


class Tensors:
    pass


class Steps:

    def __init__(self, engine, sem, base=0):
        self.engine, self.sem, self.base, self.n = engine, sem, base, 0

    def __call__(self, instruction):
        instruction.then_inc(self.sem, 1)
        self.n += 1
        self.engine.wait_ge(self.sem, self.base + self.n)


class Phase:

    def __init__(self, nc, name):
        self.nc, self.name, self.ctx, self.sems = nc, name, ExitStack(), []

    def __enter__(self):
        self.ctx.__enter__()
        return self

    def __exit__(self, *e):
        if e[0] is None:
            self.nc.clear_and_free_semaphores(self.sems)
            self.nc.all_engine_barrier()
        return self.ctx.__exit__(*e)

    def sb(self, name, shape, dt=F32):
        return self.ctx.enter_context(self.nc.sbuf_tensor(f"{self.name}_{name}", shape, dt))

    def ps(self, name, shape, dt=F32):
        return self.ctx.enter_context(self.nc.psum_tensor(f"{self.name}_{name}", shape, dt))

    def sem(self, name):
        self.sems.append(self.nc.alloc_semaphore(f"{self.name}_{name}"))
        return self.sems[-1]

    def pool_dma_sem(self, name):
        return self.nc.alloc_semaphore(f"{self.name}_{name}")


def constants(nc, g):
    with Phase(nc, "const") as ph:
        ii = ph.sb("ii", [P, P], I32)
        jj = ph.sb("jj", [P, NC // P], I32)
        made, steps = ph.sem("made"), ph.sem("steps")
        with nc.Block() as block:
            @block.gpsimd
            def _(pool):
                nc.gpsimd.iota(ii[:, :], [[1, P]], base=0, channel_multiplier=0)
                nc.gpsimd.iota(jj[:, :], [[P, NC // P]], base=0, channel_multiplier=1)
                nc.gpsimd.memset(g.ones[:, :], 1.0)
                nc.gpsimd.memset(g.ident[:, :], 1.0).then_inc(made, 1)
                pool.wait_ge(made, 1)
                nc.gpsimd.affine_select(out=g.tri[:, :], in_=g.ones[:, :], pattern=[[1, P]], compare_op=ALU.is_gt,
                                        fill=0.0, base=0, channel_multiplier=-1)
                nc.gpsimd.affine_select(out=g.ident[:, :], in_=g.ident[:, :], pattern=[[1, P]],
                                        compare_op=ALU.is_equal, fill=0.0, base=0,
                                        channel_multiplier=-1).then_inc(made, 1)

            @block.vector
            def _(dve):
                dve.wait_ge(made, 2)
                nc.vector.tensor_copy(g.iota[:, :], ii[:, :])
                nc.vector.tensor_copy(g.jcol[:, :], jj[:, :])


def split_nodes(nc, steps, ids, lo, tile):
    steps(nc.vector.tensor_copy(tile, ids))
    steps(nc.vector.tensor_scalar(lo, tile, 1.0 / NT, -0.5 + 0.5 / NT, ALU.mult, ALU.add))
    steps(nc.vector.tensor_scalar(lo, lo, RND, RND, ALU.add, ALU.subtract))
    steps(nc.vector.scalar_tensor_tensor(out=tile, in0=lo, scalar=-float(NT), in1=tile, op0=ALU.mult, op1=ALU.add))


def load_edges(nc, g, e, src, dst, attr):
    full = P - 1
    rest = E - full * EC
    with Phase(nc, "load") as ph:
        dst_i = ph.sb("dst_i", [P, ECP], I32)
        oh = [[ph.sb(f"oh{b}{k}", [P, GRP, LO if k % 2 == 0 else NT], BF16) for k in range(4)] for b in range(2)]
        deg_ps = [ph.ps("degd", [LO, NT]), ph.ps("degs", [LO, NT])]
        zero = ph.sb("zero", [P, LO], BF16)
        att_loaded = ph.sem("att_loaded")
        cleared, loaded, split, padded = ph.sem("cleared"), ph.sem("loaded"), ph.sem("split"), ph.sem("padded")
        steps_s, ready, used, total = ph.sem("steps"), ph.sem("ready"), ph.sem("used"), ph.sem("total")
        groups = ECP // GRP
        with nc.Block() as block:
            @block.sync
            def _(sp):
                sp.wait_ge(cleared, 1)
                sp.dma_start(e.att[0:full, 0:EC, :], attr[0:full * EC, :].rearrange("(p c) k -> p c k", p=full)
                             ).then_inc(att_loaded, 16)
                sp.dma_start(e.att[full:P, 0:rest, :], attr[full * EC:E, :].rearrange("(p c) k -> p c k", p=1)
                             ).then_inc(att_loaded, 16)
                for ids, given in ((e.src, src), (dst_i, dst)):
                    sp.dma_start(ids[0:full, 0:EC], given[0:full * EC].rearrange("(p c) -> p c", p=full)
                                 ).then_inc(loaded, 16)
                    sp.dma_start(ids[full:P, 0:rest], given[full * EC:E].rearrange("(p c) -> p c", p=1)
                                 ).then_inc(loaded, 16)
                sp.wait_ge(att_loaded, 32)

            @block.gpsimd
            def _(pool):
                nc.gpsimd.memset(e.att[:, :, :], 0.0)
                nc.gpsimd.memset(e.src[:, :], 0)
                nc.gpsimd.memset(zero[:, :], 0.0)
                nc.gpsimd.memset(dst_i[:, :], 0).then_inc(cleared, 1)
                pool.wait_ge(split, 1)
                for tile in (e.tiled, e.tiles):
                    nc.gpsimd.memset(tile[:, EC:ECP], -1.0)
                    last = nc.gpsimd.affine_select(out=tile[:, 0:EC], in_=tile[:, 0:EC], pattern=[[-1, EC]],
                                                   compare_op=ALU.is_ge, fill=-1.0, base=E - 1,
                                                   channel_multiplier=-EC)
                last.then_inc(padded, 1)

            @block.vector
            def _(dve):
                steps = Steps(dve, steps_s)
                dve.wait_ge(loaded, 64)
                split_nodes(nc, steps, dst_i[:, :], e.lod[:, :], e.tiled[:, :])
                split_nodes(nc, steps, e.src[:, :], e.los[:, :], e.tiles[:, :])
                nc.vector.memset(g.junk[:, :], 0.0).then_inc(split, 1)
                dve.wait_ge(padded, 1)
                with dve.Fori(0, groups // 2) as t:
                    for b in range(2):
                        dve.wait_ge(used, 2 * t + b + 1)
                        at = bass.ds((2 * t + b) * GRP, GRP)
                        for k, (keys, n) in enumerate(((e.lod, LO), (e.tiled, NT), (e.los, LO), (e.tiles, NT))):
                            last = nc.vector.tensor_tensor(oh[b][k][:, :, :], bc(g.iota[:, 0:n], 1, [P, GRP, n]),
                                                           bc(keys[:, at], 2, [P, GRP, n]), ALU.is_equal)
                        last.then_inc(ready, 1)
                dve.wait_ge(total, 1)
                nc.vector.tensor_copy(g.degd[:, :], deg_ps[0][:, :])
                nc.vector.tensor_copy(g.degs[:, :], deg_ps[1][:, :])

            @block.tensor
            def _(pe):
                pe.wait_ge(cleared, 1)
                for d in range(2):
                    last = nc.tensor.matmul(deg_ps[d][:, :], zero[:, :], zero[:, 0:NT], start=True, stop=False,
                                            skip_group_check=True)
                last.then_inc(used, 2)
                with pe.Fori(0, groups // 2) as t:
                    for b in range(2):
                        pe.wait_ge(ready, 2 * t + b + 1)
                        for d in range(2):
                            for c in range(GRP):
                                last = nc.tensor.matmul(deg_ps[d][:, :], oh[b][2 * d][:, c, :],
                                                        oh[b][2 * d + 1][:, c, :], start=False, stop=False,
                                                        skip_group_check=True)
                        last.then_inc(used, 1)
                for d in range(2):
                    last = nc.tensor.matmul(deg_ps[d][:, :], zero[:, :], zero[:, 0:NT], start=False, stop=True,
                                            skip_group_check=True)
                last.then_inc(total, 1)


def rank(nc, g, ph, block, work, key, width, buckets, chunks, row, chunk_map, map_dram):
    mg = NC // P
    m, run, pos = work
    cnt = ph.sb("cnt", [P, buckets])
    cc = ph.sb("cc", [P, buckets])
    cend = ph.sb("cend", [P, buckets])
    off = ph.sb("off", [P, buckets])
    bm = ph.sb("bm", [P, mg])
    bmi = ph.sb("bmi", [P, mg], I32)
    pre, tot = ph.ps("pre", [P, buckets]), ph.ps("tot", [P, buckets])
    scanned = ph.sem("scanned")
    steps_s, counted, summed, mapped, stored = (ph.sem(x) for x in
                                                ("steps", "counted", "summed", "mapped", "stored"))

    @block.vector
    def _(dve):
        with dve.Fori(0, buckets) as b:
            steps = Steps(dve, steps_s, b)
            steps(nc.vector.tensor_scalar(m[:, :], key, g.iota[:, bass.ds(b, 1)], None, ALU.is_equal,
                                          ALU.add, accum_out=cnt[:, bass.ds(b, 1)]))
        steps = Steps(dve, steps_s, buckets)
        steps(nc.vector.memset(pos[:, :], 0.0))
        nc.vector.memset(g.junk[:, :], 0.0).then_inc(counted, 1)
        dve.wait_ge(summed, 1)
        steps(nc.vector.tensor_scalar(cc[:, :], tot[:, :], P / 2 - 0.5, 1.0 / P, ALU.add, ALU.mult))
        steps(nc.vector.tensor_scalar(cc[:, :], cc[:, :], RND, RND, ALU.add, ALU.subtract))
        steps(nc.vector.tensor_tensor_scan(cend[:, :], cc[:, :], cc[:, :], 0.0, ALU.add, ALU.bypass))
        steps(nc.vector.tensor_tensor(cc[:, :], cend[:, :], cc[:, :], ALU.subtract))
        steps(nc.vector.tensor_scalar(cc[:, :], cc[:, :], float(P), -1.0, ALU.mult, ALU.add))
        steps(nc.vector.tensor_tensor(off[:, :], cc[:, :], pre[:, :], ALU.add))
        for q in range(mg):
            steps(nc.vector.tensor_scalar(cc[:, :], cend[:, :], g.jcol[:, q:q + 1], None, ALU.is_le,
                                          ALU.add, accum_out=bm[:, q:q + 1]))
        steps(nc.vector.tensor_scalar(bm[:, :], bm[:, :], float(buckets - 1), None, ALU.min))
        if chunk_map is not None:
            chunk_map(steps, bm)
        steps(nc.vector.tensor_copy(bmi[:, :], bm[:, :]))
        nc.vector.memset(g.junk[:, :], 0.0).then_inc(mapped, 1)
        before = steps.base + steps.n
        with dve.Fori(0, buckets) as b:
            steps = Steps(dve, steps_s, before + 3 * b)
            steps(nc.vector.tensor_scalar(m[:, :], key, g.iota[:, bass.ds(b, 1)], None, ALU.is_equal))
            steps(nc.vector.tensor_tensor_scan(run[:, :], m[:, :], m[:, :], off[:, bass.ds(b, 1)],
                                               ALU.add, ALU.bypass))
            dve.sem_inc(scanned, 1)
            steps(nc.vector.copy_predicated(pos[:, :], m[:, :].bitcast(I32), run[:, :]))
        steps = Steps(dve, steps_s, before + 3 * buckets)
        steps(nc.vector.tensor_scalar(run[:, :], pos[:, :], 1.0 / P, -0.5 + 0.5 / P, ALU.mult, ALU.add))
        steps(nc.vector.tensor_scalar(run[:, :], run[:, :], RND, RND, ALU.add, ALU.subtract))
        steps(nc.vector.scalar_tensor_tensor(out=pos[:, :], in0=run[:, :], scalar=-float(P), in1=pos[:, :],
                                             op0=ALU.mult, op1=ALU.add))
        steps(nc.vector.scalar_tensor_tensor(out=pos[:, :], in0=pos[:, :], scalar=float(chunks),
                                             in1=run[:, :], op0=ALU.mult, op1=ALU.add))
        steps(nc.vector.tensor_scalar(m[:, :], key, 0.0, BIG, ALU.is_lt, ALU.mult))
        steps(nc.vector.tensor_tensor(pos[:, :], pos[:, :], m[:, :], ALU.add))
        steps(nc.vector.tensor_copy(row, pos[:, :]))

    @block.tensor
    def _(pe):
        pe.wait_ge(counted, 1)
        nc.tensor.matmul(pre[:, :], g.tri[:, :], cnt[:, :], start=True, stop=True)
        nc.tensor.matmul(tot[:, :], g.ones[:, :], cnt[:, :], start=True, stop=True).then_inc(summed, 1)

    @block.sync
    def _(sp):
        sp.wait_ge(mapped, 1)
        with nc.allow_non_contiguous_dma("a map of chunks, one word each"):
            sp.dma_start(map_dram.rearrange("(g p) -> p g", p=P), bmi[:, :]).then_inc(stored, 16)
        sp.wait_ge(stored, 16)


def edge_cells(nc, g, ph, block, work, att, tile, key):
    pos, i0, frac = work
    steps_s = ph.sem("cell_steps")

    @block.vector
    def _(dve):
        steps = Steps(dve, steps_s)
        steps(nc.vector.memset(key, 0.0))
        for d in range(3):
            steps(nc.vector.tensor_scalar(pos[:, :], att[:, :, d], float(KS - 1), None, ALU.mult))
            cell_of(nc, steps, pos[:, :], i0[:, :], frac[:, :])
            steps(nc.vector.scalar_tensor_tensor(out=key, in0=key, scalar=4.0, in1=i0[:, :],
                                                 op0=ALU.mult, op1=ALU.add))
        steps(nc.vector.tensor_scalar(pos[:, :], tile, 0.0, None, ALU.is_ge))
        steps(nc.vector.scalar_tensor_tensor(out=key, in0=key, scalar=1.0, in1=pos[:, :], op0=ALU.add, op1=ALU.mult))
        steps(nc.vector.tensor_scalar(key, key, 1.0, None, ALU.subtract))


def scatter_records(nc, g, ph, block, fields, words, rows, table):
    groups = ECP // GRP
    at = [ph.sb(f"at{b}", [P, GRP], I32) for b in range(2)]
    rec = [ph.sb(f"rec{b}", [P, GRP, words]) for b in range(2)]
    ready, started = ph.sem("ready"), ph.sem("started")
    sent = [ph.pool_dma_sem(f"sent{b}") for b in range(2)]

    @block.scalar
    def _(act):
        def pack(t, first):
            for b in range(2):
                if not first:
                    act.wait_ge(sent[b], GRP * 16 * t)
                slots = bass.ds((2 * t + b) * GRP, GRP)
                for word, source in fields:
                    n = source.shape[2] if len(source.shape) == 3 else 1
                    to = rec[b][:, :, word:word + n] if n > 1 else rec[b][:, :, word]
                    of = source[:, slots, :] if n > 1 else source[:, slots]
                    nc.scalar.copy(to.bitcast(I32) if source.dtype == I32 else to, of)
                nc.scalar.copy(at[b][:, :], rows[:, slots]).then_inc(ready, 1)

        pack(0, True)
        with act.Fori(1, groups // 2) as t:
            pack(t, False)

    @block.gpsimd
    def _(pool):
        with pool.Fori(0, groups // 2) as t:
            for b in range(2):
                pool.wait_ge(ready, 2 * t + b + 1)
                pool.sem_inc(started, 1)
                for c in range(GRP):
                    pool.indirect_dma_start(table[:, :], bass.IndirectOffsetOnAxis(ap=at[b][:, c:c + 1], axis=0),
                                            rec[b][:, c, :], None, bounds_check=P * NC - 1,
                                            oob_is_err=False).then_inc(sent[b], 16)
        for b in range(2):
            pool.wait_ge(sent[b], GRP * 16 * (groups // 2))


def values(nc, engine_type, row, n, hi):
    _, got = nc.values_load_multi_w_load_instructions(
        row, engines=(engine_type,), min_val=0, max_val=hi,
        skip_runtime_bounds_check_because="the map is clamped to the last bucket when it is made")
    return got


def load_table(nc, g, name, pairs):
    with Phase(nc, name) as ph:
        loaded = ph.sem("loaded")
        with nc.Block() as block:
            @block.sync
            def _(sp):
                with nc.allow_non_contiguous_dma("small weights, once"):
                    for to, of in pairs:
                        sp.dma_start(to, of).then_inc(loaded, 16)
                sp.wait_ge(loaded, 16 * len(pairs))


def propagate(nc, g, name, rec, tmap, table, acc):
    groups = NC // GRP
    with Phase(nc, name) as ph:
        at = [ph.sb(f"at{b}", [P, GRP], I32) for b in range(2)]
        rows = [ph.sb(f"rows{b}", [P, GRP, D]) for b in range(2)]
        oh = [ph.sb(f"oh{b}", [P, GRP, LO]) for b in range(2)]
        sums = [ph.ps(f"sums{b}", [LO, GRP, D]) for b in range(2)]
        at_ready, oh_ready, mm_done = ph.sem("at_ready"), ph.sem("oh_ready"), ph.sem("mm_done")
        added, steps_s = ph.sem("added"), ph.sem("steps")
        started = ph.sem("started")
        got = [ph.pool_dma_sem(f"got{b}") for b in range(2)]
        with nc.Block() as block:
            @block.scalar
            def _(act):
                def stage(t, first):
                    for b in range(2):
                        if not first:
                            act.wait_ge(got[b], GRP * 16 * t)
                        nc.scalar.copy(at[b][:, :], rec[:, bass.ds((2 * t + b) * GRP, GRP), SRC].bitcast(I32)
                                       ).then_inc(at_ready, 1)

                stage(0, True)
                with act.Fori(1, groups // 2) as t:
                    stage(t, False)

            @block.gpsimd
            def _(pool):
                def gather(t, first):
                    for b in range(2):
                        pool.wait_ge(at_ready, 2 * t + b + 1)
                        pool.sem_inc(started, 1)
                        if not first:
                            pool.wait_ge(mm_done, 2 * t + b - 1)
                            pool.sem_inc(started, 1)
                        for c in range(GRP):
                            pool.indirect_dma_start(rows[b][:, c, :], None, table[:, :],
                                                    bass.IndirectOffsetOnAxis(ap=at[b][:, c:c + 1], axis=0)
                                                    ).then_inc(got[b], 16)

                gather(0, True)
                with pool.Fori(1, groups // 2) as t:
                    gather(t, False)

            @block.vector
            def _(dve):
                steps = Steps(dve, steps_s)
                steps(nc.vector.memset(acc, 0.0))

                def hot(t, b, first):
                    if not first:
                        dve.wait_ge(mm_done, 2 * t + b - 1)
                    nc.vector.tensor_tensor(oh[b][:, :, :], bc(g.iota[:, 0:LO], 1, [P, GRP, LO]),
                                            bc(rec[:, bass.ds((2 * t + b) * GRP, GRP), DLO], 2, [P, GRP, LO]),
                                            ALU.is_equal).then_inc(oh_ready, 1)

                def add(t, b):
                    dve.wait_ge(mm_done, 2 * t + b + 1)
                    add_tiles(nc, dve, steps_s, 1, 2 * t + b, tmap, acc,
                              [sums[b][:, c:c + 1, :] for c in range(GRP)], ALU.add)
                    dve.sem_inc(added, 1)

                hot(0, 0, True)
                hot(0, 1, True)
                add(0, 0)
                add(0, 1)
                with dve.Fori(1, groups // 2) as t:
                    hot(t, 0, False)
                    hot(t, 1, False)
                    add(t, 0)
                    add(t, 1)

            @block.tensor
            def _(pe):
                def product(t, first):
                    for b in range(2):
                        pe.wait_ge(oh_ready, 2 * t + b + 1)
                        pe.wait_ge(got[b], GRP * 16 * (t + 1))
                        if not first:
                            pe.wait_ge(added, 2 * t + b - 1)
                        for c in range(GRP):
                            last = nc.tensor.matmul(sums[b][:, c, :], oh[b][:, c, :], rows[b][:, c, :],
                                                    start=True, stop=True)
                        last.then_inc(mm_done, 1)

                product(0, True)
                with pe.Fori(1, groups // 2) as t:
                    product(t, False)


def layer_norm_relu(nc, g, name, x, h):
    wide = [LO, NT, D]
    with Phase(nc, name) as ph:
        sq = ph.sb("sq", wide)
        mean, var = ph.sb("mean", [LO, NT]), ph.sb("var", [LO, NT])
        steps_s, asked, rooted = ph.sem("steps"), ph.sem("asked"), ph.sem("rooted")
        with nc.Block() as block:
            @block.vector
            def _(dve):
                steps = Steps(dve, steps_s)
                steps(nc.vector.tensor_reduce(mean[:, :], x, AX, ALU.add))
                steps(nc.vector.tensor_scalar(mean[:, :], mean[:, :], 1.0 / D, None, ALU.mult))
                steps(nc.vector.tensor_tensor(h, x, bc(mean[:, :], 2, wide), ALU.subtract))
                steps(nc.vector.tensor_tensor(sq[:, :, :], h, h, ALU.mult))
                steps(nc.vector.tensor_reduce(var[:, :], sq[:, :, :], AX, ALU.add))
                nc.vector.tensor_scalar(var[:, :], var[:, :], 1.0 / D, 1.0e-5, ALU.mult, ALU.add).then_inc(asked, 1)
                dve.wait_ge(rooted, 1)
                steps(nc.vector.reciprocal(var[:, :], var[:, :]))
                steps(nc.vector.tensor_tensor(h, h, bc(var[:, :], 2, wide), ALU.mult))
                steps(nc.vector.tensor_scalar(h, h, 0.0, None, ALU.max))

            @block.scalar
            def _(act):
                act.wait_ge(asked, 1)
                nc.scalar.activation(var[:, :], var[:, :], ACT.Sqrt).then_inc(rooted, 1)


def node_scales(nc, g, lam):
    with Phase(nc, "scales") as ph:
        steps_s, asked, rooted = ph.sem("steps"), ph.sem("asked"), ph.sem("rooted")
        with nc.Block() as block:
            @block.vector
            def _(dve):
                steps = Steps(dve, steps_s)
                steps(nc.vector.tensor_scalar(g.rdeg[:, :], g.degs[:, :], 1.0, None, ALU.max))
                steps(nc.vector.reciprocal(g.rdeg[:, :], g.rdeg[:, :]))
                steps(nc.vector.reciprocal(g.re[:, 0:1], lam))
                steps(nc.vector.tensor_scalar(g.re[:, 0:1], g.re[:, 0:1], 2.0, None, ALU.mult))
                steps(nc.vector.tensor_scalar(g.re[:, 1:2], g.re[:, 0:1], -1.0, None, ALU.mult))
                steps(nc.vector.tensor_scalar(g.re[:, 2:3], g.re[:, 0:1], 1.0, None, ALU.subtract))
                steps(nc.vector.tensor_scalar(g.re[:, 3:4], g.re[:, 0:1], -2.0, None, ALU.mult))
                steps(nc.vector.tensor_scalar(g.re[:, 4:5], g.re[:, 2:3], 2.0, None, ALU.mult))
                nc.vector.tensor_scalar(g.norm[:, :], g.degd[:, :], 1.0, None, ALU.max).then_inc(asked, 1)
                dve.wait_ge(rooted, 1)
                steps(nc.vector.reciprocal(g.norm[:, :], g.norm[:, :]))

            @block.scalar
            def _(act):
                act.wait_ge(asked, 1)
                nc.scalar.activation(g.norm[:, :], g.norm[:, :], ACT.Sqrt).then_inc(rooted, 1)


def store_scaled(nc, g, name, h, scale, table):
    shape = [LO, NT, h.shape[2]]
    with Phase(nc, name) as ph:
        out = ph.sb("out", shape)
        made, stored = ph.sem("made"), ph.sem("stored")
        with nc.Block() as block:
            @block.vector
            def _(dve):
                if scale is None:
                    nc.vector.tensor_copy(out[:, :, :], h).then_inc(made, 1)
                else:
                    nc.vector.tensor_tensor(out[:, :, :], h, bc(scale, 2, shape), ALU.mult).then_inc(made, 1)

            @block.sync
            def _(sp):
                sp.wait_ge(made, 1)
                sp.dma_start(table.rearrange("(p c) f -> p c f", p=LO), out[:, :, :]).then_inc(stored, 16)
                sp.wait_ge(stored, 16)


def chebyshev(nc, g, name, acc, cat, order):
    wide = [LO, NT, D]
    a, b = (1, 2) if order == 1 else (3, 4)
    before, to = cat[:, :, (order - 1) * D:order * D], cat[:, :, order * D:(order + 1) * D]
    with Phase(nc, name) as ph:
        steps_s = ph.sem("steps")
        with nc.Block() as block:
            @block.vector
            def _(dve):
                steps = Steps(dve, steps_s)
                steps(nc.vector.tensor_tensor(acc, acc, bc(g.norm[:, :], 2, wide), ALU.mult))
                steps(nc.vector.tensor_scalar(acc, acc, g.re[:, a:a + 1], None, ALU.mult))
                steps(nc.vector.scalar_tensor_tensor(out=to, in0=before, scalar=g.re[:, b:b + 1], in1=acc,
                                                     op0=ALU.mult, op1=ALU.add))
                if order == 2:
                    steps(nc.vector.tensor_tensor(to, to, cat[:, :, 0:D], ALU.subtract))


def node_linear(nc, g, name, x, K, w, bias, FO, y, relu=False, transposed=False):
    T = 4
    with Phase(nc, name) as ph:
        xs = ph.sb("xs", [K, T, LO] if transposed else [LO, T, K])
        xt = ph.sb("xt", [K, T, LO])
        ys = ph.sb("ys", [LO, T, FO])
        pt, py = ph.ps("pt", [K, T, LO]), ph.ps("py", [LO, T, FO])
        staged, turned, kept, made, steps_s, begun = (ph.sem(s) for s in ("staged", "turned", "kept", "made",
                                                                           "steps", "begun"))
        with nc.Block() as block:
            @block.vector
            def _(dve):
                with dve.Fori(0, NT // T) as t:
                    steps = Steps(dve, steps_s, 2 * t)
                    at = bass.ds(t * T, T)
                    nc.vector.tensor_copy(xs[:, :, :], x[:, at, :]).then_inc(staged, 1)
                    if not transposed:
                        dve.wait_ge(turned, t + 1)
                        nc.vector.tensor_copy(xt[:, :, :], pt[:, :, :]).then_inc(kept, 1)
                    dve.wait_ge(made, t + 1)
                    if bias is None:
                        steps(nc.vector.tensor_copy(ys[:, :, :], py[:, :, :]))
                    else:
                        steps(nc.vector.tensor_tensor(ys[:, :, :], py[:, :, :], bc(bias, 1, [LO, T, FO]), ALU.add))
                    steps(nc.vector.tensor_scalar(y[:, at, :], ys[:, :, :], 0.0 if relu else 1.0, None,
                                                  ALU.max if relu else ALU.mult))

            @block.tensor
            def _(pe):
                with pe.Fori(0, NT // T) as t:
                    pe.wait_ge(staged, t + 1)
                    pe.sem_inc(begun, 1)
                    if not transposed:
                        for c in range(T):
                            last = nc.tensor.transpose(pt[:, c, :], xs[:, c, :], g.ident[0:LO, 0:LO])
                        last.then_inc(turned, 1)
                        pe.wait_ge(kept, t + 1)
                    for c in range(T):
                        last = nc.tensor.matmul(py[:, c, :], (xs if transposed else xt)[:, c, :], w,
                                                start=True, stop=True)
                    last.then_inc(made, 1)


def scale_bias_elu(nc, g, name, y, F, scale, bias):
    wide = [LO, NT, F]
    with Phase(nc, name) as ph:
        low = ph.sb("low", wide)
        steps_s, asked, done = ph.sem("steps"), ph.sem("asked"), ph.sem("done")
        with nc.Block() as block:
            @block.vector
            def _(dve):
                steps = Steps(dve, steps_s)
                if scale is not None:
                    steps(nc.vector.tensor_tensor(y, y, bc(scale, 2, wide), ALU.mult))
                if bias is not None:
                    steps(nc.vector.tensor_tensor(y, y, bc(bias, 1, wide), ALU.add))
                nc.vector.tensor_scalar(low[:, :, :], y, 0.0, None, ALU.min).then_inc(asked, 1)
                dve.wait_ge(done, 1)
                steps(nc.vector.tensor_scalar(low[:, :, :], low[:, :, :], 1.0, None, ALU.subtract))
                steps(nc.vector.scalar_tensor_tensor(out=y, in0=y, scalar=0.0, in1=low[:, :, :],
                                                     op0=ALU.max, op1=ALU.add))

            @block.scalar
            def _(act):
                act.wait_ge(asked, 1)
                nc.scalar.activation(low[:, :, :], low[:, :, :], ACT.Exp).then_inc(done, 1)


def add_tiles(nc, dve, sem, base, group, tmap, acc, sums, op):
    tiles = values(nc, mybir.EngineType.DVE, tmap[0:1, bass.ds(group * GRP, GRP)], GRP, NT - 1)
    steps = Steps(dve, sem, group * GRP + base)
    for c in range(GRP):
        to = acc[:, bass.ds(tiles[c], 1), :]
        steps(nc.vector.tensor_tensor(to, to, sums[c], op))


def wait(engine, sem, value):
    if not isinstance(value, int) or value > 0:
        engine.wait_ge(sem, value)


def is_group(n):
    return not isinstance(n, int) or n >= 0


def buffer_of(t, b, back):
    return (b - back) % DEEP, t + 1 if b >= back else t


def attention_scores(nc, g, rec, tmap, table, fse, fdt, attn, lgs, mx, att2):
    groups = NC // GRP
    half = GRP // 2
    with Phase(nc, "att1") as ph:
        at = [ph.sb(f"at{b}", [P, GRP], I32) for b in range(DEEP)]
        rows = [ph.sb(f"rows{b}", [P, GRP, D + 4]) for b in range(DEEP)]
        oh = [ph.sb(f"oh{b}", [P, GRP, LO], BF16) for b in range(2)]
        ohT = [ph.sb(f"ohT{b}", [LO, GRP, P]) for b in range(2)]
        ident = ph.sb("ident", [P, P], BF16)
        sc = ph.sb("sc", [P, GRP, D])
        new = ph.sb("new", [P, GRP, 3])
        am = [ph.sb(f"am{b}", [P, GRP, LO]) for b in range(2)]
        red = ph.sb("red", [LO, GRP])
        pt = [ph.ps(f"pt{b}", [LO, GRP, P], BF16) for b in range(2)]
        pa = [ph.ps(f"pa{h}", [LO, half, P]) for h in range(2)]
        px = [ph.ps(f"px{b}", [P, GRP, D + 4]) for b in range(2)]
        (at_ready, oh_ready, turned, kept, spread, masked, am_ready, am_turned, reduced, steps_s, steps_m, made) = (
            ph.sem(s) for s in ("at_ready", "oh_ready", "turned", "kept", "spread", "masked",
                                "am_ready", "am_turned", "reduced", "steps", "steps_m", "made"))
        ident_made = ph.sem("ident_made")
        started, begun = ph.sem("started"), ph.sem("begun")
        got = [ph.pool_dma_sem(f"got{b}") for b in range(DEEP)]
        stored = [ph.sem(f"stored{b}") for b in range(DEEP)]
        with nc.Block() as block:
            @block.scalar
            def _(act):
                def group(t, b):
                    n = DEEP * t + b
                    wait(act, got[b], GRP * 16 * t)
                    nc.scalar.copy(at[b][:, :], rec[:, bass.ds(n * GRP, GRP), SRC].bitcast(I32)).then_inc(at_ready, 1)
                    mask(n - 1, (b - 1) % 2)
                    act.wait_ge(turned, n + 1)
                    wait(act, spread, n - 1)
                    nc.scalar.copy(ohT[b % 2][:, :, :], pt[b % 2][:, :, :]).then_inc(kept, 1)

                def mask(n, b):
                    if is_group(n):
                        act.wait_ge(oh_ready, n + 1)
                        wait(act, am_turned, n - 1)
                        nc.scalar.activation(am[b][:, :, :], oh[b][:, :, :], ACT.Copy, bias=-LOW, scale=LOW
                                             ).then_inc(masked, 1)

                for b in range(DEEP):
                    group(0, b)
                with act.Fori(1, groups // DEEP) as t:
                    for b in range(DEEP):
                        group(t, b)
                mask(groups - 1, (groups - 1) % 2)

            @block.gpsimd
            def _(pool):
                def gather(t, b):
                    pool.wait_ge(at_ready, DEEP * t + b + 1)
                    pool.sem_inc(started, 1)
                    if is_group(t - 1):
                        pool.wait_ge(made, DEEP * t + b - DEEP + 1)
                        pool.sem_inc(started, 1)
                        pool.wait_ge(stored[b], 16 * t)
                        pool.sem_inc(started, 1)
                    for c in range(GRP):
                        pool.indirect_dma_start(rows[b][:, c, :], None, table[:, :],
                                                bass.IndirectOffsetOnAxis(ap=at[b][:, c:c + 1], axis=0)
                                                ).then_inc(got[b], 16)

                for b in range(DEEP):
                    gather(0, b)
                with pool.Fori(1, groups // DEEP) as t:
                    for b in range(DEEP):
                        gather(t, b)

            @block.sync
            def _(sp):
                to = fse.rearrange("(p j) f -> p j f", p=P)
                with sp.Fori(0, groups // DEEP) as t:
                    for b in range(DEEP):
                        sp.wait_ge(got[b], GRP * 16 * (t + 1))
                        sp.dma_start(to[:, bass.ds((DEEP * t + b) * GRP, GRP), :], rows[b][:, :, :]
                                     ).then_inc(stored[b], 16)
                for b in range(DEEP):
                    sp.wait_ge(stored[b], 16 * (groups // DEEP))

            @block.vector
            def _(dve):
                def hot(n, b):
                    wait(dve, masked, n - 1)
                    wait(dve, turned, n - 1)
                    nc.vector.tensor_tensor(oh[b % 2][:, :, :], bc(g.iota[:, 0:LO], 1, [P, GRP, LO]),
                                            bc(rec[:, bass.ds(n * GRP, GRP), DLO], 2, [P, GRP, LO]),
                                            ALU.is_equal).then_inc(oh_ready, 1)

                def score(n, b, uses):
                    slots = bass.ds(n * GRP, GRP)
                    steps = Steps(dve, steps_s, 6 * n)
                    lg = lgs[:, slots]
                    dve.wait_ge(got[b], GRP * 16 * uses)
                    dve.wait_ge(spread, n + 1)
                    nc.vector.tensor_tensor(new[:, :, :], rec[:, slots, ATT:ATT + 3], px[b % 2][:, :, D:D + 3],
                                            ALU.add)
                    steps(nc.vector.tensor_tensor(sc[:, :, :], px[b % 2][:, :, 0:D], rows[b][:, :, 0:D], ALU.add))
                    nc.vector.tensor_tensor(new[:, :, :], new[:, :, :], rows[b][:, :, D:D + 3], ALU.subtract)
                    steps(nc.vector.scalar_tensor_tensor(out=sc[:, :, :], in0=sc[:, :, :], scalar=0.2,
                                                         in1=sc[:, :, :], op0=ALU.mult, op1=ALU.max))
                    nc.vector.tensor_scalar(att2[:, slots, :], new[:, :, :], 0.0, 1.0, ALU.max, ALU.min)
                    steps(nc.vector.tensor_tensor(sc[:, :, :], sc[:, :, :], bc(attn, 1, [P, GRP, D]), ALU.mult))
                    dve.sem_inc(made, 1)
                    steps(nc.vector.tensor_reduce(lg, sc[:, :, :], AX, ALU.add))
                    dve.wait_ge(masked, n + 1)
                    steps(nc.vector.tensor_tensor(am[b % 2][:, :, :], am[b % 2][:, :, :],
                                                  bc(lg, 2, [P, GRP, LO]), ALU.add))
                    dve.sem_inc(am_ready, 1)
                    steps(nc.vector.memset(g.junk[:, :], 0.0))

                def highest(n):
                    dve.wait_ge(am_turned, n + 1)
                    for h in range(2):
                        last = nc.vector.tensor_reduce(red[:, h * half:(h + 1) * half], pa[h][:, :, :], AX, ALU.max)
                    last.then_inc(reduced, 1)
                    dve.wait_ge(reduced, n + 1)
                    add_tiles(nc, dve, steps_m, 1, n, tmap, mx, [red[:, c:c + 1].unsqueeze(2) for c in range(GRP)],
                              ALU.max)

                def group(t, b):
                    n = DEEP * t + b
                    hot(n, b)
                    if is_group(n - 1):
                        score(n - 1, *buffer_of(t, b, 1))
                    if is_group(n - 2):
                        highest(n - 2)

                nc.vector.tensor_copy(ident[:, :], g.ident[:, :]).then_inc(ident_made, 1)
                steps = Steps(dve, steps_m)
                steps(nc.vector.memset(mx, -LOW))
                for b in range(DEEP):
                    group(0, b)
                with dve.Fori(1, groups // DEEP) as t:
                    for b in range(DEEP):
                        group(t, b)
                score(groups - 1, DEEP - 1, groups // DEEP)
                highest(groups - 2)
                highest(groups - 1)

            @block.tensor
            def _(pe):
                def turn(n, b):
                    pe.wait_ge(oh_ready, n + 1)
                    wait(pe, kept, n - 1)
                    pe.sem_inc(begun, 1)
                    for c in range(GRP):
                        last = nc.tensor.transpose(pt[b][:, c, :], oh[b][:, c, :], ident[:, :])
                    last.then_inc(turned, 1)

                def spread_rows(n, b):
                    tiles = values(nc, mybir.EngineType.PE, tmap[0:1, bass.ds(n * GRP, GRP)], GRP, NT - 1)
                    pe.wait_ge(kept, n + 1)
                    wait(pe, am_ready, n - 1)
                    for c in range(GRP):
                        last = nc.tensor.matmul(px[b][:, c, :], ohT[b][:, c, :], fdt[:, bass.ds(tiles[c], 1), :],
                                                start=True, stop=True)
                    last.then_inc(spread, 1)

                def turn_scores(n, b):
                    pe.wait_ge(am_ready, n + 1)
                    wait(pe, reduced, n)
                    for c in range(GRP):
                        last = nc.tensor.transpose(pa[c // half][:, c % half, :], am[b][:, c, :], g.ident[:, :])
                    last.then_inc(am_turned, 1)

                def group(t, b):
                    n = DEEP * t + b
                    turn(n, b % 2)
                    if is_group(n - 1):
                        spread_rows(n - 1, (b - 1) % 2)
                    if is_group(n - 2):
                        turn_scores(n - 2, b % 2)

                pe.wait_ge(ident_made, 1)
                for b in range(DEEP):
                    group(0, b)
                with pe.Fori(1, groups // DEEP) as t:
                    for b in range(DEEP):
                        group(t, b)
                spread_rows(groups - 1, 1)
                turn_scores(groups - 2, 0)
                turn_scores(groups - 1, 1)


def attention_sums(nc, g, rec, tmap, fse, lgs, mx, acc):
    groups = NC // GRP
    half = GRP // 2
    W = D + 1
    with Phase(nc, "att2") as ph:
        rows = [ph.sb(f"rows{b}", [P, GRP, D + 4]) for b in range(DEEP)]
        oh = [ph.sb(f"oh{b}", [P, GRP, LO]) for b in range(DEEP)]
        ohT = [ph.sb(f"ohT{b}", [LO, GRP, P]) for b in range(2)]
        ex = [ph.sb(f"ex{b}", [P, GRP]) for b in range(2)]
        msg = [ph.sb(f"msg{b}", [P, GRP, W]) for b in range(2)]
        pt = [ph.ps(f"pt{h}", [LO, half, P]) for h in range(2)]
        pm = [ph.ps(f"pm{b}", [P, GRP]) for b in range(2)]
        sums = [ph.ps(f"sums{b}", [LO, GRP, W]) for b in range(2)]
        oh_ready, turned, kept, m_ready, less, exped, msg_ready, mm_done, added, steps_s, steps_a = (
            ph.sem(s) for s in ("oh_ready", "turned", "kept", "m_ready", "less", "exped", "msg_ready", "mm_done",
                                "added", "steps", "steps_a"))
        loaded = [ph.sem(f"loaded{b}") for b in range(DEEP)]
        with nc.Block() as block:
            @block.sync
            def _(sp):
                of = fse.rearrange("(p j) f -> p j f", p=P)

                def load(t, b):
                    wait(sp, msg_ready, DEEP * (t - 1) + b + 1)
                    sp.dma_start(rows[b][:, :, :], of[:, bass.ds((DEEP * t + b) * GRP, GRP), :]
                                 ).then_inc(loaded[b], 16)

                for b in range(DEEP):
                    load(0, b)
                with sp.Fori(1, groups // DEEP) as t:
                    for b in range(DEEP):
                        load(t, b)

            @block.scalar
            def _(act):
                def keep(n, b):
                    act.wait_ge(turned, n + 1)
                    wait(act, m_ready, n - 1)
                    for h in range(2):
                        last = nc.scalar.copy(ohT[b][:, h * half:(h + 1) * half, :], pt[h][:, :, :])
                    last.then_inc(kept, 1)

                def exponent(n, b):
                    act.wait_ge(less, n + 1)
                    nc.scalar.activation(ex[b][:, :], ex[b][:, :], ACT.Exp).then_inc(exped, 1)

                def group(n, b):
                    keep(n, b % 2)
                    if is_group(n - 1):
                        exponent(n - 1, (b - 1) % 2)

                for b in range(DEEP):
                    group(b, b)
                with act.Fori(1, groups // DEEP) as t:
                    for b in range(DEEP):
                        group(DEEP * t + b, b)
                exponent(groups - 1, 1)

            @block.vector
            def _(dve):
                def hot(n, b):
                    wait(dve, mm_done, n - DEEP + 1)
                    nc.vector.tensor_tensor(oh[b][:, :, :], bc(g.iota[:, 0:LO], 1, [P, GRP, LO]),
                                            bc(rec[:, bass.ds(n * GRP, GRP), DLO], 2, [P, GRP, LO]),
                                            ALU.is_equal).then_inc(oh_ready, 1)

                def lessen(n, b):
                    steps = Steps(dve, steps_s, n)
                    dve.wait_ge(m_ready, n + 1)
                    steps(nc.vector.tensor_tensor(ex[b][:, :], lgs[:, bass.ds(n * GRP, GRP)], pm[b][:, :],
                                                  ALU.subtract))
                    nc.vector.tensor_scalar(ex[b][:, :], ex[b][:, :], 0.0, None, ALU.min).then_inc(less, 1)

                def message(n, b, uses):
                    dve.wait_ge(exped, n + 1)
                    wait(dve, mm_done, n - 1)
                    dve.wait_ge(loaded[b], 16 * uses)
                    nc.vector.tensor_tensor(msg[b % 2][:, :, 0:D], rows[b][:, :, 0:D],
                                            bc(ex[b % 2][:, :], 2, [P, GRP, D]), ALU.mult)
                    nc.vector.tensor_copy(msg[b % 2][:, :, D], ex[b % 2][:, :]).then_inc(msg_ready, 1)

                def add(n, b):
                    dve.wait_ge(mm_done, n + 1)
                    add_tiles(nc, dve, steps_a, 1, n, tmap, acc, [sums[b][:, c:c + 1, :] for c in range(GRP)],
                              ALU.add)
                    dve.sem_inc(added, 1)

                def group(t, b):
                    n = DEEP * t + b
                    if is_group(n - 1):
                        lessen(n - 1, (b - 1) % 2)
                    hot(n, b)
                    if is_group(n - 1):
                        message(n - 1, *buffer_of(t, b, 1))
                    if is_group(n - 2):
                        add(n - 2, b % 2)

                steps = Steps(dve, steps_a)
                steps(nc.vector.memset(acc, 0.0))
                for b in range(DEEP):
                    group(0, b)
                with dve.Fori(1, groups // DEEP) as t:
                    for b in range(DEEP):
                        group(t, b)
                lessen(groups - 1, 1)
                message(groups - 1, DEEP - 1, groups // DEEP)
                add(groups - 2, 0)
                add(groups - 1, 1)

            @block.tensor
            def _(pe):
                def turn(n, b):
                    pe.wait_ge(oh_ready, n + 1)
                    wait(pe, kept, n)
                    for c in range(GRP):
                        last = nc.tensor.transpose(pt[c // half][:, c % half, :], oh[b][:, c, :], g.ident[:, :])
                    last.then_inc(turned, 1)

                def maxima(n, b):
                    tiles = values(nc, mybir.EngineType.PE, tmap[0:1, bass.ds(n * GRP, GRP)], GRP, NT - 1)
                    pe.wait_ge(kept, n + 1)
                    wait(pe, less, n - 1)
                    for c in range(GRP):
                        last = nc.tensor.matmul(pm[b][:, c:c + 1], ohT[b][:, c, :], mx[:, bass.ds(tiles[c], 1), :],
                                                start=True, stop=True)
                    last.then_inc(m_ready, 1)

                def total(n, b):
                    pe.wait_ge(msg_ready, n + 1)
                    wait(pe, added, n - 1)
                    for c in range(GRP):
                        last = nc.tensor.matmul(sums[b % 2][:, c, :], oh[b][:, c, :], msg[b % 2][:, c, :],
                                                start=True, stop=True)
                    last.then_inc(mm_done, 1)

                def group(n, b):
                    turn(n, b)
                    maxima(n, b % 2)
                    if is_group(n - 1):
                        total(n - 1, (b - 1) % DEEP)

                for b in range(DEEP):
                    group(b, b)
                with pe.Fori(1, groups // DEEP) as t:
                    for b in range(DEEP):
                        group(DEEP * t + b, b)
                total(groups - 1, DEEP - 1)


def attention_end(nc, g, acc, bias, x):
    with Phase(nc, "att3") as ph:
        den = ph.sb("den", [LO, NT])
        one = ph.sb("one", [LO, NT])
        steps_s = ph.sem("steps")
        wide = [LO, NT, D]
        with nc.Block() as block:
            @block.vector
            def _(dve):
                steps = Steps(dve, steps_s)
                steps(nc.vector.tensor_scalar(one[:, :], acc[:, :, D], 0.0, None, ALU.is_equal))
                steps(nc.vector.tensor_tensor(den[:, :], acc[:, :, D], one[:, :], ALU.add))
                steps(nc.vector.reciprocal(den[:, :], den[:, :]))
                steps(nc.vector.tensor_tensor(acc[:, :, 0:D], acc[:, :, 0:D], bc(den[:, :], 2, wide), ALU.mult))
                steps(nc.vector.tensor_tensor(acc[:, :, 0:D], acc[:, :, 0:D], bc(bias, 1, wide), ALU.add))
                steps(nc.vector.tensor_tensor(x, x, acc[:, :, 0:D], ALU.add))


def cell_of(nc, steps, pos, i0, frac):
    steps(nc.vector.tensor_scalar(frac, pos, 1.0, None, ALU.is_ge))
    steps(nc.vector.scalar_tensor_tensor(out=i0, in0=pos, scalar=2.0, in1=frac, op0=ALU.is_ge, op1=ALU.add))
    steps(nc.vector.scalar_tensor_tensor(out=i0, in0=pos, scalar=3.0, in1=i0, op0=ALU.is_ge, op1=ALU.add))
    steps(nc.vector.tensor_tensor(frac, pos, i0, ALU.subtract))


def basis_sums(nc, g, ph, block, rec, tmap, acc):
    groups = NC // GRP
    half = GRP // 2
    k5 = ph.sb("k5", [P, 2, KS])
    pos = ph.sb("pos", [P, GRP, 3])
    cell = ph.sb("cell", [P, GRP, 3])
    frac = ph.sb("frac", [P, GRP, 3])
    rest = ph.sb("rest", [P, GRP, 3])
    left = ph.sb("left", [P, GRP * 3, KS])
    hat = ph.sb("hat", [P, GRP * 3, KS])
    h01 = ph.sb("h01", [P, GRP, KS, KS])
    bas = [ph.sb(f"bas{b}", [P, GRP, K3]) for b in range(2)]
    oh = [ph.sb(f"oh{b}", [P, GRP, LO]) for b in range(2)]
    sums = [[ph.ps(f"sums{b}{h}", [K3, half, LO]) for h in range(2)] for b in range(2)]
    ready, mm_done, added, steps_s, steps_a = (ph.sem(s) for s in
                                               ("ready", "mm_done", "added", "steps", "steps_a"))
    PER = 4 + 2 + 5

    @block.vector
    def _(dve):
        def build(n, b, first):
            at = bass.ds(n * GRP, GRP)
            steps = Steps(dve, steps_s, n * PER + 1)
            steps(nc.vector.tensor_scalar(pos[:, :, :], rec[:, at, SATT:SATT + 3], float(KS - 1), None,
                                          ALU.mult))
            cell_of(nc, steps, pos[:, :, :], cell[:, :, :], frac[:, :, :])
            steps(nc.vector.tensor_scalar(rest[:, :, :], frac[:, :, :], -1.0, 1.0, ALU.mult, ALU.add))
            flat = [a[:, :, :].rearrange("p c d -> p (c d)") for a in (cell, frac, rest)]
            shape = [P, GRP * 3, KS]
            nc.vector.tensor_tensor(left[:, :, :], bc(k5[:, 0, :], 1, shape), bc(flat[0], 2, shape),
                                    ALU.is_equal)
            steps(nc.vector.tensor_tensor(hat[:, :, :], bc(k5[:, 1, :], 1, shape), bc(flat[0], 2, shape),
                                          ALU.is_equal))
            nc.vector.tensor_tensor(left[:, :, :], left[:, :, :], bc(flat[2], 2, shape), ALU.mult)
            steps(nc.vector.tensor_tensor(hat[:, :, :], hat[:, :, :], bc(flat[1], 2, shape), ALU.mult))
            steps(nc.vector.tensor_tensor(hat[:, :, :], hat[:, :, :], left[:, :, :], ALU.add))
            hats = hat[:, :, :].rearrange("p (c d) k -> p c d k", d=3)
            steps(nc.vector.tensor_tensor(h01[:, :, :, :],
                                          bc(hats[:, :, 0, :], 3, [P, GRP, KS, KS]),
                                          bc(hats[:, :, 1, :], 2, [P, GRP, KS, KS]), ALU.mult))
            if not first:
                dve.wait_ge(mm_done, n - 1)
            big = [P, GRP, KS * KS, KS]
            steps(nc.vector.tensor_tensor(
                bas[b][:, :, :].rearrange("p c (a k) -> p c a k", k=KS),
                bc(h01[:, :, :, :].rearrange("p c a k -> p c (a k)"), 3, big),
                bc(hats[:, :, 2, :], 2, big), ALU.mult))
            nc.vector.tensor_tensor(oh[b][:, :, :], bc(g.iota[:, 0:LO], 1, [P, GRP, LO]),
                                    bc(rec[:, at, SLO], 2, [P, GRP, LO]), ALU.is_equal).then_inc(ready, 1)
            assert steps.n == PER

        def add(n, b):
            dve.wait_ge(mm_done, n + 1)
            add_tiles(nc, dve, steps_a, 1, n, tmap, acc,
                      [sums[b][c // half][:, c % half:c % half + 1, :] for c in range(GRP)], ALU.add)
            dve.sem_inc(added, 1)

        steps = Steps(dve, steps_s)
        nc.vector.tensor_scalar(k5[:, 1, :], g.iota[:, 0:KS], 1.0, None, ALU.subtract)
        steps(nc.vector.tensor_copy(k5[:, 0, :], g.iota[:, 0:KS]))
        steps = Steps(dve, steps_a)
        steps(nc.vector.memset(acc, 0.0))
        build(0, 0, True)
        build(1, 1, True)
        add(0, 0)
        with dve.Fori(1, groups // 2) as t:
            for b in range(2):
                build(2 * t + b, b, False)
                add(2 * t + b - 1, 1 - b)
        add(groups - 1, 1)

    @block.tensor
    def _(pe):
        def group(n, b, first):
            pe.wait_ge(ready, n + 1)
            if not first:
                pe.wait_ge(added, n - 1)
            for c in range(GRP):
                last = nc.tensor.matmul(sums[b][c // half][:, c % half, :], bas[b][:, c, :],
                                        oh[b][:, c, :], start=True, stop=True)
            last.then_inc(mm_done, 1)

        group(0, 0, True)
        group(1, 1, True)
        with pe.Fori(1, groups // 2) as t:
            for b in range(2):
                group(2 * t + b, b, False)


def spline_cells(nc, g, name, att, dlo, key, frac):
    with Phase(nc, name) as ph:
        pos = ph.sb("pos", [P, NC, 3])
        i0 = ph.sb("i0", [P, NC, 3])
        steps_s = ph.sem("steps")
        with nc.Block() as block:
            @block.vector
            def _(dve):
                steps = Steps(dve, steps_s)
                steps(nc.vector.tensor_scalar(pos[:, :, :], att, float(KS - 1), None, ALU.mult))
                cell_of(nc, steps, pos[:, :, :], i0[:, :, :], frac)
                if key is None:
                    return
                steps(nc.vector.scalar_tensor_tensor(out=key, in0=i0[:, :, 0], scalar=4.0, in1=i0[:, :, 1],
                                                     op0=ALU.mult, op1=ALU.add))
                steps(nc.vector.scalar_tensor_tensor(out=key, in0=key, scalar=4.0, in1=i0[:, :, 2],
                                                     op0=ALU.mult, op1=ALU.add))
                steps(nc.vector.tensor_scalar(pos[:, :, 0], dlo, 0.0, None, ALU.is_ge))
                steps(nc.vector.scalar_tensor_tensor(out=key, in0=key, scalar=1.0, in1=pos[:, :, 0],
                                                     op0=ALU.add, op1=ALU.mult))
                steps(nc.vector.tensor_scalar(key, key, 1.0, None, ALU.subtract))


def cell_offsets(nc, ph_tmp, width):
    q, i0, i1 = ph_tmp

    def convert(steps, bm):
        steps(nc.vector.tensor_scalar(i0[:, :], bm[:, :], 1.0 / 16, -0.5 + 0.5 / 16, ALU.mult, ALU.add))
        steps(nc.vector.tensor_scalar(i0[:, :], i0[:, :], RND, RND, ALU.add, ALU.subtract))
        steps(nc.vector.scalar_tensor_tensor(out=q[:, :], in0=i0[:, :], scalar=-16.0, in1=bm[:, :],
                                             op0=ALU.mult, op1=ALU.add))
        steps(nc.vector.tensor_scalar(i1[:, :], q[:, :], 1.0 / 4, -0.5 + 0.5 / 4, ALU.mult, ALU.add))
        steps(nc.vector.tensor_scalar(i1[:, :], i1[:, :], RND, RND, ALU.add, ALU.subtract))
        steps(nc.vector.scalar_tensor_tensor(out=bm[:, :], in0=i0[:, :], scalar=9.0, in1=bm[:, :],
                                             op0=ALU.mult, op1=ALU.add))
        steps(nc.vector.tensor_tensor(bm[:, :], bm[:, :], i1[:, :], ALU.add))
        steps(nc.vector.tensor_scalar(bm[:, :], bm[:, :], float(width), None, ALU.mult))

    return convert


def fill_rows(nc, ph, block, tables):
    filled, cleared, marked = ph.sem("filled"), ph.sem("cleared"), ph.sem("marked")
    last_word = ph.sb("last_word", [P, 1])
    fills = [ph.sb(f"fill{n}", [P, rows // pieces, table.shape[1]])
             for n, (table, rows, pieces, marks) in enumerate(tables)]

    @block.gpsimd
    def _(pool):
        for fill in fills:
            last = nc.gpsimd.memset(fill[:, :, :], 0.0)
        last.then_inc(cleared, 1)
        pool.wait_ge(cleared, 1)
        for fill, (table, rows, pieces, marks) in zip(fills, tables):
            for word, number in marks:
                to = fill[:, :, word:word + 1]
                nc.gpsimd.memset(to.bitcast(I32) if isinstance(number, int) else to, number)
        nc.gpsimd.memset(last_word[:, :], 0.0).then_inc(marked, 1)

    @block.sync
    def _(sp):
        sp.wait_ge(marked, 1)
        for fill, (table, rows, pieces, marks) in zip(fills, tables):
            n = rows // pieces
            to = table.rearrange("(p j) w -> p j w", p=P)
            for q in range(pieces):
                sp.dma_start(to[:, q * n:(q + 1) * n, :], fill[:, :, :]).then_inc(filled, 16)
        sp.wait_ge(filled, 16 * sum(pieces for _, _, pieces, _ in tables))


def to_cells(nc, g, name, rec, tmap, h, F, frac, rowc, table):
    groups = NC // GRP
    W = F + 4
    with Phase(nc, name) as ph:
        at = [ph.sb(f"at{b}", [P, GRP], I32) for b in range(2)]
        pay = [ph.sb(f"pay{b}", [P, GRP, W]) for b in range(2)]
        oh = [ph.sb(f"oh{b}", [P, GRP, LO], BF16) for b in range(2)]
        ident = ph.sb("ident", [P, P], BF16)
        ohT = [ph.sb(f"ohT{b}", [LO, GRP, P]) for b in range(2)]
        pt = [ph.ps(f"pt{b}", [LO, GRP, P], BF16) for b in range(2)]
        px = [ph.ps(f"px{b}", [P, GRP, F]) for b in range(2)]
        oh_ready, turned, kept, spread, ready = (ph.sem(s) for s in ("oh_ready", "turned", "kept", "spread", "ready"))
        started = ph.sem("started")
        sent = [ph.pool_dma_sem(f"sent{b}") for b in range(2)]
        with nc.Block() as block:
            @block.scalar
            def _(act):
                def group(n, b, first):
                    act.wait_ge(turned, n + 1)
                    if not first:
                        act.wait_ge(spread, n - 1)
                    nc.scalar.copy(ohT[b][:, :, :], pt[b][:, :, :]).then_inc(kept, 1)

                group(0, 0, True)
                group(1, 1, True)
                with act.Fori(1, groups // 2) as t:
                    for b in range(2):
                        group(2 * t + b, b, False)

            @block.vector
            def _(dve):
                def hot(n, b, first):
                    if not first:
                        dve.wait_ge(turned, n - 1)
                    nc.vector.tensor_tensor(oh[b][:, :, :], bc(g.iota[:, 0:LO], 1, [P, GRP, LO]),
                                            bc(rec[:, bass.ds(n * GRP, GRP), DLO], 2, [P, GRP, LO]),
                                            ALU.is_equal).then_inc(oh_ready, 1)

                def pack(t, b, first):
                    n = 2 * t + b
                    slots = bass.ds(n * GRP, GRP)
                    if not first:
                        dve.wait_ge(sent[b], GRP * 16 * t)
                    nc.vector.tensor_copy(pay[b][:, :, F:F + 3], frac[:, slots, :])
                    nc.vector.tensor_copy(pay[b][:, :, F + 3].bitcast(I32), rec[:, slots, ROWS].bitcast(I32))
                    nc.vector.tensor_copy(at[b][:, :], rowc(slots))
                    dve.wait_ge(spread, n + 1)
                    nc.vector.tensor_copy(pay[b][:, :, 0:F], px[b][:, :, :]).then_inc(ready, 1)

                nc.vector.tensor_copy(ident[:, :], g.ident[:, :])
                hot(0, 0, True)
                hot(1, 1, True)
                pack(0, 0, True)
                pack(0, 1, True)
                with dve.Fori(1, groups // 2) as t:
                    hot(2 * t, 0, False)
                    hot(2 * t + 1, 1, False)
                    pack(t, 0, False)
                    pack(t, 1, False)

            @block.tensor
            def _(pe):
                def turn(n, b, first):
                    pe.wait_ge(oh_ready, n + 1)
                    if not first:
                        pe.wait_ge(kept, n - 1)
                    pe.sem_inc(started, 1)
                    for c in range(GRP):
                        last = nc.tensor.transpose(pt[b][:, c, :], oh[b][:, c, :], ident[:, :])
                    last.then_inc(turned, 1)

                def spread_rows(n, b, first):
                    tiles = values(nc, mybir.EngineType.PE, tmap[0:1, bass.ds(n * GRP, GRP)], GRP, NT - 1)
                    pe.wait_ge(kept, n + 1)
                    if not first:
                        pe.wait_ge(ready, n - 1)
                    for c in range(GRP):
                        last = nc.tensor.matmul(px[b][:, c, :], ohT[b][:, c, :], h[:, bass.ds(tiles[c], 1), :],
                                                start=True, stop=True)
                    last.then_inc(spread, 1)

                turn(0, 0, True)
                turn(1, 1, True)
                spread_rows(0, 0, True)
                spread_rows(1, 1, True)
                with pe.Fori(1, groups // 2) as t:
                    turn(2 * t, 0, False)
                    turn(2 * t + 1, 1, False)
                    spread_rows(2 * t, 0, False)
                    spread_rows(2 * t + 1, 1, False)

            @block.gpsimd
            def _(pool):
                with pool.Fori(0, groups // 2) as t:
                    for b in range(2):
                        pool.wait_ge(ready, 2 * t + b + 1)
                        pool.sem_inc(started, 1)
                        for c in range(GRP):
                            pool.indirect_dma_start(table[:, :],
                                                    bass.IndirectOffsetOnAxis(ap=at[b][:, c:c + 1], axis=0),
                                                    pay[b][:, c, :], None, bounds_check=P * NCC - 1,
                                                    oob_is_err=False).then_inc(sent[b], 16)
                for b in range(2):
                    pool.wait_ge(sent[b], GRP * 16 * (groups // 2))


def cell_messages(nc, g, name, table, cmap, w, F, FO, msgs):
    groups = NCC // GRP
    half = GRP // 2
    W = F + 4
    S = P // F
    Q = 8 * FO // S
    reach = KS * FO if S == 4 else 2 * KS * FO
    SCALE, WEIGH = (3, 3) if S == 2 else (4, 2)
    with Phase(nc, name) as ph:
        pay = [ph.sb(f"pay{b}", [P, GRP, W]) for b in range(DEEP)]
        at = [ph.sb(f"at{b}", [P, GRP], I32) for b in range(2)]
        rest = [ph.sb(f"rest{b}", [P, GRP, 3]) for b in range(2)]
        fac = ph.sb("fac", [P, GRP, S])
        hs = [ph.sb(f"hs{b}", [P, GRP, S * F]) for b in range(2)]
        hT = [ph.sb(f"hT{b}", [P, GRP, P]) for b in range(2)]
        v = ph.sb("v", [P, GRP, 2 * FO])
        v2 = ph.sb("v2", [P, GRP, 2 * FO])
        out = [ph.sb(f"out{b}", [P, GRP, FO]) for b in range(2)]
        o2 = ph.sb("o2", [P, GRP, FO])
        pt = [ph.ps(f"pt{k}", [P, half, P]) for k in range(2)]
        pp = [ph.ps(f"pp{k}", [P, half, Q]) for k in range(2)]
        scaled, turned, kept, mm_done, used, ready, steps_s, steps_w = (
            ph.sem(s) for s in ("scaled", "turned", "kept", "mm_done", "used", "ready", "steps", "steps_w"))
        started, begun = ph.sem("started"), ph.sem("begun")
        loaded = [ph.sem(f"loaded{b}") for b in range(DEEP)]
        sent = [ph.pool_dma_sem(f"sent{b}") for b in range(2)]
        with nc.Block() as block:
            @block.sync
            def _(sp):
                of = table.rearrange("(p j) w -> p j w", p=P)

                def load(t, b):
                    wait(sp, ready, DEEP * (t - 1) + b + 1)
                    sp.dma_start(pay[b][:, :, :], of[:, bass.ds((DEEP * t + b) * GRP, GRP), :]
                                 ).then_inc(loaded[b], 16)

                for b in range(DEEP):
                    load(0, b)
                with sp.Fori(1, groups // DEEP) as t:
                    for b in range(DEEP):
                        load(t, b)

            @block.tensor
            def _(pe):
                def turn(n, b):
                    pe.wait_ge(scaled, n + 1)
                    wait(pe, kept, n)
                    pe.sem_inc(begun, 1)
                    for c in range(GRP):
                        last = nc.tensor.transpose(pt[c // half][:, c % half, :], hs[b][:, c, :], g.ident[:, :])
                    last.then_inc(turned, 1)

                def product(n, b):
                    offs = values(nc, mybir.EngineType.PE, cmap[0:1, bass.ds(n * GRP, GRP)], GRP, 3 * 31 * FO)
                    pe.wait_ge(kept, n + 1)
                    for c in range(GRP):
                        k = c // half
                        if c % half == 0:
                            wait(pe, used, 2 * (n - 1) + k + 1)
                        if S == 2:
                            win = w[:, bass.ds(offs[c], reach)].rearrange("p (b y) -> p b y", b=2)[:, :, 0:2 * FO]
                            to = pp[k][:, c % half, :].rearrange("p (b y) -> p b y", b=2)
                        else:
                            win, to = w[:, bass.ds(offs[c], 2 * FO)], pp[k][:, c % half, :]
                        last = nc.tensor.matmul(to, hT[b][:, c, :], win, start=True, stop=True)
                        if c % half == half - 1:
                            last.then_inc(mm_done, 1)

                def group(n, b):
                    turn(n, b % 2)
                    if is_group(n - 1):
                        product(n - 1, (b - 1) % 2)

                for b in range(DEEP):
                    group(b, b)
                with pe.Fori(1, groups // DEEP) as t:
                    for b in range(DEEP):
                        group(DEEP * t + b, b)
                product(groups - 1, 1)

            @block.scalar
            def _(act):
                def keep(n, b):
                    act.wait_ge(turned, n + 1)
                    wait(act, mm_done, 2 * (n - 1))
                    for k in range(2):
                        last = nc.scalar.copy(hT[b][:, k * half:(k + 1) * half, :], pt[k][:, :, :])
                    last.then_inc(kept, 1)

                for b in range(DEEP):
                    keep(b, b % 2)
                with act.Fori(1, groups // DEEP) as t:
                    for b in range(DEEP):
                        keep(DEEP * t + b, b % 2)

            @block.vector
            def _(dve):
                def scale(t, b):
                    n = DEEP * t + b
                    steps = Steps(dve, steps_s, SCALE * n)
                    f, r = pay[b][:, :, F:F + 3], rest[b % 2]
                    dve.wait_ge(loaded[b], 16 * (t + 1))
                    steps(nc.vector.tensor_scalar(r[:, :, :], f, -1.0, 1.0, ALU.mult, ALU.add))
                    if S == 2:
                        nc.vector.tensor_copy(fac[:, :, 0], r[:, :, 0])
                        steps(nc.vector.tensor_copy(fac[:, :, 1], f[:, :, 0]))
                    else:
                        nc.vector.tensor_tensor(fac[:, :, 0], r[:, :, 0], r[:, :, 1], ALU.mult)
                        nc.vector.tensor_tensor(fac[:, :, 1], r[:, :, 0], f[:, :, 1], ALU.mult)
                        steps(nc.vector.tensor_tensor(fac[:, :, 2], f[:, :, 0], r[:, :, 1], ALU.mult))
                        steps(nc.vector.tensor_tensor(fac[:, :, 3], f[:, :, 0], f[:, :, 1], ALU.mult))
                    wait(dve, turned, n - 1)
                    shape = [P, GRP, S, F]
                    steps(nc.vector.tensor_tensor(hs[b % 2][:, :, :].rearrange("p c (s f) -> p c s f", s=S),
                                                  bc(pay[b][:, :, 0:F], 2, shape), bc(fac[:, :, :], 3, shape),
                                                  ALU.mult))
                    dve.sem_inc(scaled, 1)

                def weigh(n, b, uses):
                    steps = Steps(dve, steps_w, WEIGH * n)
                    f, r, o = pay[b][:, :, F:F + 3], rest[b % 2], out[b % 2]
                    part = [P, half, Q // 2]
                    for k in range(2):
                        cs = slice(k * half, (k + 1) * half)
                        d = 1 if S == 2 else 2
                        low, high = (v, v2) if S == 2 else (o, o2)
                        if S == 4 and k == 0:
                            wait(dve, sent[b % 2], uses)
                        dve.wait_ge(mm_done, 2 * n + k + 1)
                        nc.vector.tensor_tensor(low[:, cs, :], pp[k][:, :, 0:Q // 2], bc(r[:, cs, d], 2, part),
                                                ALU.mult)
                        nc.vector.tensor_tensor(high[:, cs, :], pp[k][:, :, Q // 2:Q], bc(f[:, cs, d], 2, part),
                                                ALU.mult).then_inc(used, 1)
                    dve.wait_ge(used, 2 * n + 2)
                    if S == 2:
                        steps(nc.vector.tensor_tensor(v[:, :, :], v[:, :, :], v2[:, :, :], ALU.add))
                        wait(dve, sent[b % 2], uses)
                        full = [P, GRP, FO]
                        nc.vector.tensor_tensor(o[:, :, :], v[:, :, 0:FO], bc(r[:, :, 2], 2, full), ALU.mult)
                        steps(nc.vector.tensor_tensor(o2[:, :, :], v[:, :, FO:2 * FO], bc(f[:, :, 2], 2, full),
                                                      ALU.mult))
                    else:
                        steps(nc.vector.tensor_copy(at[b % 2][:, :], pay[b][:, :, F + 3].bitcast(I32)))
                    if S == 2:
                        nc.vector.tensor_copy(at[b % 2][:, :], pay[b][:, :, F + 3].bitcast(I32))
                    steps(nc.vector.tensor_tensor(o[:, :, :], o[:, :, :], o2[:, :, :], ALU.add))
                    dve.sem_inc(ready, 1)

                def group(t, b):
                    scale(t, b)
                    n = DEEP * t + b - 1
                    if is_group(n):
                        weigh(n, (b - 1) % DEEP, GRP * 16 * (2 * t + (b - 1) // 2))

                for b in range(DEEP):
                    group(0, b)
                with dve.Fori(1, groups // DEEP) as t:
                    for b in range(DEEP):
                        group(t, b)
                weigh(groups - 1, DEEP - 1, GRP * 16 * ((groups - 1) // 2))

            @block.gpsimd
            def _(pool):
                with pool.Fori(0, groups // 2) as t:
                    for b in range(2):
                        pool.wait_ge(ready, 2 * t + b + 1)
                        pool.sem_inc(started, 1)
                        for c in range(GRP):
                            pool.indirect_dma_start(msgs[:, :],
                                                    bass.IndirectOffsetOnAxis(ap=at[b][:, c:c + 1], axis=0),
                                                    out[b][:, c, :], None, bounds_check=P * NC - 1,
                                                    oob_is_err=False).then_inc(sent[b], 16)
                for b in range(2):
                    pool.wait_ge(sent[b], GRP * 16 * (groups // 2))


def src_sums(nc, g, name, slo, tmap, msgs, F, acc):
    groups = NC // GRP
    with Phase(nc, name) as ph:
        rows = [ph.sb(f"rows{b}", [P, GRP, F]) for b in range(2)]
        oh = [ph.sb(f"oh{b}", [P, GRP, LO]) for b in range(2)]
        sums = [ph.ps(f"sums{b}", [LO, GRP, F]) for b in range(2)]
        oh_ready, mm_done, added, steps_a = (ph.sem(s) for s in ("oh_ready", "mm_done", "added", "steps_a"))
        loaded = [ph.sem(f"loaded{b}") for b in range(2)]
        with nc.Block() as block:
            @block.sync
            def _(sp):
                of = msgs.rearrange("(p j) w -> p j w", p=P)

                def load(t, first):
                    for b in range(2):
                        if not first:
                            sp.wait_ge(mm_done, 2 * t + b - 1)
                        sp.dma_start(rows[b][:, :, :], of[:, bass.ds((2 * t + b) * GRP, GRP), :]
                                     ).then_inc(loaded[b], 16)

                load(0, True)
                with sp.Fori(1, groups // 2) as t:
                    load(t, False)

            @block.vector
            def _(dve):
                def hot(n, b, first):
                    if not first:
                        dve.wait_ge(mm_done, n - 1)
                    nc.vector.tensor_tensor(oh[b][:, :, :], bc(g.iota[:, 0:LO], 1, [P, GRP, LO]),
                                            bc(slo[:, bass.ds(n * GRP, GRP)], 2, [P, GRP, LO]),
                                            ALU.is_equal).then_inc(oh_ready, 1)

                def add(n, b):
                    dve.wait_ge(mm_done, n + 1)
                    add_tiles(nc, dve, steps_a, 1, n, tmap, acc, [sums[b][:, c:c + 1, :] for c in range(GRP)],
                              ALU.add)
                    dve.sem_inc(added, 1)

                steps = Steps(dve, steps_a)
                steps(nc.vector.memset(acc, 0.0))
                hot(0, 0, True)
                hot(1, 1, True)
                add(0, 0)
                with dve.Fori(1, groups // 2) as t:
                    for b in range(2):
                        hot(2 * t + b, b, False)
                        add(2 * t + b - 1, 1 - b)
                add(groups - 1, 1)

            @block.tensor
            def _(pe):
                def product(t, b, first):
                    n = 2 * t + b
                    pe.wait_ge(oh_ready, n + 1)
                    pe.wait_ge(loaded[b], 16 * (t + 1))
                    if not first:
                        pe.wait_ge(added, n - 1)
                    for c in range(GRP):
                        last = nc.tensor.matmul(sums[b][:, c, :], oh[b][:, c, :], rows[b][:, c, :],
                                                start=True, stop=True)
                    last.then_inc(mm_done, 1)

                product(0, 0, True)
                product(0, 1, True)
                with pe.Fori(1, groups // 2) as t:
                    product(t, 0, False)
                    product(t, 1, False)


def finish(nc, g, acc, bias, x, out):
    wide = [LO, NT, D]
    with Phase(nc, "finish") as ph:
        steps_s, stored = ph.sem("steps"), ph.sem("stored")
        with nc.Block() as block:
            @block.vector
            def _(dve):
                steps = Steps(dve, steps_s)
                steps(nc.vector.tensor_tensor(acc, acc, bc(g.rdeg[:, :], 2, wide), ALU.mult))
                steps(nc.vector.tensor_tensor(acc, acc, bc(bias, 1, wide), ALU.add))
                steps(nc.vector.tensor_tensor(acc, acc, x, ALU.add))

            @block.sync
            def _(sp):
                sp.wait_ge(steps_s, 3)
                sp.dma_start(out.rearrange("(p c) f -> p c f", p=LO), acc).then_inc(stored, 16)
                sp.wait_ge(stored, 16)


def keep_column(nc, name, to, of):
    with nc.Block() as block:
        @block.vector
        def _(dve):
            nc.vector.tensor_copy(to, of)


def join_columns(nc, name, to, of, zero):
    with nc.Block() as block:
        @block.vector
        def _(dve):
            nc.vector.tensor_copy(to, of)
            nc.vector.memset(zero, 0.0)


def program(nc, x_in, src, dst, edge_attr, lam, cheb_W, cheb_b, gat_Wsrc, gat_bsrc, gat_Wdst, gat_bdst, gat_attn,
            gat_bias, stn1_w, stn1_b, stn2_w, stn2_b, stn3_w, stn3_b, stn4_w, stn4_b, conv_w, conv_b, out):
    whole = ExitStack()
    with whole:
        def sb(name, shape, dt=F32, ctx=whole):
            return ctx.enter_context(nc.sbuf_tensor(name, shape, dt))

        def dram(name, shape, dt=F32):
            return nc.dram_tensor(name, shape, dt).ap()

        g = Tensors()
        g.iota, g.ones, g.ident, g.tri = (sb(n, [P, P]) for n in ("iota", "ones", "ident", "tri"))
        g.jcol, g.junk, g.re = sb("jcol", [P, NC // P]), sb("junk", [P, 1]), sb("re", [LO, 5])
        g.degd, g.degs, g.norm, g.rdeg = (sb(n, [LO, NT]) for n in ("degd", "degs", "norm", "rdeg"))
        rec_d, rec_s = dram("rec_d", [P * NC, RECD]), dram("rec_s", [P * NC, RECS])
        map_d, map_s = dram("map_d", [NC], I32), dram("map_s", [NC], I32)
        map_c, map_c2 = dram("map_c", [NC], I32), dram("map_c2", [NC], I32)
        table = dram("table", [N, D])
        table_fst = dram("table_fst", [N, D + 4])
        fse = dram("fse", [P * NC, D + 4])
        cells1, cells2 = dram("cells1", [P * NCC, HID + 4]), dram("cells2", [P * NCC, D + 4])
        msgs1, msgs2 = dram("msgs1", [P * NC, HID]), dram("msgs2", [P * NC, D])
        row = lambda a: a.rearrange("(o c) -> o c", o=1)
        spread = lambda a, n: a.partition_broadcast(n)
        skipped = int(BIG)

        constants(nc, g)
        lam_b, w1, w3, w4 = sb("lam_b", [LO, 1]), sb("w1", [K3, HID]), sb("w3", [HID, HID]), sb("w4", [HID, 3])
        cheb_w, gat_w = sb("cheb_w", [3 * D, D]), sb("gat_w", [D, 2 * D])
        b_cheb, b_gat, b_att = sb("b_cheb", [LO, D]), sb("b_gat", [LO, 2 * D]), sb("b_att", [LO, D])
        attn = sb("attn", [P, D])
        b1, b2, b3 = (sb(f"b{k}", [LO, HID]) for k in (1, 2, 3))
        b4, b5 = sb("b4", [LO, 3]), sb("b5", [LO, D])
        slo = sb("slo", [P, NC])
        maps = sb("maps", [3, NC], I32)
        tmd, tms, cmap = maps[0:1, :], maps[1:2, :], maps[2:3, 0:NCC]

        def narrow_map(ph):
            return [ph.sb(f"tmp{k}", [P, NC // P]) for k in range(3)]

        wide = sb("wide", [LO, NT, 3 * D])
        h1 = wide[:, :, 0:HID]
        with ExitStack() as c2:
            def eb(name, dt=F32, ctx=c2):
                return sb(name, [P, ECP], dt, ctx)

            e = Tensors()
            e.src, e.rows, e.rowd, e.rowc = (eb(n, I32) for n in ("src", "row_s", "row_d", "row_c"))
            e.att, e.lod = sb("att", [P, ECP, 3], F32, c2), eb("lod")
            with ExitStack() as c3:
                e.tiled, e.los, e.tiles, key = (eb(n, F32, c3) for n in ("tiled", "los", "tiles", "cellkey"))
                load_edges(nc, g, e, src, dst, edge_attr)
                work = [eb(f"work{k}", F32, c3) for k in range(3)]
                with Phase(nc, "ranks") as pr, Phase(nc, "fill1") as pf, nc.Block() as block:
                    rank(nc, g, pr, block, work, e.tiles[:, :], ECP, NT, NC, e.rows[:, :], None, map_s)
                    fill_rows(nc, pf, block, ((rec_s, NC, 8, ((SLO, -1.0),)),
                                              (rec_d, NC, 8, ((ROWS, skipped), (ROWC, skipped), (DLO, -1.0)))))
                with Phase(nc, "scats") as ps, Phase(nc, "cellk") as pk, Phase(nc, "fill2") as pf, \
                        Phase(nc, "rankd") as pd, Phase(nc, "rankc") as pc, nc.Block() as block:
                    scatter_records(nc, g, ps, block, ((SLO, e.los), (SATT, e.att)), RECS, e.rows, rec_s)
                    edge_cells(nc, g, pk, block, work, e.att, e.tiled[:, :], key[:, :])
                    fill_rows(nc, pf, block, ((msgs1, NC, 104, ()), (msgs2, NC, 104, ()),
                                              (cells1, NCC, 96, ((HID + 3, skipped),)),
                                              (cells2, NCC, 96, ((D + 3, skipped),))))
                    rank(nc, g, pd, block, work, e.tiled[:, :], ECP, NT, NC, e.rowd[:, :], None, map_d)
                    rank(nc, g, pc, block, work, key[:, :], ECP, CELLS, NCC, e.rowc[:, :],
                         cell_offsets(nc, narrow_map(pc), HID), map_c)
            recs = sb("recs", [P, NC, RECS], F32, c2)
            bt = sb("bt", [K3, NT, LO], F32, c2)
            load_table(nc, g, "params", [
                (tmd, row(map_d)), (tms, row(map_s)), (cmap, row(map_c)[:, 0:NCC]),
                (recs[:, :, :], rec_s.rearrange("(p j) w -> p j w", p=P)), (lam_b[:, :], spread(lam, LO)),
                (w1[:, :], stn1_w.rearrange("k i o -> k (i o)")), (w3[:, :], stn3_w), (w4[:, :], stn4_w),
                (cheb_w[:, :], cheb_W.rearrange("o i -> i o")), (gat_w[:, 0:D], gat_Wsrc.rearrange("o i -> i o")),
                (gat_w[:, D:2 * D], gat_Wdst.rearrange("o i -> i o")), (b_cheb[:, :], spread(cheb_b, LO)),
                (b_gat[:, 0:D], spread(gat_bsrc, LO)), (b_gat[:, D:2 * D], spread(gat_bdst, LO)),
                (b_att[:, :], spread(gat_bias, LO)), (attn[:, :], spread(gat_attn.rearrange("a b c -> (a b c)"), P)),
                (b1[:, :], spread(stn1_b, LO)), (b2[:, :], spread(stn2_b, LO)), (b3[:, :], spread(stn3_b, LO)),
                (b4[:, :], spread(stn4_b, LO)), (b5[:, :], spread(conv_b, LO))])
            with Phase(nc, "scatd") as ps, Phase(nc, "basis") as pb, nc.Block() as block:
                scatter_records(nc, g, ps, block, ((SRC, e.src), (ROWS, e.rows), (ROWC, e.rowc), (ATT, e.att),
                                                   (DLO, e.lod)), RECD, e.rowd, rec_d)
                basis_sums(nc, g, pb, block, recs, tms, bt[:, :, :])
            keep_column(nc, "slo", slo[:, :], recs[:, :, SLO])
            node_linear(nc, g, "stn1", bt[:, :, :], K3, w1[:, :], None, HID, h1, transposed=True)
        node_scales(nc, g, lam_b[:, :])
        scale_bias_elu(nc, g, "elu1", h1, HID, g.rdeg[:, :], b1[:, :])

        rec = sb("rec", [P, NC, RECD])
        load_table(nc, g, "ldrec", [(rec[:, :, :], rec_d.rearrange("(p j) w -> p j w", p=P))])

        def stacked(w, kernel, S):
            F, moved = P // S, {2: (0, KS * KS), 4: (0, KS, KS * KS, KS * KS + KS)}[S]
            return [(w[q * F:(q + 1) * F, 0:K3 - m, :], kernel[m:K3].rearrange("k i o -> i k o"))
                    for q, m in enumerate(moved)]

        t4 = sb("t4", [LO, NT, 4])
        with ExitStack() as c2:
            frac = sb("frac", [P, NC, 3], F32, c2)
            spline_cells(nc, g, "frac", rec[:, :, ATT:ATT + 3], None, None, frac[:, :, :])
            to_cells(nc, g, "toc1", rec, tmd, h1, HID, frac,
                     lambda slots: rec[:, slots, ROWC].bitcast(I32), cells1)
        with ExitStack() as c2:
            w2 = sb("w2", [P, K3, HID], F32, c2)
            load_table(nc, g, "ldw2", stacked(w2, stn2_w, 2))
            cell_messages(nc, g, "msg1", cells1, cmap, w2[:, :, :].rearrange("i k o -> i (k o)"), HID, HID, msgs1)
        src_sums(nc, g, "sum1", slo, tms, msgs1, HID, h1)
        scale_bias_elu(nc, g, "elu2", h1, HID, g.rdeg[:, :], b2[:, :])
        with ExitStack() as c3:
            h3 = sb("h3", [LO, NT, HID], F32, c3)
            node_linear(nc, g, "stn3", h1, HID, w3[:, :], b3[:, :], HID, h3[:, :, :])
            scale_bias_elu(nc, g, "elu3", h3[:, :, :], HID, None, None)
            node_linear(nc, g, "stn4", h3[:, :, :], HID, w4[:, :], b4[:, :], 3, t4[:, :, 0:3])

        x = sb("x", [LO, NT, D])
        load_table(nc, g, "ldx", [(x[:, :, :], x_in.rearrange("(p c) f -> p c f", p=LO))])
        att2 = sb("att2", [P, NC, 3])
        with ExitStack() as c1:
            fdt = sb("fdt", [LO, NT, D + 4], F32, c1)
            with ExitStack() as c2:
                acc = sb("acc", [LO, NT, D], F32, c2)
                cat = wide
                layer_norm_relu(nc, g, "ln0", x[:, :, :], cat[:, :, 0:D])
                for layer in range(2):
                    for order in (1, 2):
                        name = f"cheb{layer}{order}"
                        store_scaled(nc, g, name + "s", cat[:, :, (order - 1) * D:order * D], g.norm[:, :], table)
                        propagate(nc, g, name + "p", rec, tmd, table, acc[:, :, :])
                        chebyshev(nc, g, name + "c", acc[:, :, :], cat, order)
                    node_linear(nc, g, f"cheb{layer}l", cat[:, :, :], 3 * D, cheb_w[:, :], b_cheb[:, :], D,
                                cat[:, :, 0:D] if layer == 0 else acc[:, :, :], relu=True)
                join_columns(nc, "joint", fdt[:, :, D:D + 3], t4[:, :, 0:3], fdt[:, :, D + 3:D + 4])
                node_linear(nc, g, "gatfs", acc[:, :, :], D, gat_w[:, 0:D], b_gat[:, 0:D], D, fdt[:, :, 0:D])
                store_scaled(nc, g, "gats", fdt[:, :, :], None, table_fst)
                node_linear(nc, g, "gatfd", acc[:, :, :], D, gat_w[:, D:2 * D], b_gat[:, D:2 * D], D, fdt[:, :, 0:D])
            lgs = sb("lgs", [P, NC], F32, c1)
            mx = sb("mx", [LO, NT, 1], F32, c1)
            attention_scores(nc, g, rec, tmd, table_fst, fse, fdt[:, :, :], attn[:, :], lgs, mx[:, :, :], att2)
            att = sb("att0", [LO, NT, D + 1], F32, c1)
            attention_sums(nc, g, rec, tmd, fse, lgs, mx[:, :, :], att[:, :, :])
            attention_end(nc, g, att[:, :, :], b_att[:, :], x[:, :, :])

        rowc = sb("rowc", [P, NC], I32)
        frac = sb("frac2", [P, NC, 3])
        with ExitStack() as c2:
            key = sb("key", [P, NC], F32, c2)
            spline_cells(nc, g, "cells2", att2[:, :, :], rec[:, :, DLO], key[:, :], frac[:, :, :])
            with Phase(nc, "rank2") as pr, nc.Block() as block:
                rank(nc, g, pr, block, [pr.sb(f"work{k}", [P, NC]) for k in range(3)], key[:, :],
                     NC, CELLS, NCC, rowc[:, :], cell_offsets(nc, narrow_map(pr), D), map_c2)
        with ExitStack() as c2:
            h = wide[:, :, 0:D]
            w5 = sb("w5", [P, K3, D], F32, c2)
            load_table(nc, g, "ldw5", stacked(w5, conv_w, 4) + [(cmap, row(map_c2)[:, 0:NCC])])
            layer_norm_relu(nc, g, "ln1", x[:, :, :], h)
            to_cells(nc, g, "toc2", rec, tmd, h, D, frac, lambda slots: rowc[:, slots], cells2)
            cell_messages(nc, g, "msg2", cells2, cmap, w5[:, :, :].rearrange("i k o -> i (k o)"), D, D, msgs2)
            src_sums(nc, g, "sum2", slo, tms, msgs2, D, h)
            finish(nc, g, h, b5[:, :], x[:, :, :], out)


_INS = ["x", "src", "dst", "edge_attr_3", "L0_gnn_laplacian_lambda_max", "L0_gnn_cheb_W", "L0_gnn_cheb_b",
        "L0_gnn_gat_Wsrc", "L0_gnn_gat_bsrc", "L0_gnn_gat_Wdst", "L0_gnn_gat_bdst", "L0_gnn_gat_attn",
        "L0_gnn_gat_bias", "L1_gnn_stn1_w", "L1_gnn_stn1_b", "L1_gnn_stn2_w", "L1_gnn_stn2_b", "L1_gnn_stn3_w",
        "L1_gnn_stn3_b", "L1_gnn_stn4_w", "L1_gnn_stn4_b", "L1_gnn_conv_w", "L1_gnn_conv_b"]


def kernel(**inputs):
    import numpy as _np
    import concourse.bacc as _bacc
    from concourse import mybir as _mybir
    from concourse.bass_utils import run_bass_kernel_spmd as _run

    nc = _bacc.Bacc("TRN2", target_bir_lowering=False, num_devices=1)
    arrays, args = {}, []
    for name in _INS:
        a = _np.ascontiguousarray(inputs[name])
        arrays[f"in_{name}_dram"] = a
        args.append(nc.dram_tensor(f"in_{name}_dram", a.shape, _mybir.dt.from_np(a.dtype), kind="ExternalInput").ap())
    out = nc.dram_tensor("out_0_dram", (12500, 32), _mybir.dt.float32, kind="ExternalOutput").ap()
    program(nc, *args, out)
    r = _run(nc, [arrays], core_ids=[0])
    return r.results[0]["out_0_dram"]
```

```python
from contextlib import ExitStack

import concourse.bass as bass
from concourse import mybir

F32, BF16, I32 = mybir.dt.float32, mybir.dt.bfloat16, mybir.dt.int32
ALU = mybir.AluOpType
ACT = mybir.ActivationFunctionType
AX = mybir.AxisListType.X

P = 128
N, D = 12500, 32
LO, NT = 125, 100
E = 200000
EC = -(-E // P)
GRP = 8
DEEP = 4
ECP = -(-EC // (2 * GRP)) * 2 * GRP
HID = 64
KS = 5
K3 = KS ** 3
CELLS = 4 ** 3
NC = -(-((E + NT * (P - 1)) // P) // (DEEP * GRP)) * DEEP * GRP
NCC = -(-((E + CELLS * (P - 1)) // P) // (2 * GRP)) * 2 * GRP
BIG = 1.0e6
RND = 12582912.0
LOW = 1.0e30
SRC, ROWS, ROWC, ATT, DLO, RECD = 0, 1, 2, 3, 6, 7
SLO, SATT, RECS = 0, 1, 4


def bc(ap, axis, shape):
    return ap.unsqueeze(axis).to_broadcast(shape)


class Tensors:
    pass


class Steps:

    def __init__(self, engine, sem, base=0):
        self.engine, self.sem, self.base, self.n = engine, sem, base, 0

    def __call__(self, instruction):
        instruction.then_inc(self.sem, 1)
        self.n += 1
        self.engine.wait_ge(self.sem, self.base + self.n)


class Phase:

    def __init__(self, nc, name):
        self.nc, self.name, self.ctx, self.sems = nc, name, ExitStack(), []

    def __enter__(self):
        self.ctx.__enter__()
        return self

    def __exit__(self, *e):
        if e[0] is None:
            self.nc.clear_and_free_semaphores(self.sems)
            self.nc.all_engine_barrier()
        return self.ctx.__exit__(*e)

    def sb(self, name, shape, dt=F32):
        return self.ctx.enter_context(self.nc.sbuf_tensor(f"{self.name}_{name}", shape, dt))

    def ps(self, name, shape, dt=F32):
        return self.ctx.enter_context(self.nc.psum_tensor(f"{self.name}_{name}", shape, dt))

    def sem(self, name):
        self.sems.append(self.nc.alloc_semaphore(f"{self.name}_{name}"))
        return self.sems[-1]

    def pool_dma_sem(self, name):
        return self.nc.alloc_semaphore(f"{self.name}_{name}")


def constants(nc, g):
    with Phase(nc, "const") as ph:
        ii = ph.sb("ii", [P, P], I32)
        jj = ph.sb("jj", [P, NC // P], I32)
        made, steps = ph.sem("made"), ph.sem("steps")
        with nc.Block() as block:
            @block.gpsimd
            def _(pool):
                nc.gpsimd.iota(ii[:, :], [[1, P]], base=0, channel_multiplier=0)
                nc.gpsimd.iota(jj[:, :], [[P, NC // P]], base=0, channel_multiplier=1)
                nc.gpsimd.memset(g.ones[:, :], 1.0)
                nc.gpsimd.memset(g.ident[:, :], 1.0).then_inc(made, 1)
                pool.wait_ge(made, 1)
                nc.gpsimd.affine_select(out=g.tri[:, :], in_=g.ones[:, :], pattern=[[1, P]], compare_op=ALU.is_gt,
                                        fill=0.0, base=0, channel_multiplier=-1)
                nc.gpsimd.affine_select(out=g.ident[:, :], in_=g.ident[:, :], pattern=[[1, P]],
                                        compare_op=ALU.is_equal, fill=0.0, base=0,
                                        channel_multiplier=-1).then_inc(made, 1)

            @block.vector
            def _(dve):
                dve.wait_ge(made, 2)
                nc.vector.tensor_copy(g.iota[:, :], ii[:, :])
                nc.vector.tensor_copy(g.jcol[:, :], jj[:, :])


def split_nodes(nc, steps, ids, lo, tile):
    steps(nc.vector.tensor_copy(tile, ids))
    steps(nc.vector.tensor_scalar(lo, tile, 1.0 / NT, -0.5 + 0.5 / NT, ALU.mult, ALU.add))
    steps(nc.vector.tensor_scalar(lo, lo, RND, RND, ALU.add, ALU.subtract))
    steps(nc.vector.scalar_tensor_tensor(out=tile, in0=lo, scalar=-float(NT), in1=tile, op0=ALU.mult, op1=ALU.add))


def load_edges(nc, g, e, src, dst, attr):
    full = P - 1
    rest = E - full * EC
    with Phase(nc, "load") as ph:
        dst_i = ph.sb("dst_i", [P, ECP], I32)
        att_loaded = ph.sem("att_loaded")
        cleared, loaded, split, padded = ph.sem("cleared"), ph.sem("loaded"), ph.sem("split"), ph.sem("padded")
        steps_s = ph.sem("steps")
        with nc.Block() as block:
            @block.sync
            def _(sp):
                sp.wait_ge(cleared, 1)
                sp.dma_start(e.att[0:full, 0:EC, :], attr[0:full * EC, :].rearrange("(p c) k -> p c k", p=full)
                             ).then_inc(att_loaded, 16)
                sp.dma_start(e.att[full:P, 0:rest, :], attr[full * EC:E, :].rearrange("(p c) k -> p c k", p=1)
                             ).then_inc(att_loaded, 16)
                for ids, given in ((e.src, src), (dst_i, dst)):
                    sp.dma_start(ids[0:full, 0:EC], given[0:full * EC].rearrange("(p c) -> p c", p=full)
                                 ).then_inc(loaded, 16)
                    sp.dma_start(ids[full:P, 0:rest], given[full * EC:E].rearrange("(p c) -> p c", p=1)
                                 ).then_inc(loaded, 16)
                sp.wait_ge(att_loaded, 32)

            @block.gpsimd
            def _(pool):
                nc.gpsimd.memset(e.att[:, :, :], 0.0)
                nc.gpsimd.memset(e.src[:, :], 0)
                nc.gpsimd.memset(dst_i[:, :], 0).then_inc(cleared, 1)
                pool.wait_ge(split, 1)
                for tile in (e.tiled, e.tiles):
                    nc.gpsimd.memset(tile[:, EC:ECP], -1.0)
                    last = nc.gpsimd.affine_select(out=tile[:, 0:EC], in_=tile[:, 0:EC], pattern=[[-1, EC]],
                                                   compare_op=ALU.is_ge, fill=-1.0, base=E - 1,
                                                   channel_multiplier=-EC)
                last.then_inc(padded, 1)

            @block.vector
            def _(dve):
                steps = Steps(dve, steps_s)
                dve.wait_ge(loaded, 64)
                split_nodes(nc, steps, dst_i[:, :], e.lod[:, :], e.tiled[:, :])
                split_nodes(nc, steps, e.src[:, :], e.los[:, :], e.tiles[:, :])
                nc.vector.memset(g.junk[:, :], 0.0).then_inc(split, 1)
                dve.wait_ge(padded, 1)


def rank(nc, g, ph, block, work, key, width, buckets, chunks, row, chunk_map, map_dram):
    mg = NC // P
    m, run, pos = work
    key16, m16 = ph.sb("key16", [P, width], BF16), ph.sb("m16", [P, width], BF16)
    cnt = ph.sb("cnt", [P, buckets])
    cc = ph.sb("cc", [P, buckets])
    cend = ph.sb("cend", [P, buckets])
    off = ph.sb("off", [P, buckets])
    bm = ph.sb("bm", [P, mg])
    bmi = ph.sb("bmi", [P, mg], I32)
    pre, tot = ph.ps("pre", [P, buckets]), ph.ps("tot", [P, buckets])
    scanned, merged = ph.sem("scanned"), ph.sem("merged")
    m2, run2 = ph.sb("m2", [P, width]), ph.sb("run2", [P, width])
    steps_s, counted, summed, mapped, stored, shortened = (
        ph.sem(x) for x in ("steps", "counted", "summed", "mapped", "stored", "shortened"))

    @block.vector
    def _(dve):
        steps = Steps(dve, shortened)
        steps(nc.vector.tensor_copy(key16[:, :], key))
        with dve.Fori(0, buckets) as b:
            steps = Steps(dve, steps_s, b)
            steps(nc.vector.tensor_scalar(m16[:, :], key16[:, :], g.iota[:, bass.ds(b, 1)], None, ALU.is_equal,
                                          ALU.add, accum_out=cnt[:, bass.ds(b, 1)]))
        steps = Steps(dve, steps_s, buckets)
        steps(nc.vector.memset(pos[:, :], 0.0))
        nc.vector.memset(g.junk[:, :], 0.0).then_inc(counted, 1)
        dve.wait_ge(summed, 1)
        steps(nc.vector.tensor_scalar(cc[:, :], tot[:, :], P / 2 - 0.5, 1.0 / P, ALU.add, ALU.mult))
        steps(nc.vector.tensor_scalar(cc[:, :], cc[:, :], RND, RND, ALU.add, ALU.subtract))
        steps(nc.vector.tensor_tensor_scan(cend[:, :], cc[:, :], cc[:, :], 0.0, ALU.add, ALU.bypass))
        steps(nc.vector.tensor_tensor(cc[:, :], cend[:, :], cc[:, :], ALU.subtract))
        steps(nc.vector.tensor_scalar(cc[:, :], cc[:, :], float(P), -1.0, ALU.mult, ALU.add))
        steps(nc.vector.tensor_tensor(off[:, :], cc[:, :], pre[:, :], ALU.add))
        for q in range(mg):
            steps(nc.vector.tensor_scalar(cc[:, :], cend[:, :], g.jcol[:, q:q + 1], None, ALU.is_le,
                                          ALU.add, accum_out=bm[:, q:q + 1]))
        steps(nc.vector.tensor_scalar(bm[:, :], bm[:, :], float(buckets - 1), None, ALU.min))
        if chunk_map is not None:
            chunk_map(steps, bm)
        steps(nc.vector.tensor_copy(bmi[:, :], bm[:, :]))
        nc.vector.memset(g.junk[:, :], 0.0).then_inc(mapped, 1)
        before = steps.base + steps.n
        with dve.Fori(0, buckets // 2) as b:
            steps = Steps(dve, steps_s, before + 3 * b)
            pair = ((m, run, 2 * b), (m2, run2, 2 * b + 1))
            for ms, rs, k in pair:
                same = nc.vector.tensor_scalar(ms[:, :], key, g.iota[:, bass.ds(k, 1)], None, ALU.is_equal)
            steps(same)
            for ms, rs, k in pair:
                scan = nc.vector.tensor_tensor_scan(rs[:, :], ms[:, :], ms[:, :], off[:, bass.ds(k, 1)],
                                                    ALU.add, ALU.bypass)
            steps(scan)
            dve.sem_inc(scanned, 1)
            nc.vector.copy_predicated(pos[:, :], m[:, :].bitcast(I32), run[:, :]).then_inc(scanned, 1)
            dve.wait_ge(scanned, 2 * b + 2)
            dve.sem_inc(merged, 1)
            steps(nc.vector.copy_predicated(pos[:, :], m2[:, :].bitcast(I32), run2[:, :]))
        steps = Steps(dve, steps_s, before + 3 * (buckets // 2))
        steps(nc.vector.tensor_scalar(run[:, :], pos[:, :], 1.0 / P, -0.5 + 0.5 / P, ALU.mult, ALU.add))
        steps(nc.vector.tensor_scalar(run[:, :], run[:, :], RND, RND, ALU.add, ALU.subtract))
        steps(nc.vector.scalar_tensor_tensor(out=pos[:, :], in0=run[:, :], scalar=-float(P), in1=pos[:, :],
                                             op0=ALU.mult, op1=ALU.add))
        steps(nc.vector.scalar_tensor_tensor(out=pos[:, :], in0=pos[:, :], scalar=float(chunks),
                                             in1=run[:, :], op0=ALU.mult, op1=ALU.add))
        steps(nc.vector.tensor_scalar(m[:, :], key, 0.0, BIG, ALU.is_lt, ALU.mult))
        steps(nc.vector.tensor_tensor(pos[:, :], pos[:, :], m[:, :], ALU.add))
        steps(nc.vector.tensor_copy(row, pos[:, :]))

    @block.tensor
    def _(pe):
        pe.wait_ge(counted, 1)
        nc.tensor.matmul(pre[:, :], g.tri[:, :], cnt[:, :], start=True, stop=True)
        nc.tensor.matmul(tot[:, :], g.ones[:, :], cnt[:, :], start=True, stop=True).then_inc(summed, 1)

    @block.sync
    def _(sp):
        sp.wait_ge(mapped, 1)
        with nc.allow_non_contiguous_dma("a map of chunks, one word each"):
            sp.dma_start(map_dram.rearrange("(g p) -> p g", p=P), bmi[:, :]).then_inc(stored, 16)
        sp.wait_ge(stored, 16)


def edge_cells(nc, g, ph, block, work, att, tile, key):
    pos, i0, frac = work
    steps_s = ph.sem("cell_steps")

    @block.vector
    def _(dve):
        steps = Steps(dve, steps_s)
        steps(nc.vector.memset(key, 0.0))
        for d in range(3):
            steps(nc.vector.tensor_scalar(pos[:, :], att[:, :, d], float(KS - 1), None, ALU.mult))
            cell_of(nc, steps, pos[:, :], i0[:, :], frac[:, :])
            steps(nc.vector.scalar_tensor_tensor(out=key, in0=key, scalar=4.0, in1=i0[:, :],
                                                 op0=ALU.mult, op1=ALU.add))
        steps(nc.vector.tensor_scalar(pos[:, :], tile, 0.0, None, ALU.is_ge))
        steps(nc.vector.scalar_tensor_tensor(out=key, in0=key, scalar=1.0, in1=pos[:, :], op0=ALU.add, op1=ALU.mult))
        steps(nc.vector.tensor_scalar(key, key, 1.0, None, ALU.subtract))


def scatter_records(nc, g, ph, block, fields, words, rows, table):
    groups = ECP // GRP
    at = [ph.sb(f"at{b}", [P, GRP], I32) for b in range(2)]
    rec = [ph.sb(f"rec{b}", [P, GRP, words]) for b in range(2)]
    ready, started = ph.sem("ready"), ph.sem("started")
    sent = [ph.pool_dma_sem(f"sent{b}") for b in range(2)]

    @block.scalar
    def _(act):
        def pack(t, first):
            for b in range(2):
                if not first:
                    act.wait_ge(sent[b], GRP * 16 * t)
                slots = bass.ds((2 * t + b) * GRP, GRP)
                for word, source in fields:
                    n = source.shape[2] if len(source.shape) == 3 else 1
                    to = rec[b][:, :, word:word + n] if n > 1 else rec[b][:, :, word]
                    of = source[:, slots, :] if n > 1 else source[:, slots]
                    nc.scalar.copy(to.bitcast(I32) if source.dtype == I32 else to, of)
                nc.scalar.copy(at[b][:, :], rows[:, slots]).then_inc(ready, 1)

        pack(0, True)
        with act.Fori(1, groups // 2) as t:
            pack(t, False)

    @block.gpsimd
    def _(pool):
        with pool.Fori(0, groups // 2) as t:
            for b in range(2):
                pool.wait_ge(ready, 2 * t + b + 1)
                pool.sem_inc(started, 1)
                for c in range(GRP):
                    pool.indirect_dma_start(table[:, :], bass.IndirectOffsetOnAxis(ap=at[b][:, c:c + 1], axis=0),
                                            rec[b][:, c, :], None, bounds_check=P * NC - 1,
                                            oob_is_err=False).then_inc(sent[b], 16)
        for b in range(2):
            pool.wait_ge(sent[b], GRP * 16 * (groups // 2))


def values(nc, engine_type, row, n, hi):
    _, got = nc.values_load_multi_w_load_instructions(
        row, engines=(engine_type,), min_val=0, max_val=hi,
        skip_runtime_bounds_check_because="the map is clamped to the last bucket when it is made")
    return got


def load_table(nc, g, name, pairs):
    with Phase(nc, name) as ph:
        loaded = ph.sem("loaded")
        with nc.Block() as block:
            @block.sync
            def _(sp):
                with nc.allow_non_contiguous_dma("small weights, once"):
                    for to, of in pairs:
                        sp.dma_start(to, of).then_inc(loaded, 16)
                sp.wait_ge(loaded, 16 * len(pairs))


def propagate(nc, g, name, rec, tmap, table, accs, messages=None):
    groups = NC // GRP
    with Phase(nc, name) as ph:
        at = [ph.sb(f"at{b}", [P, GRP], I32) for b in range(2)]
        rows = [ph.sb(f"rows{b}", [P, GRP, D]) for b in range(2)]
        oh = [ph.sb(f"oh{b}", [P, GRP, LO]) for b in range(2)]
        sums = [ph.ps(f"sums{b}", [LO, GRP, D]) for b in range(2)]
        at_ready, oh_ready, mm_done = ph.sem("at_ready"), ph.sem("oh_ready"), ph.sem("mm_done")
        added, steps_s = ph.sem("added"), ph.sem("steps")
        started = ph.sem("started")
        got = [ph.pool_dma_sem(f"got{b}") for b in range(2)]
        src = SourceSums(nc, g, ph, *messages) if messages else None
        with nc.Block() as block:
            @block.sync
            def _(sp):
                if src:
                    for b in range(2):
                        src.load(sp, 0, b, True)
                    with sp.Fori(1, groups // 2) as t:
                        for b in range(2):
                            src.load(sp, t, b, False)

            @block.scalar
            def _(act):
                def stage(t, first):
                    for b in range(2):
                        if not first:
                            act.wait_ge(got[b], GRP * 16 * t)
                        nc.scalar.copy(at[b][:, :], rec[:, bass.ds((2 * t + b) * GRP, GRP), SRC].bitcast(I32)
                                       ).then_inc(at_ready, 1)

                stage(0, True)
                with act.Fori(1, groups // 2) as t:
                    stage(t, False)

            @block.gpsimd
            def _(pool):
                def gather(t, first):
                    for b in range(2):
                        pool.wait_ge(at_ready, 2 * t + b + 1)
                        pool.sem_inc(started, 1)
                        if not first:
                            pool.wait_ge(mm_done, 2 * t + b - 1)
                            pool.sem_inc(started, 1)
                        for c in range(GRP):
                            pool.indirect_dma_start(rows[b][:, c, :], None, table[:, :],
                                                    bass.IndirectOffsetOnAxis(ap=at[b][:, c:c + 1], axis=0)
                                                    ).then_inc(got[b], 16)

                gather(0, True)
                with pool.Fori(1, groups // 2) as t:
                    gather(t, False)

            @block.vector
            def _(dve):
                steps = Steps(dve, steps_s)
                clear_tables(nc, steps, accs)
                if src:
                    src.clear(dve)

                def hot(t, b, first):
                    if not first:
                        dve.wait_ge(mm_done, 2 * t + b - 1)
                    nc.vector.tensor_tensor(oh[b][:, :, :], bc(g.iota[:, 0:LO], 1, [P, GRP, LO]),
                                            bc(rec[:, bass.ds((2 * t + b) * GRP, GRP), DLO], 2, [P, GRP, LO]),
                                            ALU.is_equal).then_inc(oh_ready, 1)

                def add(t, b):
                    dve.wait_ge(mm_done, 2 * t + b + 1)
                    add_tiles(nc, dve, steps_s, 1, 2 * t + b, tmap, accs,
                              [sums[b][:, c:c + 1, :] for c in range(GRP)], ALU.add)
                    dve.sem_inc(added, 1)

                def src_add(n, b):
                    if src:
                        src.add(dve, n, b)

                for b in range(2):
                    hot(0, b, True)
                    if src:
                        src.hot(dve, b, b, True)
                add(0, 0)
                src_add(0, 0)
                add(0, 1)
                with dve.Fori(1, groups // 2) as t:
                    for b in range(2):
                        hot(t, b, False)
                        if src:
                            src.hot(dve, 2 * t + b, b, False)
                        if b == 0:
                            src_add(2 * t - 1, 1)
                    add(t, 0)
                    src_add(2 * t, 0)
                    add(t, 1)
                src_add(groups - 1, 1)
                if src:
                    src.join(dve)
                join_tables(nc, dve, steps_s, accs)

            @block.tensor
            def _(pe):
                def product(t, first):
                    for b in range(2):
                        pe.wait_ge(oh_ready, 2 * t + b + 1)
                        pe.wait_ge(got[b], GRP * 16 * (t + 1))
                        if not first:
                            pe.wait_ge(added, 2 * t + b - 1)
                        for c in range(GRP):
                            last = nc.tensor.matmul(sums[b][:, c, :], oh[b][:, c, :], rows[b][:, c, :],
                                                    start=True, stop=True)
                        last.then_inc(mm_done, 1)
                        if src:
                            src.product(pe, t, b, first)

                product(0, True)
                with pe.Fori(1, groups // 2) as t:
                    product(t, False)


def layer_norm_relu(nc, g, name, x, h):
    wide = [LO, NT, D]
    with Phase(nc, name) as ph:
        sq = ph.sb("sq", wide)
        mean, var = ph.sb("mean", [LO, NT]), ph.sb("var", [LO, NT])
        steps_s, asked, rooted = ph.sem("steps"), ph.sem("asked"), ph.sem("rooted")
        with nc.Block() as block:
            @block.vector
            def _(dve):
                steps = Steps(dve, steps_s)
                steps(nc.vector.tensor_reduce(mean[:, :], x, AX, ALU.add))
                steps(nc.vector.tensor_scalar(mean[:, :], mean[:, :], 1.0 / D, None, ALU.mult))
                steps(nc.vector.tensor_tensor(h, x, bc(mean[:, :], 2, wide), ALU.subtract))
                steps(nc.vector.tensor_tensor(sq[:, :, :], h, h, ALU.mult))
                steps(nc.vector.tensor_reduce(var[:, :], sq[:, :, :], AX, ALU.add))
                nc.vector.tensor_scalar(var[:, :], var[:, :], 1.0 / D, 1.0e-5, ALU.mult, ALU.add).then_inc(asked, 1)
                dve.wait_ge(rooted, 1)
                steps(nc.vector.reciprocal(var[:, :], var[:, :]))
                steps(nc.vector.tensor_tensor(h, h, bc(var[:, :], 2, wide), ALU.mult))
                steps(nc.vector.tensor_scalar(h, h, 0.0, None, ALU.max))

            @block.scalar
            def _(act):
                act.wait_ge(asked, 1)
                nc.scalar.activation(var[:, :], var[:, :], ACT.Sqrt).then_inc(rooted, 1)


def out_scale(nc, g, degs):
    with Phase(nc, "outdeg") as ph:
        steps_s = ph.sem("steps")
        with nc.Block() as block:
            @block.vector
            def _(dve):
                steps = Steps(dve, steps_s)
                steps(nc.vector.tensor_scalar(g.rdeg[:, :], degs, 1.0, None, ALU.max))
                steps(nc.vector.reciprocal(g.rdeg[:, :], g.rdeg[:, :]))


def in_scale(nc, g, lam):
    with Phase(nc, "scales") as ph:
        steps_s, asked, rooted = ph.sem("steps"), ph.sem("asked"), ph.sem("rooted")
        with nc.Block() as block:
            @block.vector
            def _(dve):
                steps = Steps(dve, steps_s)
                steps(nc.vector.reciprocal(g.re[:, 0:1], lam))
                steps(nc.vector.tensor_scalar(g.re[:, 0:1], g.re[:, 0:1], 2.0, None, ALU.mult))
                steps(nc.vector.tensor_scalar(g.re[:, 1:2], g.re[:, 0:1], -1.0, None, ALU.mult))
                steps(nc.vector.tensor_scalar(g.re[:, 2:3], g.re[:, 0:1], 1.0, None, ALU.subtract))
                steps(nc.vector.tensor_scalar(g.re[:, 3:4], g.re[:, 0:1], -2.0, None, ALU.mult))
                steps(nc.vector.tensor_scalar(g.re[:, 4:5], g.re[:, 2:3], 2.0, None, ALU.mult))
                nc.vector.tensor_scalar(g.norm[:, :], g.degd[:, :], 1.0, None, ALU.max).then_inc(asked, 1)
                dve.wait_ge(rooted, 1)
                steps(nc.vector.reciprocal(g.norm[:, :], g.norm[:, :]))

            @block.scalar
            def _(act):
                act.wait_ge(asked, 1)
                nc.scalar.activation(g.norm[:, :], g.norm[:, :], ACT.Sqrt).then_inc(rooted, 1)


def store_scaled(nc, g, name, h, scale, table):
    shape = [LO, NT, h.shape[2]]
    with Phase(nc, name) as ph:
        out = ph.sb("out", shape)
        made, stored = ph.sem("made"), ph.sem("stored")
        with nc.Block() as block:
            @block.vector
            def _(dve):
                if scale is None:
                    nc.vector.tensor_copy(out[:, :, :], h).then_inc(made, 1)
                else:
                    nc.vector.tensor_tensor(out[:, :, :], h, bc(scale, 2, shape), ALU.mult).then_inc(made, 1)

            @block.sync
            def _(sp):
                sp.wait_ge(made, 1)
                sp.dma_start(table.rearrange("(p c) f -> p c f", p=LO), out[:, :, :]).then_inc(stored, 16)
                sp.wait_ge(stored, 16)


def chebyshev(nc, g, name, acc, cat, order):
    wide = [LO, NT, D]
    a, b = (1, 2) if order == 1 else (3, 4)
    before, to = cat[:, :, (order - 1) * D:order * D], cat[:, :, order * D:(order + 1) * D]
    with Phase(nc, name) as ph:
        steps_s = ph.sem("steps")
        with nc.Block() as block:
            @block.vector
            def _(dve):
                steps = Steps(dve, steps_s)
                steps(nc.vector.tensor_tensor(acc, acc, bc(g.norm[:, :], 2, wide), ALU.mult))
                steps(nc.vector.tensor_scalar(acc, acc, g.re[:, a:a + 1], None, ALU.mult))
                steps(nc.vector.scalar_tensor_tensor(out=to, in0=before, scalar=g.re[:, b:b + 1], in1=acc,
                                                     op0=ALU.mult, op1=ALU.add))
                if order == 2:
                    steps(nc.vector.tensor_tensor(to, to, cat[:, :, 0:D], ALU.subtract))


def node_linear(nc, g, name, x, K, w, bias, FO, y, relu=False, transposed=False):
    T = 4
    groups = NT // T
    assert groups % 2 == 1
    with Phase(nc, name) as ph:
        xs = [ph.sb(f"xs{b}", [K, T, LO] if transposed else [LO, T, K]) for b in range(2)]
        xt = xs if transposed else [ph.sb(f"xt{b}", [K, T, LO]) for b in range(2)]
        ys = ph.sb("ys", [LO, T, FO])
        pt, py = ([ph.ps(f"{s}{b}", shape) for b in range(2)] for s, shape in (("pt", [K, T, LO]),
                                                                               ("py", [LO, T, FO])))
        staged, turned, kept, made, steps_s, begun = (ph.sem(s) for s in ("staged", "turned", "kept", "made",
                                                                           "steps", "begun"))
        taken = staged if transposed else kept
        with nc.Block() as block:
            @block.vector
            def _(dve):
                def stage(n, b):
                    wait(dve, made if transposed else turned, n - 1)
                    nc.vector.tensor_copy(xs[b][:, :, :], x[:, bass.ds(n * T, T), :]).then_inc(staged, 1)

                def finish_group(n, b):
                    steps = Steps(dve, steps_s, 2 * n)
                    dve.wait_ge(made, n + 1)
                    if bias is None:
                        steps(nc.vector.tensor_copy(ys[:, :, :], py[b][:, :, :]))
                    else:
                        steps(nc.vector.tensor_tensor(ys[:, :, :], py[b][:, :, :], bc(bias, 1, [LO, T, FO]),
                                                      ALU.add))
                    steps(nc.vector.tensor_scalar(y[:, bass.ds(n * T, T), :], ys[:, :, :], 0.0 if relu else 1.0,
                                                  None, ALU.max if relu else ALU.mult))

                def group(n, b):
                    stage(n, b)
                    if is_group(n - 2):
                        finish_group(n - 2, b)

                for b in range(2):
                    group(b, b)
                with dve.Fori(1, groups // 2) as t:
                    for b in range(2):
                        group(2 * t + b, b)
                group(groups - 1, (groups - 1) % 2)
                finish_group(groups - 2, (groups - 2) % 2)
                finish_group(groups - 1, (groups - 1) % 2)

            @block.scalar
            def _(act):
                def keep(n, b):
                    act.wait_ge(turned, n + 1)
                    wait(act, made, n - 1)
                    nc.scalar.copy(xt[b][:, :, :], pt[b][:, :, :]).then_inc(kept, 1)

                if not transposed:
                    keep(0, 0)
                    keep(1, 1)
                    with act.Fori(1, groups // 2) as t:
                        for b in range(2):
                            keep(2 * t + b, b)
                    keep(groups - 1, (groups - 1) % 2)

            @block.tensor
            def _(pe):
                def turn(n, b):
                    if not transposed:
                        pe.wait_ge(staged, n + 1)
                        wait(pe, kept, n - 1)
                        pe.sem_inc(begun, 1)
                        for c in range(T):
                            last = nc.tensor.transpose(pt[b][:, c, :], xs[b][:, c, :], g.ident[0:LO, 0:LO])
                        last.then_inc(turned, 1)

                def product(n, b):
                    pe.wait_ge(taken, n + 1)
                    wait(pe, steps_s, 2 * (n - 1))
                    pe.sem_inc(begun, 1)
                    for c in range(T):
                        last = nc.tensor.matmul(py[b][:, c, :], xt[b][:, c, :], w, start=True, stop=True)
                    last.then_inc(made, 1)

                def group(n, b):
                    turn(n, b)
                    if is_group(n - 1):
                        product(n - 1, 1 - b)

                for b in range(2):
                    group(b, b)
                with pe.Fori(1, groups // 2) as t:
                    for b in range(2):
                        group(2 * t + b, b)
                group(groups - 1, (groups - 1) % 2)
                product(groups - 1, (groups - 1) % 2)


def scale_bias_elu(nc, g, name, y, F, scale, bias):
    wide = [LO, NT, F]
    with Phase(nc, name) as ph:
        low = ph.sb("low", wide)
        steps_s, asked, done = ph.sem("steps"), ph.sem("asked"), ph.sem("done")
        with nc.Block() as block:
            @block.vector
            def _(dve):
                steps = Steps(dve, steps_s)
                if scale is not None:
                    steps(nc.vector.tensor_tensor(y, y, bc(scale, 2, wide), ALU.mult))
                if bias is not None:
                    steps(nc.vector.tensor_tensor(y, y, bc(bias, 1, wide), ALU.add))
                nc.vector.tensor_scalar(low[:, :, :], y, 0.0, None, ALU.min).then_inc(asked, 1)
                dve.wait_ge(done, 1)
                steps(nc.vector.tensor_scalar(low[:, :, :], low[:, :, :], 1.0, None, ALU.subtract))
                steps(nc.vector.scalar_tensor_tensor(out=y, in0=y, scalar=0.0, in1=low[:, :, :],
                                                     op0=ALU.max, op1=ALU.add))

            @block.scalar
            def _(act):
                act.wait_ge(asked, 1)
                nc.scalar.activation(low[:, :, :], low[:, :, :], ACT.Exp).then_inc(done, 1)


def rounds(accs):
    return -(-GRP // len(accs))


def add_tiles(nc, dve, sem, base, group, tmap, accs, sums, op):
    tiles = values(nc, mybir.EngineType.DVE, tmap[0:1, bass.ds(group * GRP, GRP)], GRP, NT - 1)
    steps = Steps(dve, sem, group * rounds(accs) + base)
    for c in range(GRP):
        to = accs[c % len(accs)][:, bass.ds(tiles[c], 1), :]
        done = nc.vector.tensor_tensor(to, to, sums[c], op)
        if c % len(accs) == len(accs) - 1 or c == GRP - 1:
            steps(done)


def clear_tables(nc, steps, accs, number=0.0):
    for acc in accs:
        last = nc.vector.memset(acc, number)
    steps(last)


def join_tables(nc, dve, sem, accs, op=ALU.add):
    steps = Steps(dve, sem, NC // GRP * rounds(accs) + 1)
    for acc in accs[1:]:
        steps(nc.vector.tensor_tensor(accs[0], accs[0], acc, op))


def wait(engine, sem, value):
    if not isinstance(value, int) or value > 0:
        engine.wait_ge(sem, value)


def is_group(n):
    return not isinstance(n, int) or n >= 0


def buffer_of(t, b, back):
    return (b - back) % DEEP, t + 1 if b >= back else t


def attention_scores(nc, g, rec, tmap, table, fse, fdt, attn, lgs, mx, att2):
    groups = NC // GRP
    half = GRP // 2
    with Phase(nc, "att1") as ph:
        at = [ph.sb(f"at{b}", [P, GRP], I32) for b in range(DEEP)]
        rows = [ph.sb(f"rows{b}", [P, GRP, D + 4]) for b in range(DEEP)]
        oh = [ph.sb(f"oh{b}", [P, GRP, LO], BF16) for b in range(2)]
        ohT = [ph.sb(f"ohT{b}", [LO, GRP, P]) for b in range(2)]
        ident = ph.sb("ident", [P, P], BF16)
        sc = ph.sb("sc", [P, GRP, D])
        new = ph.sb("new", [P, GRP, 3])
        am = [ph.sb(f"am{b}", [P, GRP, LO]) for b in range(2)]
        red = ph.sb("red", [LO, GRP])
        mxs = [mx] + [ph.sb(f"mx{k}", [LO, NT, 1])[:, :, :] for k in range(3)]
        pt = [ph.ps(f"pt{b}", [LO, GRP, P], BF16) for b in range(2)]
        pa = [ph.ps(f"pa{h}", [LO, half, P]) for h in range(2)]
        px = [ph.ps(f"px{b}", [P, GRP, D + 4]) for b in range(2)]
        (at_ready, oh_ready, turned, kept, spread, masked, am_ready, am_turned, reduced, steps_s, steps_m, made) = (
            ph.sem(s) for s in ("at_ready", "oh_ready", "turned", "kept", "spread", "masked",
                                "am_ready", "am_turned", "reduced", "steps", "steps_m", "made"))
        ident_made = ph.sem("ident_made")
        started, begun = ph.sem("started"), ph.sem("begun")
        got = [ph.pool_dma_sem(f"got{b}") for b in range(DEEP)]
        stored = [ph.sem(f"stored{b}") for b in range(DEEP)]
        with nc.Block() as block:
            @block.scalar
            def _(act):
                def group(t, b):
                    n = DEEP * t + b
                    wait(act, got[b], GRP * 16 * t)
                    nc.scalar.copy(at[b][:, :], rec[:, bass.ds(n * GRP, GRP), SRC].bitcast(I32)).then_inc(at_ready, 1)
                    mask(n - 1, (b - 1) % 2)
                    act.wait_ge(turned, n + 1)
                    wait(act, spread, n - 1)
                    nc.scalar.copy(ohT[b % 2][:, :, :], pt[b % 2][:, :, :]).then_inc(kept, 1)

                def mask(n, b):
                    if is_group(n):
                        act.wait_ge(oh_ready, n + 1)
                        wait(act, am_turned, n - 1)
                        nc.scalar.activation(am[b][:, :, :], oh[b][:, :, :], ACT.Copy, bias=-LOW, scale=LOW
                                             ).then_inc(masked, 1)

                for b in range(DEEP):
                    group(0, b)
                with act.Fori(1, groups // DEEP) as t:
                    for b in range(DEEP):
                        group(t, b)
                mask(groups - 1, (groups - 1) % 2)

            @block.gpsimd
            def _(pool):
                def gather(t, b):
                    pool.wait_ge(at_ready, DEEP * t + b + 1)
                    pool.sem_inc(started, 1)
                    if is_group(t - 1):
                        pool.wait_ge(made, DEEP * t + b - DEEP + 1)
                        pool.sem_inc(started, 1)
                        pool.wait_ge(stored[b], 16 * t)
                        pool.sem_inc(started, 1)
                    for c in range(GRP):
                        pool.indirect_dma_start(rows[b][:, c, :], None, table[:, :],
                                                bass.IndirectOffsetOnAxis(ap=at[b][:, c:c + 1], axis=0)
                                                ).then_inc(got[b], 16)

                for b in range(DEEP):
                    gather(0, b)
                with pool.Fori(1, groups // DEEP) as t:
                    for b in range(DEEP):
                        gather(t, b)

            @block.sync
            def _(sp):
                to = fse.rearrange("(p j) f -> p j f", p=P)
                with sp.Fori(0, groups // DEEP) as t:
                    for b in range(DEEP):
                        sp.wait_ge(got[b], GRP * 16 * (t + 1))
                        sp.dma_start(to[:, bass.ds((DEEP * t + b) * GRP, GRP), :], rows[b][:, :, :]
                                     ).then_inc(stored[b], 16)
                for b in range(DEEP):
                    sp.wait_ge(stored[b], 16 * (groups // DEEP))

            @block.vector
            def _(dve):
                def hot(n, b):
                    wait(dve, masked, n - 1)
                    wait(dve, turned, n - 1)
                    nc.vector.tensor_tensor(oh[b % 2][:, :, :], bc(g.iota[:, 0:LO], 1, [P, GRP, LO]),
                                            bc(rec[:, bass.ds(n * GRP, GRP), DLO], 2, [P, GRP, LO]),
                                            ALU.is_equal).then_inc(oh_ready, 1)

                def score(n, b, uses):
                    slots = bass.ds(n * GRP, GRP)
                    steps = Steps(dve, steps_s, 5 * n)
                    lg = lgs[:, slots]
                    dve.wait_ge(got[b], GRP * 16 * uses)
                    dve.wait_ge(spread, n + 1)
                    nc.vector.tensor_tensor(new[:, :, :], rec[:, slots, ATT:ATT + 3], px[b % 2][:, :, D:D + 3],
                                            ALU.add)
                    steps(nc.vector.tensor_tensor(sc[:, :, :], px[b % 2][:, :, 0:D], rows[b][:, :, 0:D], ALU.add))
                    nc.vector.tensor_tensor(new[:, :, :], new[:, :, :], rows[b][:, :, D:D + 3], ALU.subtract)
                    steps(nc.vector.scalar_tensor_tensor(out=sc[:, :, :], in0=sc[:, :, :], scalar=0.2,
                                                         in1=sc[:, :, :], op0=ALU.mult, op1=ALU.max))
                    nc.vector.tensor_scalar(att2[:, slots, :], new[:, :, :], 0.0, 1.0, ALU.max, ALU.min)
                    steps(nc.vector.tensor_tensor(sc[:, :, :], sc[:, :, :], bc(attn, 1, [P, GRP, D]), ALU.mult))
                    dve.sem_inc(made, 1)
                    steps(nc.vector.tensor_reduce(lg, sc[:, :, :], AX, ALU.add))
                    dve.wait_ge(masked, n + 1)
                    steps(nc.vector.tensor_tensor(am[b % 2][:, :, :], am[b % 2][:, :, :],
                                                  bc(lg, 2, [P, GRP, LO]), ALU.add))
                    dve.sem_inc(am_ready, 1)

                def highest(n):
                    dve.wait_ge(am_turned, n + 1)
                    for h in range(2):
                        last = nc.vector.tensor_reduce(red[:, h * half:(h + 1) * half], pa[h][:, :, :], AX, ALU.max)
                    last.then_inc(reduced, 1)
                    dve.wait_ge(reduced, n + 1)
                    add_tiles(nc, dve, steps_m, 1, n, tmap, mxs, [red[:, c:c + 1].unsqueeze(2) for c in range(GRP)],
                              ALU.max)

                def group(t, b):
                    n = DEEP * t + b
                    if is_group(n - 2):
                        highest(n - 2)
                    if is_group(n - 1):
                        score(n - 1, *buffer_of(t, b, 1))
                    if not (isinstance(n, int) and n == groups - 1):
                        hot(n + 1, b + 1)

                nc.vector.tensor_copy(ident[:, :], g.ident[:, :]).then_inc(ident_made, 1)
                steps = Steps(dve, steps_m)
                clear_tables(nc, steps, mxs, -LOW)
                hot(0, 0)
                for b in range(DEEP):
                    group(0, b)
                with dve.Fori(1, groups // DEEP - 1) as t:
                    for b in range(DEEP):
                        group(t, b)
                for b in range(DEEP):
                    group(groups // DEEP - 1, b)
                highest(groups - 2)
                score(groups - 1, DEEP - 1, groups // DEEP)
                highest(groups - 1)
                join_tables(nc, dve, steps_m, mxs, ALU.max)

            @block.tensor
            def _(pe):
                def turn(n, b):
                    pe.wait_ge(oh_ready, n + 1)
                    wait(pe, kept, n - 1)
                    pe.sem_inc(begun, 1)
                    for c in range(GRP):
                        last = nc.tensor.transpose(pt[b][:, c, :], oh[b][:, c, :], ident[:, :])
                    last.then_inc(turned, 1)

                def spread_rows(n, b):
                    tiles = values(nc, mybir.EngineType.PE, tmap[0:1, bass.ds(n * GRP, GRP)], GRP, NT - 1)
                    pe.wait_ge(kept, n + 1)
                    wait(pe, am_ready, n - 1)
                    for c in range(GRP):
                        last = nc.tensor.matmul(px[b][:, c, :], ohT[b][:, c, :], fdt[:, bass.ds(tiles[c], 1), :],
                                                start=True, stop=True)
                    last.then_inc(spread, 1)

                def turn_scores(n, b):
                    pe.wait_ge(am_ready, n + 1)
                    wait(pe, reduced, n)
                    for c in range(GRP):
                        last = nc.tensor.transpose(pa[c // half][:, c % half, :], am[b][:, c, :], g.ident[:, :])
                    last.then_inc(am_turned, 1)

                def group(t, b):
                    n = DEEP * t + b
                    if is_group(n - 1):
                        spread_rows(n - 1, (b - 1) % 2)
                    if is_group(n - 2):
                        turn_scores(n - 2, b % 2)
                    turn(n, b % 2)

                pe.wait_ge(ident_made, 1)
                for b in range(DEEP):
                    group(0, b)
                with pe.Fori(1, groups // DEEP) as t:
                    for b in range(DEEP):
                        group(t, b)
                spread_rows(groups - 1, 1)
                turn_scores(groups - 2, 0)
                turn_scores(groups - 1, 1)


def attention_sums(nc, g, rec, tmap, fse, lgs, mx, accs):
    groups = NC // GRP
    half = GRP // 2
    W = D + 1
    with Phase(nc, "att2") as ph:
        rows = [ph.sb(f"rows{b}", [P, GRP, D + 4]) for b in range(DEEP)]
        oh = [ph.sb(f"oh{b}", [P, GRP, LO]) for b in range(DEEP)]
        ohT = [ph.sb(f"ohT{b}", [LO, GRP, P], BF16) for b in range(2)]
        parts, left = ph.sb("parts", [LO, NT, 3], BF16), ph.sb("left", [LO, NT, 1])
        top = ph.sb("top", [P, GRP])
        ex = [ph.sb(f"ex{b}", [P, GRP]) for b in range(2)]
        msg = [ph.sb(f"msg{b}", [P, GRP, W]) for b in range(2)]
        pt = [ph.ps(f"pt{h}", [LO, half, P]) for h in range(2)]
        pm = [ph.ps(f"pm{b}", [P, GRP, 3]) for b in range(2)]
        sums = [ph.ps(f"sums{b}", [LO, GRP, W]) for b in range(2)]
        oh_ready, turned, kept, m_ready, less, exped, msg_ready, mm_done, added, steps_s, steps_a = (
            ph.sem(s) for s in ("oh_ready", "turned", "kept", "m_ready", "less", "exped", "msg_ready", "mm_done",
                                "added", "steps", "steps_a"))
        split = ph.sem("split")
        loaded = [ph.sem(f"loaded{b}") for b in range(DEEP)]
        with nc.Block() as block:
            @block.sync
            def _(sp):
                of = fse.rearrange("(p j) f -> p j f", p=P)

                def load(t, b):
                    wait(sp, msg_ready, DEEP * (t - 1) + b + 1)
                    sp.dma_start(rows[b][:, :, :], of[:, bass.ds((DEEP * t + b) * GRP, GRP), :]
                                 ).then_inc(loaded[b], 16)

                for b in range(DEEP):
                    load(0, b)
                with sp.Fori(1, groups // DEEP) as t:
                    for b in range(DEEP):
                        load(t, b)

            @block.scalar
            def _(act):
                def keep(n, b):
                    act.wait_ge(turned, n + 1)
                    wait(act, m_ready, n - 1)
                    for h in range(2):
                        last = nc.scalar.copy(ohT[b][:, h * half:(h + 1) * half, :], pt[h][:, :, :])
                    last.then_inc(kept, 1)

                def exponent(n, b):
                    act.wait_ge(less, n + 1)
                    nc.scalar.activation(ex[b][:, :], ex[b][:, :], ACT.Exp).then_inc(exped, 1)

                def group(n, b):
                    if is_group(n - 1):
                        exponent(n - 1, (b - 1) % 2)
                    keep(n, b % 2)

                for b in range(DEEP):
                    group(b, b)
                with act.Fori(1, groups // DEEP) as t:
                    for b in range(DEEP):
                        group(DEEP * t + b, b)
                exponent(groups - 1, 1)

            @block.vector
            def _(dve):
                def hot(n, b):
                    wait(dve, mm_done, n - DEEP + 1)
                    nc.vector.tensor_tensor(oh[b][:, :, :], bc(g.iota[:, 0:LO], 1, [P, GRP, LO]),
                                            bc(rec[:, bass.ds(n * GRP, GRP), DLO], 2, [P, GRP, LO]),
                                            ALU.is_equal).then_inc(oh_ready, 1)

                def lessen(n, b):
                    steps = Steps(dve, steps_s, 2 * n)
                    dve.wait_ge(m_ready, n + 1)
                    steps(nc.vector.tensor_reduce(top[:, :], pm[b][:, :, :], AX, ALU.add))
                    steps(nc.vector.tensor_tensor(ex[b][:, :], lgs[:, bass.ds(n * GRP, GRP)], top[:, :],
                                                  ALU.subtract))
                    nc.vector.tensor_scalar(ex[b][:, :], ex[b][:, :], 0.0, None, ALU.min).then_inc(less, 1)

                def message(n, b, uses):
                    dve.wait_ge(exped, n + 1)
                    wait(dve, mm_done, n - 1)
                    dve.wait_ge(loaded[b], 16 * uses)
                    nc.vector.tensor_tensor(msg[b % 2][:, :, 0:D], rows[b][:, :, 0:D],
                                            bc(ex[b % 2][:, :], 2, [P, GRP, D]), ALU.mult)
                    nc.vector.tensor_copy(msg[b % 2][:, :, D], ex[b % 2][:, :]).then_inc(msg_ready, 1)

                def add(n, b):
                    dve.wait_ge(mm_done, n + 1)
                    add_tiles(nc, dve, steps_a, 1, n, tmap, accs, [sums[b][:, c:c + 1, :] for c in range(GRP)],
                              ALU.add)
                    dve.sem_inc(added, 1)

                def group(t, b):
                    n = DEEP * t + b
                    if is_group(n - 1):
                        lessen(n - 1, (b - 1) % 2)
                    if is_group(n - 1):
                        message(n - 1, *buffer_of(t, b, 1))
                    if not (isinstance(n, int) and n == groups - 1):
                        hot(n + 1, (b + 1) % DEEP)
                    if is_group(n - 2):
                        add(n - 2, b % 2)

                steps = Steps(dve, split)
                steps(nc.vector.tensor_copy(parts[:, :, 0], mx[:, :, 0]))
                steps(nc.vector.tensor_tensor(left[:, :, 0], mx[:, :, 0], parts[:, :, 0], ALU.subtract))
                steps(nc.vector.tensor_copy(parts[:, :, 1], left[:, :, 0]))
                steps(nc.vector.tensor_tensor(left[:, :, 0], left[:, :, 0], parts[:, :, 1], ALU.subtract))
                steps(nc.vector.tensor_copy(parts[:, :, 2], left[:, :, 0]))
                steps = Steps(dve, steps_a)
                clear_tables(nc, steps, accs)
                hot(0, 0)
                for b in range(DEEP):
                    group(0, b)
                with dve.Fori(1, groups // DEEP - 1) as t:
                    for b in range(DEEP):
                        group(t, b)
                for b in range(DEEP):
                    group(groups // DEEP - 1, b)
                lessen(groups - 1, 1)
                message(groups - 1, DEEP - 1, groups // DEEP)
                add(groups - 2, 0)
                add(groups - 1, 1)
                join_tables(nc, dve, steps_a, accs)

            @block.tensor
            def _(pe):
                def turn(n, b):
                    pe.wait_ge(oh_ready, n + 1)
                    wait(pe, kept, n)
                    for c in range(GRP):
                        last = nc.tensor.transpose(pt[c // half][:, c % half, :], oh[b][:, c, :], g.ident[:, :])
                    last.then_inc(turned, 1)

                def maxima(n, b):
                    tiles = values(nc, mybir.EngineType.PE, tmap[0:1, bass.ds(n * GRP, GRP)], GRP, NT - 1)
                    pe.wait_ge(kept, n + 1)
                    wait(pe, less, n - 1)
                    for c in range(GRP):
                        last = nc.tensor.matmul(pm[b][:, c, :], ohT[b][:, c, :], parts[:, bass.ds(tiles[c], 1), :],
                                                start=True, stop=True)
                    last.then_inc(m_ready, 1)

                def total(n, b):
                    pe.wait_ge(msg_ready, n + 1)
                    wait(pe, added, n - 1)
                    for c in range(GRP):
                        last = nc.tensor.matmul(sums[b % 2][:, c, :], oh[b][:, c, :], msg[b % 2][:, c, :],
                                                start=True, stop=True)
                    last.then_inc(mm_done, 1)

                def group(n, b):
                    turn(n, b)
                    if is_group(n - 1):
                        total(n - 1, (b - 1) % DEEP)
                    maxima(n, b % 2)

                pe.wait_ge(split, 5)
                for b in range(DEEP):
                    group(b, b)
                with pe.Fori(1, groups // DEEP) as t:
                    for b in range(DEEP):
                        group(DEEP * t + b, b)
                total(groups - 1, DEEP - 1)


def attention_end(nc, g, acc, bias, x):
    with Phase(nc, "att3") as ph:
        den = ph.sb("den", [LO, NT])
        one = ph.sb("one", [LO, NT])
        steps_s = ph.sem("steps")
        wide = [LO, NT, D]
        with nc.Block() as block:
            @block.vector
            def _(dve):
                steps = Steps(dve, steps_s)
                steps(nc.vector.tensor_scalar(one[:, :], acc[:, :, D], 0.0, None, ALU.is_equal))
                steps(nc.vector.tensor_tensor(den[:, :], acc[:, :, D], one[:, :], ALU.add))
                steps(nc.vector.reciprocal(den[:, :], den[:, :]))
                steps(nc.vector.tensor_tensor(acc[:, :, 0:D], acc[:, :, 0:D], bc(den[:, :], 2, wide), ALU.mult))
                steps(nc.vector.tensor_tensor(acc[:, :, 0:D], acc[:, :, 0:D], bc(bias, 1, wide), ALU.add))
                steps(nc.vector.tensor_tensor(x, x, acc[:, :, 0:D], ALU.add))


def cell_of(nc, steps, pos, i0, frac):
    steps(nc.vector.tensor_scalar(frac, pos, 1.0, None, ALU.is_ge))
    steps(nc.vector.scalar_tensor_tensor(out=i0, in0=pos, scalar=2.0, in1=frac, op0=ALU.is_ge, op1=ALU.add))
    steps(nc.vector.scalar_tensor_tensor(out=i0, in0=pos, scalar=3.0, in1=i0, op0=ALU.is_ge, op1=ALU.add))
    steps(nc.vector.tensor_tensor(frac, pos, i0, ALU.subtract))


def basis_sums(nc, g, ph, block, rec, tmap, acc):
    groups = NC // GRP
    half = GRP // 2
    k5 = ph.sb("k5", [P, 2, KS])
    pos, cell, frac, rest = (ph.sb(n, [P, 2 * GRP, 3]) for n in ("pos", "cell", "frac", "rest"))
    left, hat = (ph.sb(n, [P, 2 * GRP * 3, KS]) for n in ("left", "hat"))
    h01 = ph.sb("h01", [P, GRP, KS, KS])
    bas = [ph.sb(f"bas{b}", [P, GRP, K3 + 1]) for b in range(2)]
    oh = [ph.sb(f"oh{b}", [P, GRP, LO]) for b in range(2)]
    sums = [[ph.ps(f"sums{b}{h}", [K3 + 1, half, LO]) for h in range(2)] for b in range(2)]
    ready, mm_done, added, steps_s, steps_a = (ph.sem(s) for s in
                                               ("ready", "mm_done", "added", "steps", "steps_a"))
    HATS, BUILD = 9, 2
    PAIR = HATS + 2 * BUILD

    @block.vector
    def _(dve):
        def hats_of(t):
            at = bass.ds(2 * t * GRP, 2 * GRP)
            steps = Steps(dve, steps_s, t * PAIR + 1)
            steps(nc.vector.tensor_scalar(pos[:, :, :], rec[:, at, SATT:SATT + 3], float(KS - 1), None,
                                          ALU.mult))
            cell_of(nc, steps, pos[:, :, :], cell[:, :, :], frac[:, :, :])
            steps(nc.vector.tensor_scalar(rest[:, :, :], frac[:, :, :], -1.0, 1.0, ALU.mult, ALU.add))
            flat = [a[:, :, :].rearrange("p c d -> p (c d)") for a in (cell, frac, rest)]
            shape = [P, 2 * GRP * 3, KS]
            nc.vector.tensor_tensor(left[:, :, :], bc(k5[:, 0, :], 1, shape), bc(flat[0], 2, shape),
                                    ALU.is_equal)
            steps(nc.vector.tensor_tensor(hat[:, :, :], bc(k5[:, 1, :], 1, shape), bc(flat[0], 2, shape),
                                          ALU.is_equal))
            nc.vector.tensor_tensor(left[:, :, :], left[:, :, :], bc(flat[2], 2, shape), ALU.mult)
            steps(nc.vector.tensor_tensor(hat[:, :, :], hat[:, :, :], bc(flat[1], 2, shape), ALU.mult))
            steps(nc.vector.tensor_tensor(hat[:, :, :], hat[:, :, :], left[:, :, :], ALU.add))
            assert steps.n == HATS

        def build(t, b, first):
            n = 2 * t + b
            at = bass.ds(n * GRP, GRP)
            steps = Steps(dve, steps_s, t * PAIR + HATS + b * BUILD + 1)
            hats = hat[:, b * GRP * 3:(b + 1) * GRP * 3, :].rearrange("p (c d) k -> p c d k", d=3)
            steps(nc.vector.tensor_tensor(h01[:, :, :, :],
                                          bc(hats[:, :, 0, :], 3, [P, GRP, KS, KS]),
                                          bc(hats[:, :, 1, :], 2, [P, GRP, KS, KS]), ALU.mult))
            if not first:
                dve.wait_ge(mm_done, n - 1)
            big = [P, GRP, KS * KS, KS]
            steps(nc.vector.tensor_tensor(
                bas[b][:, :, 0:K3].rearrange("p c (a k) -> p c a k", k=KS),
                bc(h01[:, :, :, :].rearrange("p c a k -> p c (a k)"), 3, big),
                bc(hats[:, :, 2, :], 2, big), ALU.mult))
            nc.vector.tensor_tensor(oh[b][:, :, :], bc(g.iota[:, 0:LO], 1, [P, GRP, LO]),
                                    bc(rec[:, at, SLO], 2, [P, GRP, LO]), ALU.is_equal).then_inc(ready, 1)
            assert steps.n == BUILD

        def add(n, b):
            dve.wait_ge(mm_done, n + 1)
            add_tiles(nc, dve, steps_a, 1, n, tmap, [acc],
                      [sums[b][c // half][:, c % half:c % half + 1, :] for c in range(GRP)], ALU.add)
            dve.sem_inc(added, 1)

        steps = Steps(dve, steps_s)
        for b in range(2):
            nc.vector.memset(bas[b][:, :, K3:K3 + 1], 1.0)
        nc.vector.tensor_scalar(k5[:, 1, :], g.iota[:, 0:KS], 1.0, None, ALU.subtract)
        steps(nc.vector.tensor_copy(k5[:, 0, :], g.iota[:, 0:KS]))
        steps = Steps(dve, steps_a)
        steps(nc.vector.memset(acc, 0.0))
        hats_of(0)
        build(0, 0, True)
        build(0, 1, True)
        add(0, 0)
        with dve.Fori(1, groups // 2) as t:
            hats_of(t)
            for b in range(2):
                build(t, b, False)
                add(2 * t + b - 1, 1 - b)
        add(groups - 1, 1)

    @block.tensor
    def _(pe):
        def group(n, b, first):
            pe.wait_ge(ready, n + 1)
            if not first:
                pe.wait_ge(added, n - 1)
            for c in range(GRP):
                last = nc.tensor.matmul(sums[b][c // half][:, c % half, :], bas[b][:, c, :],
                                        oh[b][:, c, :], start=True, stop=True)
            last.then_inc(mm_done, 1)

        group(0, 0, True)
        group(1, 1, True)
        with pe.Fori(1, groups // 2) as t:
            for b in range(2):
                group(2 * t + b, b, False)


def spline_cells(nc, g, name, att, dlo, key, frac):
    with Phase(nc, name) as ph:
        pos = ph.sb("pos", [P, NC, 3])
        i0 = ph.sb("i0", [P, NC, 3])
        steps_s = ph.sem("steps")
        with nc.Block() as block:
            @block.vector
            def _(dve):
                steps = Steps(dve, steps_s)
                steps(nc.vector.tensor_scalar(pos[:, :, :], att, float(KS - 1), None, ALU.mult))
                cell_of(nc, steps, pos[:, :, :], i0[:, :, :], frac)
                if key is None:
                    return
                steps(nc.vector.scalar_tensor_tensor(out=key, in0=i0[:, :, 0], scalar=4.0, in1=i0[:, :, 1],
                                                     op0=ALU.mult, op1=ALU.add))
                steps(nc.vector.scalar_tensor_tensor(out=key, in0=key, scalar=4.0, in1=i0[:, :, 2],
                                                     op0=ALU.mult, op1=ALU.add))
                steps(nc.vector.tensor_scalar(pos[:, :, 0], dlo, 0.0, None, ALU.is_ge))
                steps(nc.vector.scalar_tensor_tensor(out=key, in0=key, scalar=1.0, in1=pos[:, :, 0],
                                                     op0=ALU.add, op1=ALU.mult))
                steps(nc.vector.tensor_scalar(key, key, 1.0, None, ALU.subtract))


def cell_offsets(nc, ph_tmp, width):
    q, i0, i1 = ph_tmp

    def convert(steps, bm):
        steps(nc.vector.tensor_scalar(i0[:, :], bm[:, :], 1.0 / 16, -0.5 + 0.5 / 16, ALU.mult, ALU.add))
        steps(nc.vector.tensor_scalar(i0[:, :], i0[:, :], RND, RND, ALU.add, ALU.subtract))
        steps(nc.vector.scalar_tensor_tensor(out=q[:, :], in0=i0[:, :], scalar=-16.0, in1=bm[:, :],
                                             op0=ALU.mult, op1=ALU.add))
        steps(nc.vector.tensor_scalar(i1[:, :], q[:, :], 1.0 / 4, -0.5 + 0.5 / 4, ALU.mult, ALU.add))
        steps(nc.vector.tensor_scalar(i1[:, :], i1[:, :], RND, RND, ALU.add, ALU.subtract))
        steps(nc.vector.scalar_tensor_tensor(out=bm[:, :], in0=i0[:, :], scalar=9.0, in1=bm[:, :],
                                             op0=ALU.mult, op1=ALU.add))
        steps(nc.vector.tensor_tensor(bm[:, :], bm[:, :], i1[:, :], ALU.add))
        steps(nc.vector.tensor_scalar(bm[:, :], bm[:, :], float(width), None, ALU.mult))

    return convert


def fill_rows(nc, ph, block, tables):
    filled, cleared, marked = ph.sem("filled"), ph.sem("cleared"), ph.sem("marked")
    last_word = ph.sb("last_word", [P, 1])
    fills = [ph.sb(f"fill{n}", [P, rows // pieces, table.shape[1]])
             for n, (table, rows, pieces, marks) in enumerate(tables)]

    @block.gpsimd
    def _(pool):
        for fill in fills:
            last = nc.gpsimd.memset(fill[:, :, :], 0.0)
        last.then_inc(cleared, 1)
        pool.wait_ge(cleared, 1)
        for fill, (table, rows, pieces, marks) in zip(fills, tables):
            for word, number in marks:
                to = fill[:, :, word:word + 1]
                nc.gpsimd.memset(to.bitcast(I32) if isinstance(number, int) else to, number)
        nc.gpsimd.memset(last_word[:, :], 0.0).then_inc(marked, 1)

    @block.sync
    def _(sp):
        sp.wait_ge(marked, 1)
        for fill, (table, rows, pieces, marks) in zip(fills, tables):
            n = rows // pieces
            to = table.rearrange("(p j) w -> p j w", p=P)
            for q in range(pieces):
                sp.dma_start(to[:, q * n:(q + 1) * n, :], fill[:, :, :]).then_inc(filled, 16)
        sp.wait_ge(filled, 16 * sum(pieces for _, _, pieces, _ in tables))


def to_cells(nc, g, name, rec, tmap, h, F, frac, rowc, table, degree=None):
    groups = NC // GRP
    W = F + 4
    with Phase(nc, name) as ph:
        at = [ph.sb(f"at{b}", [P, GRP], I32) for b in range(2)]
        pay = [ph.sb(f"pay{b}", [P, GRP, W]) for b in range(2)]
        oh = [ph.sb(f"oh{b}", [P, GRP, LO], BF16) for b in range(2)]
        ident = ph.sb("ident", [P, P], BF16)
        ohT = [ph.sb(f"ohT{b}", [LO, GRP, P]) for b in range(2)]
        pt = [ph.ps(f"pt{b}", [LO, GRP, P], BF16) for b in range(2)]
        px = [ph.ps(f"px{b}", [P, GRP, F]) for b in range(2)]
        oh_ready, turned, kept, spread, ready = (ph.sem(s) for s in ("oh_ready", "turned", "kept", "spread", "ready"))
        started = ph.sem("started")
        if degree is not None:
            one = ph.sb("one", [P, 1], BF16)
            degrees = [degree.unsqueeze(2)] + [ph.sb(f"degree{k}", [LO, NT, 1])[:, :, :] for k in range(3)]
            pc = [ph.ps(f"pc{b}", [LO, GRP]) for b in range(2)]
            counted, tallied, steps_c = (ph.sem(s) for s in ("counted", "tallied", "steps_c"))
        sent = [ph.pool_dma_sem(f"sent{b}") for b in range(2)]
        with nc.Block() as block:
            @block.scalar
            def _(act):
                def group(n, b, first):
                    act.wait_ge(turned, n + 1)
                    if not first:
                        act.wait_ge(spread, n - 1)
                    nc.scalar.copy(ohT[b][:, :, :], pt[b][:, :, :]).then_inc(kept, 1)

                group(0, 0, True)
                group(1, 1, True)
                with act.Fori(1, groups // 2) as t:
                    for b in range(2):
                        group(2 * t + b, b, False)

            @block.vector
            def _(dve):
                def hot(n, b, first):
                    if not first:
                        dve.wait_ge(turned, n - 1)
                        if degree is not None:
                            dve.wait_ge(counted, n - 1)
                    nc.vector.tensor_tensor(oh[b][:, :, :], bc(g.iota[:, 0:LO], 1, [P, GRP, LO]),
                                            bc(rec[:, bass.ds(n * GRP, GRP), DLO], 2, [P, GRP, LO]),
                                            ALU.is_equal).then_inc(oh_ready, 1)

                def pack(t, b, first):
                    n = 2 * t + b
                    slots = bass.ds(n * GRP, GRP)
                    if not first:
                        dve.wait_ge(sent[b], GRP * 16 * t)
                    nc.vector.tensor_copy(pay[b][:, :, F:F + 3], frac[:, slots, :])
                    nc.vector.tensor_copy(pay[b][:, :, F + 3].bitcast(I32), rec[:, slots, ROWS].bitcast(I32))
                    nc.vector.tensor_copy(at[b][:, :], rowc(slots))
                    dve.wait_ge(spread, n + 1)
                    nc.vector.tensor_copy(pay[b][:, :, 0:F], px[b][:, :, :]).then_inc(ready, 1)
                    if degree is not None:
                        dve.wait_ge(counted, n + 1)
                        add_tiles(nc, dve, steps_c, 1, n, tmap, degrees,
                                  [pc[b][:, c:c + 1].unsqueeze(2) for c in range(GRP)], ALU.add)
                        dve.sem_inc(tallied, 1)

                nc.vector.tensor_copy(ident[:, :], g.ident[:, :])
                if degree is not None:
                    nc.vector.memset(one[:, :], 1.0)
                    clear_tables(nc, Steps(dve, steps_c), degrees)
                hot(0, 0, True)
                hot(1, 1, True)
                pack(0, 0, True)
                pack(0, 1, True)
                with dve.Fori(1, groups // 2) as t:
                    hot(2 * t, 0, False)
                    hot(2 * t + 1, 1, False)
                    pack(t, 0, False)
                    pack(t, 1, False)
                if degree is not None:
                    join_tables(nc, dve, steps_c, degrees)

            @block.tensor
            def _(pe):
                def turn(n, b, first):
                    pe.wait_ge(oh_ready, n + 1)
                    if not first:
                        pe.wait_ge(kept, n - 1)
                    pe.sem_inc(started, 1)
                    for c in range(GRP):
                        last = nc.tensor.transpose(pt[b][:, c, :], oh[b][:, c, :], ident[:, :])
                    last.then_inc(turned, 1)
                    if degree is not None:
                        if not first:
                            pe.wait_ge(tallied, n - 1)
                            pe.sem_inc(started, 1)
                        for c in range(GRP):
                            last = nc.tensor.matmul(pc[b][:, c:c + 1], oh[b][:, c, :], one[:, :],
                                                    start=True, stop=True)
                        last.then_inc(counted, 1)

                def spread_rows(n, b, first):
                    tiles = values(nc, mybir.EngineType.PE, tmap[0:1, bass.ds(n * GRP, GRP)], GRP, NT - 1)
                    pe.wait_ge(kept, n + 1)
                    if not first:
                        pe.wait_ge(ready, n - 1)
                    for c in range(GRP):
                        last = nc.tensor.matmul(px[b][:, c, :], ohT[b][:, c, :], h[:, bass.ds(tiles[c], 1), :],
                                                start=True, stop=True)
                    last.then_inc(spread, 1)

                turn(0, 0, True)
                turn(1, 1, True)
                spread_rows(0, 0, True)
                spread_rows(1, 1, True)
                with pe.Fori(1, groups // 2) as t:
                    turn(2 * t, 0, False)
                    turn(2 * t + 1, 1, False)
                    spread_rows(2 * t, 0, False)
                    spread_rows(2 * t + 1, 1, False)

            @block.gpsimd
            def _(pool):
                with pool.Fori(0, groups // 2) as t:
                    for b in range(2):
                        pool.wait_ge(ready, 2 * t + b + 1)
                        pool.sem_inc(started, 1)
                        for c in range(GRP):
                            pool.indirect_dma_start(table[:, :],
                                                    bass.IndirectOffsetOnAxis(ap=at[b][:, c:c + 1], axis=0),
                                                    pay[b][:, c, :], None, bounds_check=P * NCC - 1,
                                                    oob_is_err=False).then_inc(sent[b], 16)
                for b in range(2):
                    pool.wait_ge(sent[b], GRP * 16 * (groups // 2))


def cell_messages(nc, g, name, table, cmap, w, F, FO, msgs):
    groups = NCC // GRP
    half = GRP // 2
    W = F + 4
    S = P // F
    Q = 8 * FO // S
    reach = KS * FO if S == 4 else 2 * KS * FO
    SCALE, WEIGH = (3, 3) if S == 2 else (4, 2)
    with Phase(nc, name) as ph:
        pay = [ph.sb(f"pay{b}", [P, GRP, W]) for b in range(DEEP)]
        at = [ph.sb(f"at{b}", [P, GRP], I32) for b in range(2)]
        rest = [ph.sb(f"rest{b}", [P, GRP, 3]) for b in range(2)]
        fac = ph.sb("fac", [P, GRP, S])
        hs = [ph.sb(f"hs{b}", [P, GRP, S * F]) for b in range(2)]
        hT = [ph.sb(f"hT{b}", [P, GRP, P]) for b in range(2)]
        v = ph.sb("v", [P, GRP, 2 * FO])
        v2 = ph.sb("v2", [P, GRP, 2 * FO])
        out = [ph.sb(f"out{b}", [P, GRP, FO]) for b in range(2)]
        o2 = ph.sb("o2", [P, GRP, FO])
        pt = [ph.ps(f"pt{k}", [P, half, P]) for k in range(2)]
        pp = [ph.ps(f"pp{k}", [P, half, Q]) for k in range(2)]
        scaled, turned, kept, mm_done, used, ready, steps_s, steps_w = (
            ph.sem(s) for s in ("scaled", "turned", "kept", "mm_done", "used", "ready", "steps", "steps_w"))
        started, begun = ph.sem("started"), ph.sem("begun")
        loaded = [ph.sem(f"loaded{b}") for b in range(DEEP)]
        sent = [ph.pool_dma_sem(f"sent{b}") for b in range(2)]
        with nc.Block() as block:
            @block.sync
            def _(sp):
                of = table.rearrange("(p j) w -> p j w", p=P)

                def load(t, b):
                    wait(sp, ready, DEEP * (t - 1) + b + 1)
                    sp.dma_start(pay[b][:, :, :], of[:, bass.ds((DEEP * t + b) * GRP, GRP), :]
                                 ).then_inc(loaded[b], 16)

                for b in range(DEEP):
                    load(0, b)
                with sp.Fori(1, groups // DEEP) as t:
                    for b in range(DEEP):
                        load(t, b)

            @block.tensor
            def _(pe):
                def turn(n, b):
                    pe.wait_ge(scaled, n + 1)
                    wait(pe, kept, n)
                    pe.sem_inc(begun, 1)
                    for c in range(GRP):
                        last = nc.tensor.transpose(pt[c // half][:, c % half, :], hs[b][:, c, :], g.ident[:, :])
                    last.then_inc(turned, 1)

                def product(n, b):
                    offs = values(nc, mybir.EngineType.PE, cmap[0:1, bass.ds(n * GRP, GRP)], GRP, 3 * 31 * FO)
                    pe.wait_ge(kept, n + 1)
                    for c in range(GRP):
                        k = c // half
                        if c % half == 0:
                            wait(pe, used, 2 * (n - 1) + k + 1)
                        if S == 2:
                            win = w[:, bass.ds(offs[c], reach)].rearrange("p (b y) -> p b y", b=2)[:, :, 0:2 * FO]
                            to = pp[k][:, c % half, :].rearrange("p (b y) -> p b y", b=2)
                        else:
                            win, to = w[:, bass.ds(offs[c], 2 * FO)], pp[k][:, c % half, :]
                        last = nc.tensor.matmul(to, hT[b][:, c, :], win, start=True, stop=True)
                        if c % half == half - 1:
                            last.then_inc(mm_done, 1)

                def group(n, b):
                    if is_group(n - 1):
                        product(n - 1, (b - 1) % 2)
                    turn(n, b % 2)

                for b in range(DEEP):
                    group(b, b)
                with pe.Fori(1, groups // DEEP) as t:
                    for b in range(DEEP):
                        group(DEEP * t + b, b)
                product(groups - 1, 1)

            @block.scalar
            def _(act):
                def keep(n, b):
                    act.wait_ge(turned, n + 1)
                    wait(act, mm_done, 2 * (n - 1))
                    for k in range(2):
                        last = nc.scalar.copy(hT[b][:, k * half:(k + 1) * half, :], pt[k][:, :, :])
                    last.then_inc(kept, 1)

                for b in range(DEEP):
                    keep(b, b % 2)
                with act.Fori(1, groups // DEEP) as t:
                    for b in range(DEEP):
                        keep(DEEP * t + b, b % 2)

            @block.vector
            def _(dve):
                def scale(t, b):
                    n = DEEP * t + b
                    steps = Steps(dve, steps_s, SCALE * n)
                    f, r = pay[b][:, :, F:F + 3], rest[b % 2]
                    dve.wait_ge(loaded[b], 16 * (t + 1))
                    steps(nc.vector.tensor_scalar(r[:, :, :], f, -1.0, 1.0, ALU.mult, ALU.add))
                    if S == 2:
                        nc.vector.tensor_copy(fac[:, :, 0], r[:, :, 0])
                        steps(nc.vector.tensor_copy(fac[:, :, 1], f[:, :, 0]))
                    else:
                        nc.vector.tensor_tensor(fac[:, :, 0], r[:, :, 0], r[:, :, 1], ALU.mult)
                        nc.vector.tensor_tensor(fac[:, :, 1], r[:, :, 0], f[:, :, 1], ALU.mult)
                        steps(nc.vector.tensor_tensor(fac[:, :, 2], f[:, :, 0], r[:, :, 1], ALU.mult))
                        steps(nc.vector.tensor_tensor(fac[:, :, 3], f[:, :, 0], f[:, :, 1], ALU.mult))
                    wait(dve, turned, n - 1)
                    shape = [P, GRP, S, F]
                    steps(nc.vector.tensor_tensor(hs[b % 2][:, :, :].rearrange("p c (s f) -> p c s f", s=S),
                                                  bc(pay[b][:, :, 0:F], 2, shape), bc(fac[:, :, :], 3, shape),
                                                  ALU.mult))
                    dve.sem_inc(scaled, 1)

                def weigh(n, b, uses):
                    steps = Steps(dve, steps_w, WEIGH * n)
                    f, r, o = pay[b][:, :, F:F + 3], rest[b % 2], out[b % 2]
                    part = [P, half, Q // 2]
                    for k in range(2):
                        cs = slice(k * half, (k + 1) * half)
                        d = 1 if S == 2 else 2
                        low, high = (v, v2) if S == 2 else (o, o2)
                        if S == 4 and k == 0:
                            wait(dve, sent[b % 2], uses)
                        dve.wait_ge(mm_done, 2 * n + k + 1)
                        nc.vector.tensor_tensor(low[:, cs, :], pp[k][:, :, 0:Q // 2], bc(r[:, cs, d], 2, part),
                                                ALU.mult)
                        nc.vector.tensor_tensor(high[:, cs, :], pp[k][:, :, Q // 2:Q], bc(f[:, cs, d], 2, part),
                                                ALU.mult).then_inc(used, 1)
                    dve.wait_ge(used, 2 * n + 2)
                    if S == 2:
                        steps(nc.vector.tensor_tensor(v[:, :, :], v[:, :, :], v2[:, :, :], ALU.add))
                        wait(dve, sent[b % 2], uses)
                        full = [P, GRP, FO]
                        nc.vector.tensor_tensor(o[:, :, :], v[:, :, 0:FO], bc(r[:, :, 2], 2, full), ALU.mult)
                        steps(nc.vector.tensor_tensor(o2[:, :, :], v[:, :, FO:2 * FO], bc(f[:, :, 2], 2, full),
                                                      ALU.mult))
                    else:
                        steps(nc.vector.tensor_copy(at[b % 2][:, :], pay[b][:, :, F + 3].bitcast(I32)))
                    if S == 2:
                        nc.vector.tensor_copy(at[b % 2][:, :], pay[b][:, :, F + 3].bitcast(I32))
                    steps(nc.vector.tensor_tensor(o[:, :, :], o[:, :, :], o2[:, :, :], ALU.add))
                    dve.sem_inc(ready, 1)

                def group(t, b):
                    scale(t, b)
                    n = DEEP * t + b - 1
                    if is_group(n):
                        weigh(n, (b - 1) % DEEP, GRP * 16 * (2 * t + (b - 1) // 2))

                for b in range(DEEP):
                    group(0, b)
                with dve.Fori(1, groups // DEEP) as t:
                    for b in range(DEEP):
                        group(t, b)
                weigh(groups - 1, DEEP - 1, GRP * 16 * ((groups - 1) // 2))

            @block.gpsimd
            def _(pool):
                with pool.Fori(0, groups // 2) as t:
                    for b in range(2):
                        pool.wait_ge(ready, 2 * t + b + 1)
                        pool.sem_inc(started, 1)
                        for c in range(GRP):
                            pool.indirect_dma_start(msgs[:, :],
                                                    bass.IndirectOffsetOnAxis(ap=at[b][:, c:c + 1], axis=0),
                                                    out[b][:, c, :], None, bounds_check=P * NC - 1,
                                                    oob_is_err=False).then_inc(sent[b], 16)
                for b in range(2):
                    pool.wait_ge(sent[b], GRP * 16 * (groups // 2))


class SourceSums:

    def __init__(self, nc, g, ph, slo, tmap, msgs, F, accs, deep=2):
        self.deep = deep
        self.nc, self.g, self.slo, self.tmap, self.msgs, self.accs = nc, g, slo, tmap, msgs, accs
        self.rows = [ph.sb(f"msg_rows{b}", [P, GRP, F]) for b in range(deep)]
        self.oh = [ph.sb(f"src_oh{b}", [P, GRP, LO]) for b in range(deep)]
        self.sums = [ph.ps(f"src_sums{b}", [LO, GRP, F]) for b in range(deep)]
        self.oh_ready, self.mm_done, self.added, self.steps_a = (
            ph.sem(s) for s in ("src_oh_ready", "src_mm_done", "src_added", "src_steps_a"))
        self.loaded = [ph.sem(f"msg_loaded{b}") for b in range(deep)]

    def load(self, sp, t, b, first):
        n = self.deep * t + b
        if not first:
            sp.wait_ge(self.mm_done, n - self.deep + 1)
        of = self.msgs.rearrange("(p j) w -> p j w", p=P)
        sp.dma_start(self.rows[b][:, :, :], of[:, bass.ds(n * GRP, GRP), :]).then_inc(self.loaded[b], 16)

    def clear(self, dve):
        steps = Steps(dve, self.steps_a)
        clear_tables(self.nc, steps, self.accs)

    def hot(self, dve, n, b, first):
        if not first:
            dve.wait_ge(self.mm_done, n - self.deep + 1)
        self.nc.vector.tensor_tensor(self.oh[b][:, :, :], bc(self.g.iota[:, 0:LO], 1, [P, GRP, LO]),
                                     bc(self.slo[:, bass.ds(n * GRP, GRP)], 2, [P, GRP, LO]),
                                     ALU.is_equal).then_inc(self.oh_ready, 1)

    def add(self, dve, n, b):
        dve.wait_ge(self.mm_done, n + 1)
        add_tiles(self.nc, dve, self.steps_a, 1, n, self.tmap, self.accs,
                  [self.sums[b][:, c:c + 1, :] for c in range(GRP)], ALU.add)
        dve.sem_inc(self.added, 1)

    def join(self, dve):
        join_tables(self.nc, dve, self.steps_a, self.accs)

    def product(self, pe, t, b, first):
        n = self.deep * t + b
        pe.wait_ge(self.oh_ready, n + 1)
        pe.wait_ge(self.loaded[b], 16 * (t + 1))
        if not first:
            pe.wait_ge(self.added, n - self.deep + 1)
        for c in range(GRP):
            last = self.nc.tensor.matmul(self.sums[b][:, c, :], self.oh[b][:, c, :], self.rows[b][:, c, :],
                                         start=True, stop=True)
        last.then_inc(self.mm_done, 1)


def src_sums(nc, g, name, slo, tmap, msgs, F, accs):
    groups = NC // GRP
    with Phase(nc, name) as ph:
        src = SourceSums(nc, g, ph, slo, tmap, msgs, F, accs, DEEP)
        with nc.Block() as block:
            @block.sync
            def _(sp):
                for b in range(DEEP):
                    src.load(sp, 0, b, True)
                with sp.Fori(1, groups // DEEP) as t:
                    for b in range(DEEP):
                        src.load(sp, t, b, False)

            @block.vector
            def _(dve):
                src.clear(dve)
                for b in range(DEEP):
                    src.hot(dve, b, b, True)
                    if b >= 2:
                        src.add(dve, b - 2, b - 2)
                with dve.Fori(1, groups // DEEP) as t:
                    for b in range(DEEP):
                        src.hot(dve, DEEP * t + b, b, False)
                        src.add(dve, DEEP * t + b - 2, (b - 2) % DEEP)
                src.add(dve, groups - 2, DEEP - 2)
                src.add(dve, groups - 1, DEEP - 1)
                src.join(dve)

            @block.tensor
            def _(pe):
                for b in range(DEEP):
                    src.product(pe, 0, b, True)
                with pe.Fori(1, groups // DEEP) as t:
                    for b in range(DEEP):
                        src.product(pe, t, b, False)


def finish(nc, g, acc, bias, x, out):
    wide = [LO, NT, D]
    with Phase(nc, "finish") as ph:
        steps_s, stored = ph.sem("steps"), ph.sem("stored")
        with nc.Block() as block:
            @block.vector
            def _(dve):
                steps = Steps(dve, steps_s)
                steps(nc.vector.tensor_tensor(acc, acc, bc(g.rdeg[:, :], 2, wide), ALU.mult))
                steps(nc.vector.tensor_tensor(acc, acc, bc(bias, 1, wide), ALU.add))
                steps(nc.vector.tensor_tensor(acc, acc, x, ALU.add))

            @block.sync
            def _(sp):
                sp.wait_ge(steps_s, 3)
                sp.dma_start(out.rearrange("(p c) f -> p c f", p=LO), acc).then_inc(stored, 16)
                sp.wait_ge(stored, 16)


def keep_column(nc, name, to, of):
    with nc.Block() as block:
        @block.vector
        def _(dve):
            nc.vector.tensor_copy(to, of)


def join_columns(nc, name, to, of, zero):
    with nc.Block() as block:
        @block.vector
        def _(dve):
            nc.vector.tensor_copy(to, of)
            nc.vector.memset(zero, 0.0)


def count_too(nc, g, w):
    with Phase(nc, "count") as ph:
        cleared = ph.sem("cleared")
        with nc.Block() as block:
            @block.vector
            def _(dve):
                steps = Steps(dve, cleared)
                steps(nc.vector.memset(w, 0.0))
                nc.vector.tensor_copy(w[:, HID:HID + 1], g.ident[0:K3 + 1, K3:K3 + 1])


def program(nc, x_in, src, dst, edge_attr, lam, cheb_W, cheb_b, gat_Wsrc, gat_bsrc, gat_Wdst, gat_bdst, gat_attn,
            gat_bias, stn1_w, stn1_b, stn2_w, stn2_b, stn3_w, stn3_b, stn4_w, stn4_b, conv_w, conv_b, out):
    whole = ExitStack()
    with whole:
        def sb(name, shape, dt=F32, ctx=whole):
            return ctx.enter_context(nc.sbuf_tensor(name, shape, dt))

        def dram(name, shape, dt=F32):
            return nc.dram_tensor(name, shape, dt).ap()

        g = Tensors()
        g.iota, g.ones, g.ident, g.tri = (sb(n, [P, P]) for n in ("iota", "ones", "ident", "tri"))
        g.jcol, g.junk, g.re = sb("jcol", [P, NC // P]), sb("junk", [P, 1]), sb("re", [LO, 5])
        g.degd, g.norm, g.rdeg = (sb(n, [LO, NT]) for n in ("degd", "norm", "rdeg"))
        rec_d, rec_s = dram("rec_d", [P * NC, RECD]), dram("rec_s", [P * NC, RECS])
        map_d, map_s = dram("map_d", [NC], I32), dram("map_s", [NC], I32)
        map_c, map_c2 = dram("map_c", [NC], I32), dram("map_c2", [NC], I32)
        table = dram("table", [N, D])
        table_fst = dram("table_fst", [N, D + 4])
        fse = dram("fse", [P * NC, D + 4])
        cells1, cells2 = dram("cells1", [P * NCC, HID + 4]), dram("cells2", [P * NCC, D + 4])
        msgs1, msgs2 = dram("msgs1", [P * NC, HID]), dram("msgs2", [P * NC, D])
        row = lambda a: a.rearrange("(o c) -> o c", o=1)
        spread = lambda a, n: a.partition_broadcast(n)
        skipped = int(BIG)

        constants(nc, g)
        lam_b, w1, w3, w4 = sb("lam_b", [LO, 1]), sb("w1", [K3 + 1, HID + 1]), sb("w3", [HID, HID]), sb("w4", [HID, 3])
        cheb_w, gat_w = sb("cheb_w", [3 * D, D]), sb("gat_w", [D, 2 * D])
        b_cheb, b_gat, b_att = sb("b_cheb", [LO, D]), sb("b_gat", [LO, 2 * D]), sb("b_att", [LO, D])
        attn = sb("attn", [P, D])
        b1, b2, b3 = (sb(f"b{k}", [LO, HID]) for k in (1, 2, 3))
        b4, b5 = sb("b4", [LO, 3]), sb("b5", [LO, D])
        slo = sb("slo", [P, NC])
        maps = sb("maps", [3, NC], I32)
        tmd, tms, cmap = maps[0:1, :], maps[1:2, :], maps[2:3, 0:NCC]

        def narrow_map(ph):
            return [ph.sb(f"tmp{k}", [P, NC // P]) for k in range(3)]

        wide = sb("wide", [LO, NT, 3 * D])
        h1 = wide[:, :, 0:HID]
        with ExitStack() as c2:
            def eb(name, dt=F32, ctx=c2):
                return sb(name, [P, ECP], dt, ctx)

            e = Tensors()
            e.src, e.rows, e.rowd, e.rowc = (eb(n, I32) for n in ("src", "row_s", "row_d", "row_c"))
            e.att, e.lod = sb("att", [P, ECP, 3], F32, c2), eb("lod")
            with ExitStack() as c3:
                e.tiled, e.los, e.tiles, key = (eb(n, F32, c3) for n in ("tiled", "los", "tiles", "cellkey"))
                load_edges(nc, g, e, src, dst, edge_attr)
                work = [eb(f"work{k}", F32, c3) for k in range(3)]
                with Phase(nc, "ranks") as pr, Phase(nc, "fill1") as pf, nc.Block() as block:
                    rank(nc, g, pr, block, work, e.tiles[:, :], ECP, NT, NC, e.rows[:, :], None, map_s)
                    fill_rows(nc, pf, block, ((rec_s, NC, 8, ((SLO, -1.0),)),
                                              (rec_d, NC, 8, ((ROWS, skipped), (ROWC, skipped), (DLO, -1.0)))))
                with Phase(nc, "fill2") as pf, Phase(nc, "scats") as ps, Phase(nc, "cellk") as pk, \
                        Phase(nc, "rankd") as pd, Phase(nc, "rankc") as pc, nc.Block() as block:
                    fill_rows(nc, pf, block, ((cells1, NCC, 96, ((HID + 3, skipped),)),
                                              (cells2, NCC, 96, ((D + 3, skipped),))))
                    scatter_records(nc, g, ps, block, ((SLO, e.los), (SATT, e.att)), RECS, e.rows, rec_s)
                    edge_cells(nc, g, pk, block, work, e.att, e.tiled[:, :], key[:, :])
                    rank(nc, g, pd, block, work, e.tiled[:, :], ECP, NT, NC, e.rowd[:, :], None, map_d)
                    rank(nc, g, pc, block, work, key[:, :], ECP, CELLS, NCC, e.rowc[:, :],
                         cell_offsets(nc, narrow_map(pc), HID), map_c)
            recs = sb("recs", [P, NC, RECS], F32, c2)
            bt = sb("bt", [K3 + 1, NT, LO], F32, c2)
            count_too(nc, g, w1[:, :])
            load_table(nc, g, "params", [
                (tmd, row(map_d)), (tms, row(map_s)), (cmap, row(map_c)[:, 0:NCC]),
                (recs[:, :, :], rec_s.rearrange("(p j) w -> p j w", p=P)), (lam_b[:, :], spread(lam, LO)),
                (w1[0:K3, 0:HID], stn1_w.rearrange("k i o -> k (i o)")), (w3[:, :], stn3_w), (w4[:, :], stn4_w),
                (cheb_w[:, :], cheb_W.rearrange("o i -> i o")), (gat_w[:, 0:D], gat_Wsrc.rearrange("o i -> i o")),
                (gat_w[:, D:2 * D], gat_Wdst.rearrange("o i -> i o")), (b_cheb[:, :], spread(cheb_b, LO)),
                (b_gat[:, 0:D], spread(gat_bsrc, LO)), (b_gat[:, D:2 * D], spread(gat_bdst, LO)),
                (b_att[:, :], spread(gat_bias, LO)), (attn[:, :], spread(gat_attn.rearrange("a b c -> (a b c)"), P)),
                (b1[:, :], spread(stn1_b, LO)), (b2[:, :], spread(stn2_b, LO)), (b3[:, :], spread(stn3_b, LO)),
                (b4[:, :], spread(stn4_b, LO)), (b5[:, :], spread(conv_b, LO))])
            with Phase(nc, "fill3") as pf, Phase(nc, "scatd") as ps, Phase(nc, "basis") as pb, nc.Block() as block:
                fill_rows(nc, pf, block, ((msgs1, NC, 104, ()), (msgs2, NC, 104, ())))
                scatter_records(nc, g, ps, block, ((SRC, e.src), (ROWS, e.rows), (ROWC, e.rowc), (ATT, e.att),
                                                   (DLO, e.lod)), RECD, e.rowd, rec_d)
                basis_sums(nc, g, pb, block, recs, tms, bt[:, :, :])
            keep_column(nc, "slo", slo[:, :], recs[:, :, SLO])
            node_linear(nc, g, "stn1", bt[:, :, :], K3 + 1, w1[:, :], None, HID + 1, wide[:, :, 0:HID + 1],
                        transposed=True)
        out_scale(nc, g, wide[:, :, HID])
        scale_bias_elu(nc, g, "elu1", h1, HID, g.rdeg[:, :], b1[:, :])

        rec = sb("rec", [P, NC, RECD])
        load_table(nc, g, "ldrec", [(rec[:, :, :], rec_d.rearrange("(p j) w -> p j w", p=P))])

        def stacked(w, kernel, S):
            F, moved = P // S, {2: (0, KS * KS), 4: (0, KS, KS * KS, KS * KS + KS)}[S]
            return [(w[q * F:(q + 1) * F, 0:K3 - m, :], kernel[m:K3].rearrange("k i o -> i k o"))
                    for q, m in enumerate(moved)]

        t4 = sb("t4", [LO, NT, 4])
        with ExitStack() as c2:
            frac = sb("frac", [P, NC, 3], F32, c2)
            spline_cells(nc, g, "frac", rec[:, :, ATT:ATT + 3], None, None, frac[:, :, :])
            to_cells(nc, g, "toc1", rec, tmd, h1, HID, frac,
                     lambda slots: rec[:, slots, ROWC].bitcast(I32), cells1, g.degd[:, :])
        in_scale(nc, g, lam_b[:, :])
        with ExitStack() as c2:
            w2 = sb("w2", [P, K3, HID], F32, c2)
            load_table(nc, g, "ldw2", stacked(w2, stn2_w, 2))
            cell_messages(nc, g, "msg1", cells1, cmap, w2[:, :, :].rearrange("i k o -> i (k o)"), HID, HID, msgs1)

        def movement(nodes):
            scale_bias_elu(nc, g, "elu2", nodes, HID, g.rdeg[:, :], b2[:, :])
            node_linear(nc, g, "stn3", nodes, HID, w3[:, :], b3[:, :], HID, nodes)
            scale_bias_elu(nc, g, "elu3", nodes, HID, None, None)
            node_linear(nc, g, "stn4", nodes, HID, w4[:, :], b4[:, :], 3, t4[:, :, 0:3])

        x = sb("x", [LO, NT, D])
        load_table(nc, g, "ldx", [(x[:, :, :], x_in.rearrange("(p c) f -> p c f", p=LO))])
        att2 = rec[:, :, ATT:ATT + 3]
        with ExitStack() as c1:
            acc = sb("acc", [LO, NT, D], F32, c1)
            cat = wide
            layer_norm_relu(nc, g, "ln0", x[:, :, :], cat[:, :, 0:D])
            for layer in range(2):
                for order in (1, 2):
                    name = f"cheb{layer}{order}"
                    store_scaled(nc, g, name + "s", cat[:, :, (order - 1) * D:order * D], g.norm[:, :], table)
                    if layer == 0 and order == 1:
                        with ExitStack() as c3:
                            h2, h2b = (sb(n, [LO, NT, HID], F32, c3) for n in ("h2", "h2b"))
                            propagate(nc, g, name + "p", rec, tmd, table,
                                      [acc[:, :, :], cat[:, :, 2 * D:3 * D]],
                                      (slo, tms, msgs1, HID, [h2[:, :, :], h2b[:, :, :]]))
                            movement(h2[:, :, :])
                    else:
                        propagate(nc, g, name + "p", rec, tmd, table, [acc[:, :, :]])
                    chebyshev(nc, g, name + "c", acc[:, :, :], cat, order)
                node_linear(nc, g, f"cheb{layer}l", cat[:, :, :], 3 * D, cheb_w[:, :], b_cheb[:, :], D,
                            cat[:, :, 0:D] if layer == 0 else acc[:, :, :], relu=True)
            fdt = sb("fdt", [LO, NT, D + 4], F32, c1)
            node_linear(nc, g, "gatf", acc[:, :, :], D, gat_w[:, :], b_gat[:, :], 2 * D, cat[:, :, 0:2 * D])
            join_columns(nc, "joint", fdt[:, :, D:D + 3], t4[:, :, 0:3], fdt[:, :, D + 3:D + 4])
            keep_column(nc, "fs", fdt[:, :, 0:D], cat[:, :, 0:D])
            store_scaled(nc, g, "gats", fdt[:, :, :], None, table_fst)
            keep_column(nc, "fd", fdt[:, :, 0:D], cat[:, :, D:2 * D])
            lgs = sb("lgs", [P, NC], F32, c1)
            mx = sb("mx", [LO, NT, 1], F32, c1)
            attention_scores(nc, g, rec, tmd, table_fst, fse, fdt[:, :, :], attn[:, :], lgs, mx[:, :, :], att2)
            att = sb("att0", [LO, NT, D + 1], F32, c1)
            att_b = sb("att_b", [LO, NT, D + 1], F32, c1)
            attention_sums(nc, g, rec, tmd, fse, lgs, mx[:, :, :],
                           [att[:, :, :], att_b[:, :, :], wide[:, :, 0:D + 1], wide[:, :, D + 1:2 * D + 2]])
            attention_end(nc, g, att[:, :, :], b_att[:, :], x[:, :, :])

        rowc = sb("rowc", [P, NC], I32)
        frac = sb("frac2", [P, NC, 3])
        with ExitStack() as c2:
            key = sb("key", [P, NC], F32, c2)
            spline_cells(nc, g, "cells2", att2, rec[:, :, DLO], key[:, :], frac[:, :, :])
            with Phase(nc, "rank2") as pr, nc.Block() as block:
                rank(nc, g, pr, block, [pr.sb(f"work{k}", [P, NC]) for k in range(3)], key[:, :],
                     NC, CELLS, NCC, rowc[:, :], cell_offsets(nc, narrow_map(pr), D), map_c2)
        with ExitStack() as c2:
            h = wide[:, :, 0:D]
            w5 = sb("w5", [P, K3, D], F32, c2)
            load_table(nc, g, "ldw5", stacked(w5, conv_w, 4) + [(cmap, row(map_c2)[:, 0:NCC])])
            layer_norm_relu(nc, g, "ln1", x[:, :, :], h)
            to_cells(nc, g, "toc2", rec, tmd, h, D, frac, lambda slots: rowc[:, slots], cells2)
            cell_messages(nc, g, "msg2", cells2, cmap, w5[:, :, :].rearrange("i k o -> i (k o)"), D, D, msgs2)
            more = sb("more", [LO, NT, D], F32, c2)
            src_sums(nc, g, "sum2", slo, tms, msgs2, D,
                     [h, wide[:, :, D:2 * D], wide[:, :, 2 * D:3 * D], more[:, :, :]])
            finish(nc, g, h, b5[:, :], x[:, :, :], out)


_INS = ["x", "src", "dst", "edge_attr_3", "L0_gnn_laplacian_lambda_max", "L0_gnn_cheb_W", "L0_gnn_cheb_b",
        "L0_gnn_gat_Wsrc", "L0_gnn_gat_bsrc", "L0_gnn_gat_Wdst", "L0_gnn_gat_bdst", "L0_gnn_gat_attn",
        "L0_gnn_gat_bias", "L1_gnn_stn1_w", "L1_gnn_stn1_b", "L1_gnn_stn2_w", "L1_gnn_stn2_b", "L1_gnn_stn3_w",
        "L1_gnn_stn3_b", "L1_gnn_stn4_w", "L1_gnn_stn4_b", "L1_gnn_conv_w", "L1_gnn_conv_b"]


def kernel(**inputs):
    import numpy as _np
    import concourse.bacc as _bacc
    from concourse import mybir as _mybir
    from concourse.bass_utils import run_bass_kernel_spmd as _run

    nc = _bacc.Bacc("TRN2", target_bir_lowering=False, num_devices=1)
    arrays, args = {}, []
    for name in _INS:
        a = _np.ascontiguousarray(inputs[name])
        arrays[f"in_{name}_dram"] = a
        args.append(nc.dram_tensor(f"in_{name}_dram", a.shape, _mybir.dt.from_np(a.dtype), kind="ExternalInput").ap())
    out = nc.dram_tensor("out_0_dram", (12500, 32), _mybir.dt.float32, kind="ExternalOutput").ap()
    program(nc, *args, out)
    r = _run(nc, [arrays], core_ids=[0])
    return r.results[0]["out_0_dram"]
```
